# Optimizing a Trainium2 kernel written in Bass

```python
import numpy as np
import jax
import jax.numpy as jnp

def _softmax(x, axis=-1):
    return jax.nn.softmax(x, axis=axis)

def _gelu(x):
    return jax.nn.gelu(x, approximate=True)

def _silu(x):
    return jax.nn.silu(x)

def _sigmoid(x):
    return jax.nn.sigmoid(x)

def _layernorm(x, axis=-1, eps=1e-05):
    m = jnp.mean(x, axis=axis, keepdims=True)
    v = jnp.var(x, axis=axis, keepdims=True)
    return (x - m) / jnp.sqrt(v + eps)

def _scatter_add(tgt, idx, src, axis=0):
    return tgt.at[idx].add(src)

def _segment_sum(src, seg, n):
    return jax.ops.segment_sum(src, seg, n)
kernel_name = 'mk_seq_postln_d2_jaxref_r8_359c28'

def setup_inputs(seed: int=0):
    np.random.seed(seed)
    _w = jnp.asarray

    def _L0_attn_setup():
        import jax, jax.numpy as jnp
        import numpy as np
        B, T, E, H = (2, 256, 256, 16)
        D = E // H
        key = jax.random.key(seed)
        ks = jax.random.split(key, 5)
        s = 0.02
        return {'x': jax.random.normal(ks[0], (B, T, E), jnp.float32), 'Wq': jax.random.normal(ks[1], (E, E), jnp.float32) * s, 'Wk': jax.random.normal(ks[2], (E, E), jnp.float32) * s, 'Wv': jax.random.normal(ks[3], (E, E), jnp.float32) * s, 'Wp': jax.random.normal(ks[4], (E, E), jnp.float32) * s, 'bp': jnp.zeros((E,), jnp.float32)}
    _L0_attn_in = _L0_attn_setup()

    def _L0_ffn_setup():
        import jax, jax.numpy as jnp
        import numpy as np
        B, S, H, E, D, K = (2, 256, 256, 8, 256, 2)
        key = jax.random.key(seed)
        ks = jax.random.split(key, 4)
        return {'x': jax.random.normal(ks[0], (B, S, H), jnp.float32), 'router_w': jax.random.normal(ks[1], (H, E), jnp.float32) / np.sqrt(H).astype(np.float32), 'router_b': jnp.zeros((E,), jnp.float32), 'expert_w': jax.random.normal(ks[2], (E, H, D), jnp.float32) / np.sqrt(H).astype(np.float32), 'expert_b': jnp.zeros((E, D), jnp.float32), 'out_w': jax.random.normal(ks[3], (D, D), jnp.float32) / np.sqrt(D).astype(np.float32), 'out_b': jnp.zeros((D,), jnp.float32)}
    _L0_ffn_in = _L0_ffn_setup()

    def _L1_attn_setup():
        import jax, jax.numpy as jnp
        import numpy as np
        B, SQ, HIDDEN = (2, 256, 256)
        HEADS, GROUPS, KVC = (16, 4, 128)
        HPG = HEADS // GROUPS
        LAYER_INDEX = 1
        SCALE = KVC ** (-0.5)
        key = jax.random.key(seed)
        k1, k2, k3, k4 = jax.random.split(key, 4)
        return {'x': jax.random.normal(k1, (B, SQ, HIDDEN), jnp.float32), 'w_q': jax.random.normal(k2, (HIDDEN, HEADS * KVC), jnp.float32) * 0.02, 'w_kv': jax.random.normal(k3, (HIDDEN, 2 * GROUPS * KVC), jnp.float32) * 0.02, 'w_dense': jax.random.normal(k4, (HEADS * KVC, HIDDEN), jnp.float32) * 0.02}
    _L1_attn_in = _L1_attn_setup()

    def _L1_ffn_setup():
        import jax, jax.numpy as jnp
        import numpy as np
        E = 8
        K = 2
        CAP = 64
        H = 256
        F = 1024
        key = jax.random.key(seed)
        ks = jax.random.split(key, 6)
        inp = {'hidden_states': jax.random.normal(ks[0], (2, 128, H), jnp.float32), 'router_w': jax.random.normal(ks[1], (E, H), jnp.float32) * (0.01 / np.sqrt(H)), 'w1': jax.random.normal(ks[2], (F, H), jnp.float32) * (1.0 / np.sqrt(H)), 'b1': jax.random.normal(ks[3], (F,), jnp.float32) * 0.01, 'w2': jax.random.normal(ks[4], (H, F), jnp.float32) * (1.0 / np.sqrt(F)), 'b2': jax.random.normal(ks[5], (H,), jnp.float32) * 0.01}
        return inp
    _L1_ffn_in = _L1_ffn_setup()
    _d = {'L0_attn_x': _L0_attn_in['x'], 'L0_attn_Wq': _L0_attn_in['Wq'], 'L0_attn_Wk': _L0_attn_in['Wk'], 'L0_attn_Wv': _L0_attn_in['Wv'], 'L0_attn_Wp': _L0_attn_in['Wp'], 'L0_attn_bp': _L0_attn_in['bp'], 'L0_ffn_router_w': _L0_ffn_in['router_w'], 'L0_ffn_router_b': _L0_ffn_in['router_b'], 'L0_ffn_expert_w': _L0_ffn_in['expert_w'], 'L0_ffn_expert_b': _L0_ffn_in['expert_b'], 'L0_ffn_out_w': _L0_ffn_in['out_w'], 'L0_ffn_out_b': _L0_ffn_in['out_b'], 'L1_attn_w_q': _L1_attn_in['w_q'], 'L1_attn_w_kv': _L1_attn_in['w_kv'], 'L1_attn_w_dense': _L1_attn_in['w_dense'], 'L1_ffn_router_w': _L1_ffn_in['router_w'], 'L1_ffn_w1': _L1_ffn_in['w1'], 'L1_ffn_b1': _L1_ffn_in['b1'], 'L1_ffn_w2': _L1_ffn_in['w2'], 'L1_ffn_b2': _L1_ffn_in['b2']}
    _x0 = _d['L0_attn_x']
    _d['L0_attn_x'] = jax.random.normal(jax.random.fold_in(jax.random.key(seed), 1), (4, 512, 256), dtype=_x0.dtype)
    del _x0
    return _d

def reference(L0_attn_x, L0_attn_Wq, L0_attn_Wk, L0_attn_Wv, L0_attn_Wp, L0_attn_bp, L0_ffn_router_w, L0_ffn_router_b, L0_ffn_expert_w, L0_ffn_expert_b, L0_ffn_out_w, L0_ffn_out_b, L1_attn_w_q, L1_attn_w_kv, L1_attn_w_dense, L1_ffn_router_w, L1_ffn_w1, L1_ffn_b1, L1_ffn_w2, L1_ffn_b2):

    def _L0_attn_ref(x, Wq, Wk, Wv, Wp, bp):
        import jax, jax.numpy as jnp
        import numpy as np
        B, T, E, H = (2, 256, 256, 16)
        D = E // H
        b, t, e = x.shape
        h, d = (H, E // H)
        Q = (x @ Wq.T).reshape(b, h, t, d)
        K = (x @ Wk.T).reshape(b, h, t, d)
        V = (x @ Wv.T).reshape(b, h, t, d)
        scores = jnp.einsum('bhqd,bhkd->bhqk', Q, K)
        causal = jnp.triu(jnp.ones((t, t), bool), k=1)
        scores = jnp.where(causal, -jnp.inf, scores)
        weights = jax.nn.softmax(scores / jnp.sqrt(jnp.float32(d)), axis=-1)
        ctx = jnp.einsum('bhqk,bhkd->bhqd', weights, V)
        ctx = ctx.transpose(0, 2, 1, 3).reshape(b, t, e)
        return ctx @ Wp.T + bp

    def _L0_ffn_ref(x, router_w, router_b, expert_w, expert_b, out_w, out_b):
        import jax, jax.numpy as jnp
        import numpy as np
        B, S, H, E, D, K = (2, 256, 256, 8, 256, 2)
        num_experts = expert_w.shape[0]
        router_logits = jnp.einsum('bsh,he->bse', x, router_w) + router_b
        router_probs = jax.nn.softmax(router_logits, axis=-1)
        top_k_probs, top_k_indices = jax.lax.top_k(router_probs, K)
        top_k_probs = top_k_probs / jnp.sum(top_k_probs, axis=-1, keepdims=True)
        onehot = jax.nn.one_hot(top_k_indices, num_experts, dtype=x.dtype)
        gates = jnp.einsum('bsk,bske->bse', top_k_probs, onehot)
        expert_out = jax.nn.gelu(jnp.einsum('bsh,ehd->ebsd', x, expert_w) + expert_b[:, None, None, :])
        combined = jnp.einsum('bse,ebsd->bsd', gates, expert_out)
        return jnp.einsum('bsd,df->bsf', combined, out_w) + out_b

    def _L1_attn_ref(x, w_q, w_kv, w_dense):
        import jax, jax.numpy as jnp
        import numpy as np
        B, SQ, HIDDEN = (2, 256, 256)
        HEADS, GROUPS, KVC = (16, 4, 128)
        HPG = HEADS // GROUPS
        LAYER_INDEX = 1
        SCALE = KVC ** (-0.5)
        b, sq, _ = x.shape
        sk = sq
        q = jnp.einsum('bsh,he->bse', x, w_q).reshape(b, sq, GROUPS, HPG, KVC)
        kv = jnp.einsum('bsh,he->bse', x, w_kv)
        k, v = jnp.split(kv, 2, axis=-1)
        k = k.reshape(b, sk, GROUPS, KVC)
        v = v.reshape(b, sk, GROUPS, KVC)
        scores = jnp.einsum('bqgpd,bkgd->bgqpk', q, k) * (SCALE / LAYER_INDEX)
        scores = scores.astype(jnp.float32) * LAYER_INDEX
        causal = jnp.arange(sq)[:, None] >= jnp.arange(sk)[None, :]
        scores = jnp.where(causal[None, None, :, None, :], scores, -jnp.inf)
        probs = jax.nn.softmax(scores, axis=-1).astype(x.dtype)
        ctx = jnp.einsum('bgqpk,bkgd->bqgpd', probs, v).reshape(b, sq, HEADS * KVC)
        return jnp.einsum('bse,eh->bsh', ctx, w_dense)

    def _L1_ffn_ref(hidden_states, router_w, w1, b1, w2, b2):
        import jax, jax.numpy as jnp
        import numpy as np
        E = 8
        K = 2
        CAP = 64
        H = 256
        F = 1024
        orig_shape = hidden_states.shape
        x = hidden_states.reshape(-1, H)
        N = x.shape[0]
        logits = x @ router_w.T
        probs = jax.nn.softmax(logits, axis=-1)
        top_p, top_i = jax.lax.top_k(probs, K)
        expert_flat = top_i.T.reshape(-1)
        probs_flat = top_p.T.reshape(-1)
        token_idx = jnp.tile(jnp.arange(N), K)
        onehot = (expert_flat[:, None] == jnp.arange(E)[None, :]).astype(jnp.int32)
        pos = jnp.take_along_axis(jnp.cumsum(onehot, axis=0), expert_flat[:, None], axis=1)[:, 0] - 1
        keep = pos < CAP
        dest = expert_flat * CAP + pos
        dest_m = jnp.where(keep, dest, E * CAP)
        buf = jnp.zeros((E * CAP, H), x.dtype).at[dest_m].set(x[token_idx], mode='drop')
        h = jax.nn.gelu(buf @ w1.T + b1, approximate=False) @ w2.T + b2
        gathered = jnp.where(keep[:, None], h[jnp.where(keep, dest, 0)], 0.0) * probs_flat[:, None]
        out = jnp.zeros_like(x).at[token_idx].add(gathered)
        return out.reshape(orig_shape)
    x = L0_attn_x
    x = _layernorm(x + _L0_attn_ref(x, L0_attn_Wq, L0_attn_Wk, L0_attn_Wv, L0_attn_Wp, L0_attn_bp), axis=-1)
    x = _layernorm(x + _L0_ffn_ref(x, L0_ffn_router_w, L0_ffn_router_b, L0_ffn_expert_w, L0_ffn_expert_b, L0_ffn_out_w, L0_ffn_out_b), axis=-1)
    x = _layernorm(x + _L1_attn_ref(x, L1_attn_w_q, L1_attn_w_kv, L1_attn_w_dense), axis=-1)
    x = _layernorm(x + _L1_ffn_ref(x, L1_ffn_router_w, L1_ffn_w1, L1_ffn_b1, L1_ffn_w2, L1_ffn_b2), axis=-1)
    return x

_drawn_inputs = setup_inputs


def setup_inputs(seed=0):
    import zlib

    import numpy as np

    out = dict(_drawn_inputs(seed))
    spreads = {'L0_attn_bp': (0.0, 0.1),
     'L0_ffn_router_b': (0.0, 0.1),
     'L0_ffn_expert_b': (0.0, 0.1),
     'L0_ffn_out_b': (0.0, 0.1)}
    factors = {'L0_attn_Wq': 8.0,
     'L0_attn_Wk': 8.0,
     'L1_attn_w_q': 8.0,
     'L1_ffn_b1': 64.0,
     'L1_ffn_b2': 64.0}
    for name, (base, spread) in spreads.items():
        noise = np.random.default_rng([zlib.crc32(name.encode()), seed]).standard_normal(out[name].shape)
        drawn = base * np.exp(spread * noise) if base else spread * noise
        out[name] = jnp.asarray(drawn.astype(out[name].dtype))
    for name, factor in factors.items():
        out[name] = (out[name] * factor).astype(out[name].dtype)
    return out
```

```python
from contextlib import ExitStack

import concourse.bass as bass
from concourse import mybir

F32 = mybir.dt.float32
BF16 = mybir.dt.bfloat16
ALU = mybir.AluOpType
ACT = mybir.ActivationFunctionType
AX = mybir.AxisListType

P = 128
E = 256
KE = E // P
NB = 4
TOK = 512
TT = TOK // P
NT = NB * TT
HEADS = 16
D0 = E // HEADS
D1 = 128
NH = NB * HEADS
NX = 8
FF = 1024
NF = FF // P
CAP = 64
EPS = 1e-5
CH = 1024
NCH = 19
CONSTS = 3 * P + 512
MASKED = -1e30
HUGE = 3e38

S_CHUNKS = (((3, 0),), ((2, 0), (0, 384)), ((1, 0),))
S_OFF = {3: 0, 2: 512, 0: 896, 1: 1024}
S_COLS = 1280
T_CHUNKS = (
    tuple((0, qt, qt * P) for qt in range(4)),
    tuple((1, qt, (qt - 1) * P) for qt in range(1, 4)) + ((3, 3, 384),),
    tuple((2, qt, (qt - 2) * P) for qt in range(2, 4)),
)
T_OFF = (0, 512, 1024)
T_LEN = (512, 512, 256)
PT_COL = {(kt, qt): T_OFF[c] + col for c, chunk in enumerate(T_CHUNKS) for kt, qt, col in chunk}

Q_HI, Q_HI2, Q_LO, Q_ROWS = 0, 16, 32, 48
K_HI, K_LO, K_HI2, V_HI, V_LO, K_ROWS = 0, 16, 32, 48, 64, 80

LATE = [("cm", 0), ("cm", 1), ("x2", 0), ("cm", 2), ("x2", 1), ("cm", 3), ("x2", 2), ("x2", 3)]
USES = 8 + len(LATE)
E_CHAIN = 22
C_ALL = 6


def proj_use(g, j):
    last = isinstance(g, int) and g == NT - 1
    return 6 * g + ((2, 3, 4, 5) if last else (2, 3, 5, 7))[j]


WP, OUTW, EXPW, WQ, WKV, WD, W1, W2 = 0, 512, CH, 5 * CH, 9 * CH, 11 * CH, 15 * CH, 17 * CH


def build(nc, x_tok_d, x_t_d, wqkv_d, wall_d, const_d, bp_d, outb_d, b2_d, rb_d, eb_d, rw0_d, rw1_d, b1_d, out_d):
    ctx = ExitStack()
    with ctx:
        def sb(name, shape, dt=F32):
            return ctx.enter_context(nc.sbuf_tensor(name, shape, dt))

        def sem(name):
            return ctx.enter_context(nc.semaphore(name))

        x_tok = sb("x_tok", [P, NT * E])
        xt_hi = sb("xt_hi", [P, KE, NB * TOK], BF16)
        xt_lo = sb("xt_lo", [P, KE, NB * TOK], BF16)
        w_hi = sb("w_hi", [P, NCH * CH], BF16)
        w_lo = sb("w_lo", [P, NCH * CH], BF16)
        wqkv_hi = sb("wqkv_hi", [P, KE, 3 * E], BF16)
        wqkv_lo = sb("wqkv_lo", [P, KE, 3 * E], BF16)
        scr = sb("scr", [P, 16384])
        s_sb = [sb(f"s_sb{i}", [P, S_COLS]) for i in range(2)]
        pt_hi = [sb(f"pt_hi{i}", [P, S_COLS], BF16) for i in range(2)]
        pt_lo = [sb(f"pt_lo{i}", [P, S_COLS], BF16) for i in range(2)]
        consts = sb("consts", [P, CONSTS])
        ident_b = sb("ident_b", [P, P], BF16)
        ones_b = sb("ones_b", [P, P], BF16)
        upper_b = sb("upper_b", [P, P], BF16)
        bp_bc = sb("bp_bc", [P, E])
        outb_bc = sb("outb_bc", [P, E])
        b2_bc = sb("b2_bc", [P, E])
        rb_bc = sb("rb_bc", [P, NX])
        b1_col = sb("b1_col", [P, NF])
        rw_f = sb("rw_f", [P, 2, KE * NX])
        rw_hi = sb("rw_hi", [P, 2, KE * NX], BF16)
        rw_lo = sb("rw_lo", [P, 2, KE * NX], BF16)
        nm = sb("nm", [P, 2, 4])
        rs = sb("rs", [P, 2, 4])
        rr = sb("rr", [P, 2, 4])
        v0 = [sb(f"v0_{i}", [P, 4, 2 * D0], BF16) for i in range(2)]
        stats = sb("stats", [P, 4, 6])
        mv = sb("mv", [P, 4, 2])
        var_e = sb("var_e", [P, 4])
        rstd = sb("rstd", [P, 4])
        one_f = sb("one_f", [P, 1])
        neg_half = sb("neg_half", [P, 4])
        e_base = sb("e_base", [P, NT * NX])
        r1c = sb("r1c", [P, 4, NT])
        g1 = sb("g1", [P, NT])
        g1b = sb("g1b", [P, TT])

        ident_f = consts[:, 0:P]
        upper_f = consts[:, P:2 * P]
        mask = consts[:, 2 * P:2 * P + 512]
        iota8 = consts[:, 768:768 + P]

        qt_hi = [w_hi[:, TOK * i:TOK * (i + 1)] for i in range(2)]
        qt_lo = [w_lo[:, TOK * i:TOK * (i + 1)] for i in range(2)]
        k1_hi, k1_lo = w_hi[:, 1024:2048], w_lo[:, 1024:2048]
        v1_hi, v1_lo = w_hi[:, 2048:3072], w_lo[:, 2048:3072]
        rt = s_sb[0][:, 0:8 * NT * NX].rearrange("p (i c) -> p i c", i=8)
        lg = s_sb[0][:, 1024:1152].rearrange("p (t x) -> p t x", x=NX)
        gates = s_sb[0][:, 1152:1280].rearrange("p (t x) -> p t x", x=NX)
        cnt = s_sb[1][:, 0:2 * NT * NX]
        picks = s_sb[1][:, 256:384].bitcast(BF16).rearrange("p (t x) -> p t x", x=NX)

        xt_f = scr[:, 0:2048].rearrange("p (s c) -> p s c", s=2)
        stage = scr[:, 2048:4096]
        ctx0 = scr[:, 4096:8192].rearrange("p (u q d) -> p u q d", q=TT, d=D0)
        q_st = [scr[:, 8192 + 1024 * i:9216 + 1024 * i].bitcast(BF16) for i in range(2)]
        k_st = [scr[:, 10240 + 1024 * i:11264 + 1024 * i].bitcast(BF16) for i in range(2)]
        q_tok = scr[:, 12288:13312].bitcast(BF16).rearrange("p (c s) -> p c s", s=P)
        k_tok = scr[:, 13312:14336].bitcast(BF16).rearrange("p (c s) -> p c s", s=P)
        wqkv_f = scr[:, 14336:14336 + KE * 3 * E]
        eb_f = scr[0:16, 2048:2176]
        eb_p = scr[0:16, 2176:2368].bitcast(BF16).rearrange("p (i d) -> p i d", i=3)
        eb_r = scr[0:16, 2368:2624].rearrange("p (i d) -> p i d", i=2)
        eb3 = scr[0:3, 15360:16384].bitcast(BF16)
        def tiles(base, n, width, dt=F32):
            return [scr[:, base + width * i:base + width * (i + 1)].bitcast(dt) if dt != F32
                    else scr[:, base + width * i:base + width * (i + 1)] for i in range(n)]

        ta_hi, ta_lo = tiles(0, 4, P, BF16), tiles(512, 4, P, BF16)
        tb_hi, tb_lo = tiles(1024, 4, P, BF16), tiles(1536, 4, P, BF16)
        cc = tiles(8192, 4, E)
        x1 = tiles(9216, 4, E)
        x1b = tiles(10240, 4, E)
        comb = tiles(11264, 4, E)
        x2 = tiles(12288, 4, E)
        ge = tiles(13312, 4, 512)
        ct_hi = scr[:, 0:8192].bitcast(BF16)
        ct_lo = scr[:, 8192:16384].bitcast(BF16)
        x3 = tiles(0, 4, E)
        hf = tiles(1024, 2, 512)
        h_hi, h_lo = tiles(2048, 2, 256, BF16), tiles(2560, 2, 256, BF16)
        x3b = tiles(3072, 4, E)
        y4 = tiles(4096, 4, E)

        bank = [ctx.enter_context(nc.psum_tensor(f"bank{i}", [P, 512], F32)) for i in range(8)]

        ld_w = sem("ld_w")
        ld_x = [sem(f"ld_x{i}") for i in range(2)]
        ld_xtok = sem("ld_xtok")
        ld_c = sem("ld_c")
        ld_b = sem("ld_b")
        ld_ch = [sem(f"ld_ch{i}") for i in range(2)]
        ch_done = sem("ch_done")
        eb_ready = sem("eb_ready")
        eb_moved = sem("eb_moved")
        c_ready = sem("c_ready")
        z_ready = sem("z_ready")
        w_hi_d = sem("w_hi_d")
        w_lo_d = sem("w_lo_d")
        x_hi_d = sem("x_hi_d")
        x_lo_d = sem("x_lo_d")
        pool_seq = sem("pool_seq")
        eb_seq = sem("eb_seq")
        xb_done = sem("xb_done")
        out_done = sem("out_done")

        names = ("pe", "act", "dve", "pool")
        stepped = {n: sem(f"stepped_{n}") for n in names}

        def hold(eng, who, semaphore, value):
            if isinstance(value, int):
                if value > 0:
                    eng.wait_ge(semaphore, value)
            else:
                eng.wait_ge(semaphore, value).then_inc(stepped[who], 1)

        def group_sems(p):
            return {n: sem(f"{p}_{n}") for n in (
                "proj", "stk", "s", "v", "t", "pv", "phi", "plo", "dup", "stka", "stkd", "max", "exp",
                "thi", "tlo", "vc", "rr", "nrm", "ctx", "chi", "clo", "o", "od", "st", "mv", "seq", "rstd", "x")}

        a = group_sems("l0")
        c = group_sems("l1")
        m = {n: sem(f"mix_{n}") for n in (
            "cc", "tp", "thi", "tlo", "o", "r", "agg", "rstd", "x", "xb", "lg", "lgc", "lgd", "ex", "gates",
            "f", "ge", "mul", "out", "dve", "pool")}
        e = {n: sem(f"ffn_{n}") for n in (
            "cc", "tp", "thi", "tlo", "lg", "lgc", "lgd", "ex", "picks", "rank", "gates", "h", "ge", "hhi", "hlo",
            "y", "yr", "xb", "seq",  "agg", "rstd", "x", "dve", "pool")}

        block = ctx.enter_context(nc.Block())

        def loop_groups(eng, body):
            body(0)
            with eng.Fori(1, NT - 1) as g:
                body(g)
            body(NT - 1)

        def is_first(g):
            return isinstance(g, int) and g == 0

        def is_last(g):
            return isinstance(g, int) and g == NT - 1

        def par(g):
            return g % 2

        @block.sync
        def _(sp):
            sp.dma_start(wqkv_f, wqkv_d).then_inc(ld_w, 16)
            for b in range(2):
                sp.dma_start(xt_f[:, b, :], x_t_d[:, b, :]).then_inc(ld_x[b], 16)
            sp.dma_start(consts[:, :], const_d).then_inc(ld_c, 16)
            for cc in range(2):
                sp.dma_start(stage[:, cc * CH:cc * CH + CH], wall_d[:, cc * CH:cc * CH + CH]).then_inc(ld_ch[cc], 16)
            sp.dma_start(x_tok[:, :].rearrange("p (t e) -> p t e", e=E), x_tok_d).then_inc(ld_xtok, 16)
            sp.dma_start(bp_bc[:, :], bp_d.partition_broadcast(P)).then_inc(ld_b, 16)
            sp.dma_start(outb_bc[:, :], outb_d.partition_broadcast(P)).then_inc(ld_b, 16)
            sp.dma_start(b2_bc[:, :], b2_d.partition_broadcast(P)).then_inc(ld_b, 16)
            sp.dma_start(rb_bc[:, :], rb_d.partition_broadcast(P)).then_inc(ld_b, 16)
            sp.dma_start(rw_f[:, 0, :], rw0_d).then_inc(ld_b, 16)
            sp.dma_start(rw_f[:, 1, :], rw1_d).then_inc(ld_b, 16)
            sp.dma_start(b1_col[:, :], b1_d).then_inc(ld_b, 16)
            for b in range(2, NB):
                sp.wait_ge(x_lo_d, b - 1)
                sp.dma_start(xt_f[:, b % 2, :], x_t_d[:, b, :]).then_inc(ld_x[b % 2], 16)
            for cc in range(2, NCH):
                sp.wait_ge(ch_done, cc - 1)
                sp.dma_start(stage[:, (cc % 2) * CH:(cc % 2) * CH + CH],
                             wall_d[:, cc * CH:cc * CH + CH]).then_inc(ld_ch[cc % 2], 16)
            sp.wait_ge(ch_done, NCH)
            sp.dma_start(eb_f, eb_d).then_inc(ld_b, 16)
            sp.wait_ge(eb_ready, 1)
            sp.wait_ge(w_lo_d, 1)
            for i in range(3):
                sp.dma_start(eb3[i:i + 1, :], eb_p[:, i, :]).then_inc(eb_moved, 16)
            for b in range(NB):
                sp.wait_ge(e["x"], TT * (b + 1))
                sp.dma_start(out_d[:, b * TT:(b + 1) * TT, :],
                             x_tok[:, b * TT * E:(b + 1) * TT * E].rearrange("p (t e) -> p t e", e=E)
                             ).then_inc(out_done, 16)
            sp.wait_ge(out_done, 16 * NB)

        @block.tensor
        def _(pe):
            def mm3(out, l_hi, l_lo, r_hi, r_lo, start, stop, check=False):
                pe.matmul(out, l_hi, r_hi, start=start, stop=False, skip_group_check=check)
                pe.matmul(out, l_hi, r_lo, start=False, stop=False, skip_group_check=check)
                return pe.matmul(out, l_lo, r_hi, start=False, stop=stop, skip_group_check=check)

            def l0_project(g):
                t0 = g * P
                b = g // TT
                hold(pe, "pe", x_lo_d, b + 1)
                if is_first(g):
                    pe.wait_ge(w_lo_d, 1)
                hold(pe, "pe", a["stka"], 2 * g)
                hold(pe, "pe", a["stkd"], 2 * g)
                for k in range(KE):
                    last = mm3(bank[4][:, 0:512], xt_hi[:, k, bass.ds(t0, P)], xt_lo[:, k, bass.ds(t0, P)],
                               wqkv_hi[:, k, 0:512], wqkv_lo[:, k, 0:512], k == 0, k == KE - 1)
                last.then_inc(a["proj"], 1)
                for k in range(KE):
                    last = mm3(bank[5][:, 0:E], xt_hi[:, k, bass.ds(t0, P)], xt_lo[:, k, bass.ds(t0, P)],
                               wqkv_hi[:, k, 512:768], wqkv_lo[:, k, 512:768], k == 0, k == KE - 1)
                last.then_inc(a["proj"], 1)

            def l0_stack(g, which):
                tok = (q_tok, k_tok)[which]
                if which == 0:
                    hold(pe, "pe", a["plo"], 2 * g + 2)
                    hold(pe, "pe", a["dup"], 2 * g + 2)
                    if is_first(g):
                        pe.wait_ge(z_ready, 2)
                        pe.wait_ge(c_ready, C_ALL)
                for half in range(2):
                    if which == 1:
                        hold(pe, "pe", a[("stka", "stkd")[half]], 2 * g + 1)
                    out = bank[4 + half][:, :].bitcast(BF16)
                    for i in range(8):
                        last = pe.transpose(out[:, i * P:(i + 1) * P], tok[:, 8 * half + i, :], ident_b[:, :])
                    last.then_inc(a["stk"], 1)

            def l0_scores(g, j, chunk):
                u = g * 4 + j
                if j == 0 and chunk == 0:
                    hold(pe, "pe", a["stka"], 2 * g + 2)
                    hold(pe, "pe", a["stkd"], 2 * g + 2)
                n = 3 * u + chunk
                hold(pe, "pe", a["max"], n - 1)
                for qt, col in S_CHUNKS[chunk]:
                    w = (qt + 1) * P
                    last = pe.matmul(bank[(3 * j + chunk) % 2][:, col:col + w],
                                     q_stv(g)[:, bass.ds(q_off(g) + j * TOK + qt * P, P)],
                                     k_stv(g)[:, bass.ds(q_off(g) + j * TOK, w)], start=True, stop=True)
                last.then_inc(a["s"], 1)

            def q_stv(g):
                return scr[:, 8192:10240].bitcast(BF16)

            def k_stv(g):
                return scr[:, 10240:12288].bitcast(BF16)

            def q_off(g):
                return par(g) * 2048

            def l0_values(g, j):
                u = g * 4 + j
                hold(pe, "pe", a["vc"], u)
                for kt in range(TT):
                    last = pe.matmul(bank[7][:, kt * 32:kt * 32 + 32],
                                     k_stv(g)[:, bass.ds(q_off(g) + j * TOK + kt * P, P)],
                                     ident_b[:, V_HI:V_HI + 2 * D0], start=True, stop=True)
                last.then_inc(a["v"], 1)

            def transposes(s, u, jp, chunk):
                if chunk == 0:
                    hold(pe, "pe", s["nrm"], u + 1) if s is c else hold(pe, "pe", s["exp"], 3 * u + 3)
                hold(pe, "pe", s["tlo"], 3 * u + chunk - 1)
                tb = bank[2 + (jp * 3 + chunk) % 2]
                for kt, qt, col in T_CHUNKS[chunk]:
                    last = pe.transpose(tb[:, col:col + P], s_sb[jp][:, S_OFF[qt] + kt * P:S_OFF[qt] + kt * P + P],
                                        ident_f)
                last.then_inc(s["t"], 1)

            def l0_pv(u, jp):
                hold(pe, "pe", a["tlo"], 3 * u + 3)
                hold(pe, "pe", a["vc"], u + 1)
                hold(pe, "pe", a["ctx"], u)
                for qt in range(TT):
                    out = bank[6][:, qt * D0:(qt + 1) * D0]
                    for kt in range(qt + 1):
                        col = PT_COL[kt, qt]
                        hi, lo = pt_hi[jp][:, col:col + P], pt_lo[jp][:, col:col + P]
                        pe.matmul(out, hi, v0[jp][:, kt, 0:D0], start=(kt == 0), stop=False)
                        pe.matmul(out, hi, v0[jp][:, kt, D0:2 * D0], start=False, stop=False)
                        last = pe.matmul(out, lo, v0[jp][:, kt, 0:D0], start=False, stop=(kt == qt))
                last.then_inc(a["pv"], 1)

            def l0_group(g):
                for j in range(4):
                    u = g * 4 + j
                    first = is_first(g) and j == 0
                    l0_scores(g, j, 0)
                    l0_scores(g, j, 1)
                    if not first:
                        transposes(a, u - 1, (j + 1) % 2, 0)
                        transposes(a, u - 1, (j + 1) % 2, 1)
                    l0_scores(g, j, 2)
                    if not first:
                        transposes(a, u - 1, (j + 1) % 2, 2)
                    l0_values(g, j)
                    if not is_last(g):
                        if j == 0:
                            l0_project(g + 1)
                        if j == 1:
                            l0_stack(g + 1, 0)
                        if j == 2:
                            l0_stack(g + 1, 1)
                    if not first:
                        l0_pv(u - 1, (j + 1) % 2)

            pe.wait_ge(ld_c, 16)
            l0_project(0)
            l0_stack(0, 0)
            l0_stack(0, 1)
            loop_groups(pe, l0_group)
            for chunk in range(3):
                transposes(a, NH - 1, 1, chunk)
            l0_pv(NH - 1, 1)


            def turn(p, use, src):
                hold(pe, "pe", p["tlo"], use[0] + 1)
                for k in range(KE):
                    last = pe.transpose(bank[use[1] % 2][:, k * P:(k + 1) * P], src[:, k * P:(k + 1) * P], ident_f)
                last.then_inc(p["tp"], 1)

            def project(out, t_hi, t_lo, base, n=E):
                for k in range(KE):
                    last = mm3(out, t_hi[:, k * P:(k + 1) * P], t_lo[:, k * P:(k + 1) * P],
                               w_hi[:, base + k * n:base + (k + 1) * n], w_lo[:, base + k * n:base + (k + 1) * n],
                               k == 0, k == KE - 1)
                return last

            pe.wait_ge(ch_done, NCH)
            pe.wait_ge(eb_moved, 48)
            pe.wait_ge(c_ready, C_ALL)
            pe.wait_ge(a["ctx"], NH)
            with pe.Fori(0, NB) as b:
                def use(i):
                    return (USES * b + i, i)

                for t in range(TT):
                    hold(pe, "pe", m["cc"], TT * b + t + 1)
                    turn(m, use(t), cc[t])
                for t in range(TT):
                    hold(pe, "pe", m["tlo"], USES * b + t + 1 + 2)
                    hold(pe, "pe", m["r"], 8 * b + t + 1)
                    project(bank[2 + t % 2][:, 0:E], ta_hi[t], ta_lo[t], WP).then_inc(m["o"], 1)
                for t in range(TT):
                    hold(pe, "pe", m["x"], 8 * b + t + 1)
                    turn(m, use(4 + t), x1[t])
                hold(pe, "pe", m["tlo"], USES * b + 8 + 2)
                hold(pe, "pe", m["ge"], 16 * b + 4)
                for t in range(TT):
                    for k in range(KE):
                        ks = slice(k * NX, (k + 1) * NX)
                        last = mm3(bank[4][:, t * NX:(t + 1) * NX], tb_hi[t][:, k * P:(k + 1) * P],
                                   tb_lo[t][:, k * P:(k + 1) * P], rw_hi[:, 0, ks], rw_lo[:, 0, ks],
                                   k == 0, k == KE - 1)
                last.then_inc(m["lg"], 1)
                hold(pe, "pe", m["lgc"], b + 1)

                def experts(t):
                    for p in range(4):
                        hold(pe, "pe", m["ge"], 16 * b + 4 * t + p + 1)
                        out = bank[4 + p][:, :]
                        pe.matmul(out, ones_b[0:3, :], eb3[:, p * 512:(p + 1) * 512], start=True, stop=False)
                        for k in range(KE):
                            cs = slice(EXPW + k * NX * E + p * 512, EXPW + k * NX * E + (p + 1) * 512)
                            last = mm3(out, tb_hi[t][:, k * P:(k + 1) * P], tb_lo[t][:, k * P:(k + 1) * P],
                                       w_hi[:, cs], w_lo[:, cs], False, k == KE - 1)
                        last.then_inc(m["f"], 1)

                def mixed(t):
                    hold(pe, "pe", m["mul"], 32 * b + 8 * t + 8 + 8)
                    turn(m, use(LATE.index(("cm", t)) + 8), comb[t])

                def out_project(t):
                    hold(pe, "pe", m["tlo"], USES * b + LATE.index(("cm", t)) + 8 + 1 + 2)
                    hold(pe, "pe", m["r"], 8 * b + 4 + t + 1)
                    project(bank[2 + t % 2][:, 0:E], ta_hi[t], ta_lo[t], OUTW).then_inc(m["o"], 1)

                def normed(t):
                    hold(pe, "pe", m["x"], 8 * b + 4 + t + 1)
                    turn(m, use(LATE.index(("x2", t)) + 8), x2[t])

                for t in range(TT):
                    experts(t)
                    if t >= 1:
                        mixed(t - 1)
                    if t >= 2:
                        normed(t - 2)
                    if t >= 1:
                        out_project(t - 1)
                mixed(TT - 1)
                normed(TT - 2)
                out_project(TT - 1)
                normed(TT - 1)

            def l1_project(which, g, use, j=0):
                tok = (g // 4) * TOK
                hold(pe, "pe", c["plo"], use)
                out = bank[4]
                if which == "v":
                    for tt in range(TT):
                        for k in range(KE):
                            base = WKV + k * 1024 + 512
                            last = mm3(out[:, tt * P:(tt + 1) * P],
                                       xt_hi[:, k, bass.ds(tok + tt * P, P)], xt_lo[:, k, bass.ds(tok + tt * P, P)],
                                       w_hi[:, bass.ds(base + (g % 4) * P, P)],
                                       w_lo[:, bass.ds(base + (g % 4) * P, P)], k == 0, k == KE - 1)
                else:
                    for k in range(KE):
                        base = WKV + k * 1024 + (g % 4) * P if which == "k" else WQ + k * 2048 + (g % 4) * TOK + j * P
                        last = mm3(out[:, :], w_hi[:, bass.ds(base, P)], w_lo[:, bass.ds(base, P)],
                                   xt_hi[:, k, bass.ds(tok, TOK)], xt_lo[:, k, bass.ds(tok, TOK)],
                                   k == 0, k == KE - 1)
                last.then_inc(c["proj"], 1)

            def l1_scores(g, j, chunk):
                u = 4 * g + j
                if chunk == 0:
                    hold(pe, "pe", c["plo"], proj_use(g, j) + 1)
                n = 3 * u + chunk
                hold(pe, "pe", c["max"], n - 1)
                kb = (g % 2) * TOK
                for qt, col in S_CHUNKS[chunk]:
                    w = (qt + 1) * P
                    qs = slice(qt * P, (qt + 1) * P)
                    last = mm3(bank[(3 * j + chunk) % 2][:, col:col + w], qt_hi[j % 2][:, qs], qt_lo[j % 2][:, qs],
                               k1_hi[:, bass.ds(kb, w)], k1_lo[:, bass.ds(kb, w)], True, True)
                last.then_inc(c["s"], 1)

            def l1_pv(g, j):
                u = 4 * g + j
                hold(pe, "pe", c["tlo"], 3 * u + 3)
                hold(pe, "pe", c["clo"], u)
                vb = (g % 2) * TOK
                for kt in range(TT):
                    col = PT_COL[kt, kt]
                    w = TOK - kt * P
                    ps = slice(col, col + w)
                    vs = bass.ds(vb + kt * P, P)
                    out = bank[6][:, kt * P:TOK]
                    pe.matmul(out, v1_hi[:, vs], pt_hi[j % 2][:, ps], start=(kt == 0), stop=False)
                    pe.matmul(out, v1_hi[:, vs], pt_lo[j % 2][:, ps], start=False, stop=False)
                    last = pe.matmul(out, v1_lo[:, vs], pt_hi[j % 2][:, ps], start=False, stop=(kt == TT - 1))
                last.then_inc(c["pv"], 1)

            def l1_dense(g, part, parts, ready):
                hold(pe, "pe", c["clo"], ready)
                if part == 0:
                    hold(pe, "pe", c["od"], g - TT + 1)
                cb = ((g // 4 + 1) % 2) * HEADS * TOK + (g % 4) * P
                edges = [HEADS * i // parts for i in range(parts + 1)]
                for hd in range(edges[part], edges[part + 1]):
                    cs = bass.ds(cb + hd * TOK, P)
                    ws = slice(WD + hd * E, WD + (hd + 1) * E)
                    last = mm3(bank[7][:, 0:E], ct_hi[:, cs], ct_lo[:, cs], w_hi[:, ws], w_lo[:, ws],
                               hd == 0, hd == HEADS - 1)
                if part == parts - 1:
                    last.then_inc(c["o"], 1)

            def l1_group(g, dense):
                for j in range(4):
                    u = 4 * g + j
                    first = is_first(g) and j == 0
                    gp, jp = (g, j - 1) if j else (g - 1, 3)
                    l1_scores(g, j, 0)
                    l1_scores(g, j, 1)
                    if not first:
                        transposes(c, u - 1, (j + 1) % 2, 0)
                        transposes(c, u - 1, (j + 1) % 2, 1)
                    if not (is_last(g) and j == 3):
                        gn, jn = (g, j + 1) if j < 3 else (g + 1, 0)
                        l1_project("q", gn, proj_use(gn, jn), jn)
                    l1_scores(g, j, 2)
                    if not first:
                        transposes(c, u - 1, (j + 1) % 2, 2)
                    if dense and j < 3:
                        l1_dense(g, j, 3, u - 1)
                    if not is_last(g) and j < 2:
                        l1_project("kv"[j], g + 1, 3 + 6 * g + 2 * j + 1)
                    if not first:
                        l1_pv(gp, jp)

            pe.wait_ge(m["tlo"], USES * NB + 2)
            l1_project("k", 0, 0)
            l1_project("v", 0, 1)
            l1_project("q", 0, 2)
            l1_group(0, False)
            with pe.Fori(1, TT) as g:
                l1_group(g, False)
            with pe.Fori(TT, NT - 1) as g:
                l1_group(g, True)
            l1_group(NT - 1, True)
            for chunk in range(3):
                transposes(c, NH - 1, 1, chunk)
            l1_pv(NT - 1, 3)
            with pe.Fori(NT, NT + TT) as g:
                l1_dense(g, 0, 1, NH)

            pe.wait_ge(c["x"], NT)
            with pe.Fori(0, NB) as b:
                for t in range(TT):
                    hold(pe, "pe", e["cc"], TT * b + t + 1)
                    turn(e, (TT * b + t, t), x3[t])
                hold(pe, "pe", e["tlo"], TT * b + TT + 2)
                hold(pe, "pe", e["lgc"], b + 1)
                for t in range(TT):
                    tok = b * TOK + t * P
                    for k in range(KE):
                        ks = slice(k * NX, (k + 1) * NX)
                        last = mm3(bank[2][:, t * NX:(t + 1) * NX], xt_hi[:, k, bass.ds(tok, P)],
                                   xt_lo[:, k, bass.ds(tok, P)], rw_hi[:, 1, ks], rw_lo[:, 1, ks],
                                   k == 0, k == KE - 1)
                last.then_inc(e["lg"], 1)
            pe.wait_ge(e["picks"], 2)
            pe.matmul(bank[3][:, 0:2 * NT * NX], upper_b[:, :], picks[:, :, :], start=True, stop=False)
            for n in range(2 * NT - 1):
                after = 2 * NT - 1 - n
                last = pe.matmul(bank[3][:, (n + 1) * NX:2 * NT * NX], ones_b[:, :],
                                 picks[:, n:n + 1, :].to_broadcast([P, after, NX]),
                                 start=False, stop=(after == 1))
            last.then_inc(e["rank"], 1)
            pe.sem_inc(e["y"], 2)
            with pe.Fori(0, NB) as b:
                def outputs(i):
                    hold(pe, "pe", e["hlo"], NF * b + i + 1)
                    if i == 0:
                        hold(pe, "pe", e["yr"], TT * b + 1)
                    for t in range(TT):
                        ts = slice(t * P, (t + 1) * P)
                        ws = slice(W2 + i * E, W2 + (i + 1) * E)
                        last = mm3(bank[6 + t // 2][:, (t % 2) * E:(t % 2 + 1) * E], h_hi[i % 2][:, ts],
                                   h_lo[i % 2][:, ts], w_hi[:, ws], w_lo[:, ws],
                                   i == 0 and t % 2 == 0, i == NF - 1 and t % 2 == 1, True)
                    last.then_inc(e["y"], 1)

                for i in range(NF):
                    hold(pe, "pe", e["ge"], NF * b + i + 1)
                    for k in range(KE):
                        ws = slice(W1 + k * FF + i * P, W1 + k * FF + (i + 1) * P)
                        last = mm3(bank[4 + i % 2][:, :], w_hi[:, ws], w_lo[:, ws],
                                   xt_hi[:, k, bass.ds(b * TOK, TOK)], xt_lo[:, k, bass.ds(b * TOK, TOK)],
                                   k == 0, k == KE - 1)
                    last.then_inc(e["h"], 1)
                    if i >= 1:
                        outputs(i - 1)
                outputs(NF - 1)

        @block.scalar
        def _(act):
            def copy(out, in_):
                return act.activation(out, in_, ACT.Copy)

            act.wait_ge(ld_w, 16)
            copy(wqkv_hi[:, :, :].rearrange("p k n -> p (k n)"), wqkv_f).then_inc(w_hi_d, 1)

            def x_high(b):
                act.wait_ge(ld_x[b % 2], 16 * (b // 2 + 1))
                copy(xt_hi[:, :, b * TOK:(b + 1) * TOK], xt_f[:, b % 2, :].rearrange("p (k t) -> p k t", k=KE)
                     ).then_inc(x_hi_d, 1)

            def l0_parts_high(g):
                hold(act, "act", a["stk"], 4 * g)
                hold(act, "act", a["proj"], 2 * g + 1)
                copy(q_tok[:, :, Q_HI:Q_HI + D0], bank[4][:, 0:E].rearrange("p (c d) -> p c d", d=D0))
                copy(k_tok[:, :, K_HI:K_HI + D0], bank[4][:, E:2 * E].rearrange("p (c d) -> p c d", d=D0)
                     ).then_inc(a["phi"], 1)
                hold(act, "act", a["proj"], 2 * g + 2)
                copy(k_tok[:, :, V_HI:V_HI + D0], bank[5][:, 0:E].rearrange("p (c d) -> p c d", d=D0)
                     ).then_inc(a["phi"], 1)

            def l0_rows_even(g, which):
                hold(act, "act", a["stk"], 4 * g + 2 * which + 1)
                rows = (Q_ROWS, K_ROWS)[which]
                base = (8192, 10240)[which]
                dst = scr[:, base:base + 2048].bitcast(BF16)
                copy(dst[0:rows, bass.ds((g % 2) * 2048, 2048)].rearrange("p (t c) -> p t c", c=16)[:, :, 0:8],
                     bank[4][:, :].bitcast(BF16).rearrange("p (c t) -> p t c", t=P)[0:rows]
                     ).then_inc(a["stka"], 1)

            def exponentials(s, g, j, chunk):
                u = 4 * g + j
                hold(act, "act", s["max"], 3 * u + chunk + 1)
                if chunk == 0:
                    hold(act, "act", s["rr"], u - 1)
                for qt, _ in S_CHUNKS[chunk]:
                    at = s_sb[j % 2][:, S_OFF[qt]:S_OFF[qt] + (qt + 1) * P]
                    last = act.activation(at, at, ACT.Exp, bias=nm[:, j % 2, qt:qt + 1], scale=-1.0,
                                          accum_out=rs[:, j % 2, qt:qt + 1])
                last.then_inc(s["exp"], 1)

            def probs_high(s, u, jp, chunk):
                hold(act, "act", s["t"], 3 * u + chunk + 1)
                if chunk == 0:
                    hold(act, "act", s["pv"], u - 1)
                w = T_LEN[chunk]
                copy(pt_hi[jp][:, T_OFF[chunk]:T_OFF[chunk] + w], bank[2 + (3 * jp + chunk) % 2][:, 0:w]
                     ).then_inc(s["thi"], 1)

            def l0_group(g):
                for j in range(4):
                    u = 4 * g + j
                    first = is_first(g) and j == 0
                    for chunk in range(3):
                        exponentials(a, g, j, chunk)
                        if not first:
                            probs_high(a, u - 1, (j + 1) % 2, chunk)
                    hold(act, "act", a["v"], u + 1)
                    hold(act, "act", a["pv"], u - 1)
                    copy(v0[j % 2][:, :, :].rearrange("p k d -> p (k d)"), bank[7][:, 0:P]).then_inc(a["vc"], 1)
                    if not is_last(g):
                        if j == 0:
                            l0_parts_high(g + 1)
                        if j in (1, 2):
                            l0_rows_even(g + 1, j - 1)

            x_high(0)
            l0_parts_high(0)
            x_high(1)
            act.wait_ge(z_ready, 2)
            l0_rows_even(0, 0)
            l0_rows_even(0, 1)
            x_high(2)
            x_high(3)
            loop_groups(act, l0_group)
            for chunk in range(3):
                probs_high(a, NH - 1, 1, chunk)

            def turned_high(p, dst, use):
                hold(act, "act", p["tp"], use[0] + 1)
                copy(dst, bank[use[1] % 2][:, 0:E].rearrange("p (k t) -> p k t", k=KE)).then_inc(p["thi"], 1)

            def kt(ap):
                return ap.rearrange("p (k t) -> p k t", k=KE)

            act.wait_ge(a["ctx"], NH)
            act.sem_inc(m["ge"], 4)
            with act.Fori(0, NB) as b:
                def use(i):
                    return (USES * b + i, i)

                for t in range(TT):
                    hold(act, "act", m["tlo"], USES * b + 2)
                    copy(cc[t].rearrange("p (h d) -> p h d", d=D0),
                         ctx0[:, bass.ds(b * HEADS, HEADS), t, :]).then_inc(m["cc"], 1)
                for t in range(TT):
                    turned_high(m, kt(ta_hi[t]), use(t))
                for t in range(TT):
                    turned_high(m, kt(tb_hi[t]), use(4 + t))

                def gelus(t):
                    for p in range(4):
                        hold(act, "act", m["f"], 16 * b + 4 * t + p + 1)
                        hold(act, "act", m["mul"], 32 * b + 8 * t + 2 * p + 2)
                        act.activation(ge[p], bank[4 + p][:, :], ACT.Gelu_apprx_tanh).then_inc(m["ge"], 1)

                def late(kind, t):
                    i = LATE.index((kind, t)) + 8
                    if kind == "cm":
                        turned_high(m, kt(ta_hi[t]), use(i))
                    else:
                        turned_high(m, xt_hi[:, :, bass.ds(b * TOK + t * P, P)], use(i))
                        copy(x_tok[:, bass.ds(b * TT * E + t * E, E)], x2[t]).then_inc(m["out"], 1)

                for t in range(TT):
                    gelus(t)
                    if t >= 1:
                        late("cm", t - 1)
                    if t >= 2:
                        late("x2", t - 2)
                late("cm", TT - 1)
                late("x2", TT - 2)
                late("x2", TT - 1)

            def l1_high(which, g, use, j=0):
                hold(act, "act", c["proj"], use + 1)
                dst = {"q": lambda: qt_hi[j % 2][:, :], "k": lambda: k1_hi[:, bass.ds((g % 2) * TOK, TOK)],
                       "v": lambda: v1_hi[:, bass.ds((g % 2) * TOK, TOK)]}[which]()
                copy(dst, bank[4][:, :]).then_inc(c["phi"], 1)

            def l1_context_high(g, j):
                u = 4 * g + j
                hold(act, "act", c["pv"], u + 1)
                at = ((g // 4) % 2) * HEADS * TOK + (g % 4) * 4 * TOK + j * TOK
                copy(ct_hi[:, bass.ds(at, TOK)], bank[6][:, :]).then_inc(c["chi"], 1)

            def l1_group(g):
                for j in range(4):
                    u = 4 * g + j
                    first = is_first(g) and j == 0
                    exponentials(c, g, j, 0)
                    if not first:
                        probs_high(c, u - 1, (j + 1) % 2, 0)
                    exponentials(c, g, j, 1)
                    if not first:
                        probs_high(c, u - 1, (j + 1) % 2, 1)
                    if not (is_last(g) and j == 3):
                        gn, jn = (g, j + 1) if j < 3 else (g + 1, 0)
                        l1_high("q", gn, proj_use(gn, jn), jn)
                    exponentials(c, g, j, 2)
                    if not first:
                        probs_high(c, u - 1, (j + 1) % 2, 2)
                    if not is_last(g) and j < 2:
                        l1_high("kv"[j], g + 1, 3 + 6 * g + 2 * j + 1)
                    if not first:
                        l1_context_high(*((g, j - 1) if j else (g - 1, 3)))

            for i, which in enumerate("kvq"):
                l1_high(which, 0, i)
            loop_groups(act, l1_group)
            for chunk in range(3):
                probs_high(c, NH - 1, 1, chunk)
            l1_context_high(NT - 1, 3)

            act.wait_ge(c["x"], NT)
            with act.Fori(0, NB) as b:
                hold(act, "act", e["tlo"], TT * b + 2)
                for t in range(TT):
                    copy(x3[t], x_tok[:, bass.ds(b * TT * E + t * E, E)]).then_inc(e["cc"], 1)
                for t in range(TT):
                    turned_high(e, xt_hi[:, :, bass.ds(b * TOK + t * P, P)], (TT * b + t, t))
            act.sem_inc(e["ge"], 2)
            act.wait_ge(ld_b, 8 * 16)
            with act.Fori(0, NB) as b:
                for i in range(NF):
                    n = NF * b + i
                    hold(act, "act", e["h"], n + 1)
                    hold(act, "act", e["y"], n + 1)
                    act.activation(hf[i % 2], bank[4 + i % 2][:, :], ACT.Gelu, bias=b1_col[:, i:i + 1]
                                   ).then_inc(e["ge"], 1)
                    hold(act, "act", e["ge"], n + 1 + 2)
                    copy(h_hi[i % 2], hf[i % 2]).then_inc(e["hhi"], 1)

        class Chain:

            def __init__(self, eng, who, semaphore, base):
                self.eng, self.who, self.sem, self.base, self.n = eng, who, semaphore, base, 0

            def __call__(self, ins):
                ins.then_inc(self.sem, 1)
                self.n += 1
                hold(self.eng, self.who, self.sem, self.base + self.n)

        def router(dve, chain, logits, n, ex_ready, lgd, ex, turn):
            w = n * NX

            def row(i):
                return rt[:, i, 0:w].rearrange("p (t x) -> p t x", x=NX)

            def wide(i):
                return r1c[:, i, 0:n].unsqueeze(2).to_broadcast([P, n, NX])

            rev = iota8[:, 0:w].rearrange("p (t x) -> p t x", x=NX)
            top = [r1c[:, i, 0:n] for i in range(4)]
            chain(dve.tensor_reduce(top[2], logits, AX.X, ALU.max))
            dve.tensor_tensor(row(0), logits, wide(2), ALU.subtract).then_inc(lgd, 1)
            hold(dve, "dve", ex, turn)
            chain(dve.tensor_reduce(top[2], row(1), AX.X, ALU.add))
            chain(dve.reciprocal(top[3], top[2]))
            chain(dve.tensor_tensor(row(2), row(1), wide(3), ALU.mult))
            for i, (src, ones) in enumerate(((2, 5), (3, 6))):
                chain(dve.tensor_reduce(top[i], row(src), AX.X, ALU.max))
                chain(dve.tensor_tensor(row(4), row(src), wide(i), ALU.is_equal))
                chain(dve.tensor_tensor(row(4), row(4), rev, ALU.mult))
                chain(dve.tensor_reduce(top[2], row(4), AX.X, ALU.max))
                chain(dve.tensor_tensor(row(ones), rev, wide(2), ALU.is_equal))
                if i == 0:
                    chain(dve.scalar_tensor_tensor(rt[:, 3, 0:w], rt[:, 5, 0:w], -2.0, rt[:, 2, 0:w],
                                                   ALU.mult, ALU.add))
            return row, wide, top

        @block.vector
        def _(dve):
            def low(out, bank_cols, hi):
                return dve.tensor_tensor(out, bank_cols, hi, ALU.subtract)

            dve.memset(scr[:, 12288:14336], 0.0).then_inc(z_ready, 1)
            dve.memset(scr[:, 8192:12288], 0.0).then_inc(z_ready, 1)
            dve.wait_ge(z_ready, 2)
            dve.wait_ge(w_hi_d, 1)
            low(wqkv_lo[:, :, :].rearrange("p k n -> p (k n)"), wqkv_f,
                wqkv_hi[:, :, :].rearrange("p k n -> p (k n)")).then_inc(w_lo_d, 1)

            def x_low(b):
                dve.wait_ge(x_hi_d, b + 1)
                low(xt_lo[:, :, b * TOK:(b + 1) * TOK], xt_f[:, b % 2, :].rearrange("p (k t) -> p k t", k=KE),
                    xt_hi[:, :, b * TOK:(b + 1) * TOK]).then_inc(x_lo_d, 1)

            def l0_parts_low(g):
                hold(dve, "dve", a["phi"], 2 * g + 1)
                low(q_tok[:, :, Q_LO:Q_LO + D0], bank[4][:, 0:E].rearrange("p (c d) -> p c d", d=D0),
                    q_tok[:, :, Q_HI:Q_HI + D0])
                low(k_tok[:, :, K_LO:K_LO + D0], bank[4][:, E:2 * E].rearrange("p (c d) -> p c d", d=D0),
                    k_tok[:, :, K_HI:K_HI + D0]).then_inc(a["plo"], 1)
                hold(dve, "dve", a["phi"], 2 * g + 2)
                low(k_tok[:, :, V_LO:V_LO + D0], bank[5][:, 0:E].rearrange("p (c d) -> p c d", d=D0),
                    k_tok[:, :, V_HI:V_HI + D0]).then_inc(a["plo"], 1)

            def l0_rows_odd(g, which):
                hold(dve, "dve", a["stk"], 4 * g + 2 * which + 2)
                rows = (Q_ROWS, K_ROWS)[which]
                base = (8192, 10240)[which]
                dst = scr[:, base:base + 2048].bitcast(BF16)
                dve.tensor_copy(
                    dst[0:rows, bass.ds((g % 2) * 2048, 2048)].rearrange("p (t c) -> p t c", c=16)[:, :, 8:16],
                    bank[5][:, :].bitcast(BF16).rearrange("p (c t) -> p t c", t=P)[0:rows]).then_inc(a["stkd"], 1)

            def maxima(s, g, j, chunk, scale):
                u = 4 * g + j
                hold(dve, "dve", s["s"], 3 * u + chunk + 1)
                for qt, col in S_CHUNKS[chunk]:
                    w = (qt + 1) * P
                    last = dve.tensor_tensor_reduce(
                        s_sb[j % 2][:, S_OFF[qt]:S_OFF[qt] + w], bank[(3 * j + chunk) % 2][:, col:col + w],
                        mask[:, 512 - w:512], -scale, HUGE, ALU.add, ALU.min, nm[:, j % 2, qt:qt + 1])
                last.then_inc(s["max"], 1)

            def probs_low(s, u, jp, chunk):
                hold(dve, "dve", s["thi"], 3 * u + chunk + 1)
                w = T_LEN[chunk]
                at = slice(T_OFF[chunk], T_OFF[chunk] + w)
                low(pt_lo[jp][:, at], bank[2 + (3 * jp + chunk) % 2][:, 0:w], pt_hi[jp][:, at]).then_inc(s["tlo"], 1)

            def inverse_sums(s, u, jp):
                hold(dve, "dve", s["exp"], 3 * u + 3)
                dve.reciprocal(rr[:, jp, :], rs[:, jp, :]).then_inc(s["rr"], 1)

            def l0_context(u, jp):
                inverse_sums(a, u, jp)
                hold(dve, "dve", a["rr"], u + 1)
                hold(dve, "dve", a["pv"], u + 1)
                dve.tensor_tensor(ctx0[:, bass.ds(u, 1), :, :].rearrange("p u q d -> p (u q) d"),
                                  bank[6][:, 0:TT * D0].rearrange("p (q d) -> p q d", d=D0),
                                  rr[:, jp, :].unsqueeze(2).to_broadcast([P, TT, D0]), ALU.mult
                                  ).then_inc(a["ctx"], 1)

            def l0_group(g):
                for j in range(4):
                    u = 4 * g + j
                    first = is_first(g) and j == 0
                    jp = (j + 1) % 2
                    maxima(a, g, j, 0, D0 ** -0.5)
                    maxima(a, g, j, 1, D0 ** -0.5)
                    if not first:
                        probs_low(a, u - 1, jp, 0)
                    maxima(a, g, j, 2, D0 ** -0.5)
                    if not first:
                        probs_low(a, u - 1, jp, 1)
                        probs_low(a, u - 1, jp, 2)
                    if not is_last(g):
                        if j == 0:
                            l0_parts_low(g + 1)
                        if j in (1, 2):
                            l0_rows_odd(g + 1, j - 1)
                    if not first:
                        l0_context(u - 1, jp)

            x_low(0)
            l0_parts_low(0)
            x_low(1)
            l0_rows_odd(0, 0)
            l0_rows_odd(0, 1)
            x_low(2)
            x_low(3)
            dve.wait_ge(ld_c, 16)
            loop_groups(dve, l0_group)
            for chunk in range(3):
                probs_low(a, NH - 1, 1, chunk)
            l0_context(NH - 1, 1)

            def turned_low(p, dst, hi, use):
                hold(dve, "dve", p["thi"], use[0] + 1)
                low(dst, bank[use[1] % 2][:, 0:E].rearrange("p (k t) -> p k t", k=KE), hi).then_inc(p["tlo"], 1)

            def kt(ap):
                return ap.rearrange("p (k t) -> p k t", k=KE)

            dve.sem_inc(m["tlo"], 2)
            dve.sem_inc(m["r"], 2)
            dve.sem_inc(m["mul"], 8)
            dve.sem_inc(m["out"], 1)
            dve.wait_ge(a["ctx"], NH)
            dve.wait_ge(xb_done, NB)
            M_CHAIN = 15 + 8 + 6
            with dve.Fori(0, NB) as b:
                chain = Chain(dve, "dve", m["dve"], M_CHAIN * b)

                def use(i):
                    return (USES * b + i, i)

                def joined(t, n, src, out, add):
                    hold(dve, "dve", m["o"], 8 * b + n + 1)
                    dve.tensor_tensor(out, src, add, ALU.add).then_inc(m["r"], 1)
                    hold(dve, "dve", m["r"], 8 * b + n + 1 + 2)
                    chain(dve.bn_stats(stats[:, t, :], out))
                    dve.bn_aggr(mv[:, t, :], stats[:, t, :]).then_inc(m["agg"], 1)

                def norm(t, n, rows):
                    hold(dve, "dve", m["rstd"], 8 * b + n + 1)
                    dve.tensor_scalar(rows, rows, mv[:, t, 0:1], rstd[:, t:t + 1], ALU.subtract, ALU.mult
                                      ).then_inc(m["x"], 1)

                for t in range(TT):
                    turned_low(m, kt(ta_lo[t]), kt(ta_hi[t]), use(t))
                for t in range(TT):
                    joined(t, t, bank[2 + t % 2][:, 0:E], x1[t], x_tok[:, bass.ds(b * TT * E + t * E, E)])
                for t in range(TT):
                    norm(t, t, x1[t])
                for t in range(TT):
                    turned_low(m, kt(tb_lo[t]), kt(tb_hi[t]), use(4 + t))
                hold(dve, "dve", m["lg"], b + 1)
                dve.tensor_tensor(lg[:, 0:TT, :], bank[4][:, 0:TT * NX].rearrange("p (t x) -> p t x", x=NX),
                                  rb_bc[:, :].unsqueeze(1).to_broadcast([P, TT, NX]), ALU.add).then_inc(m["lgc"], 1)
                hold(dve, "dve", m["lgc"], b + 1)
                row, wide, top = router(dve, chain, lg[:, 0:TT, :], TT, None, m["lgd"], m["ex"], b + 1)
                chain(dve.tensor_tensor(top[2], top[0], top[1], ALU.add))
                chain(dve.reciprocal(top[3], top[2]))
                chain(dve.tensor_tensor(row(0), row(5), wide(0), ALU.mult))
                chain(dve.tensor_tensor(row(1), row(6), wide(1), ALU.mult))
                chain(dve.tensor_tensor(row(0), row(0), row(1), ALU.add))
                chain(dve.tensor_tensor(gates[:, 0:TT, :], row(0), wide(3), ALU.mult))
                hold(dve, "dve", m["out"], TT * b + 1)

                def mix(t):
                    for x in range(NX):
                        p = x // 2
                        hold(dve, "dve", m["ge"], 16 * b + 4 * t + p + 1 + 4)
                        part = ge[p][:, (x % 2) * E:(x % 2 + 1) * E]
                        gate = gates[:, t, x:x + 1]
                        if x == 0:
                            ins = dve.tensor_scalar(comb[t], part, gate, None, ALU.mult)
                        else:
                            hold(dve, "dve", m["mul"], 32 * b + 8 * t + x + 8)
                            ins = dve.scalar_tensor_tensor(comb[t], part, gate, comb[t], ALU.mult, ALU.add)
                        ins.then_inc(m["mul"], 1)

                def late(kind, t):
                    i = LATE.index((kind, t)) + 8
                    if kind == "cm":
                        turned_low(m, kt(ta_lo[t]), kt(ta_hi[t]), use(i))
                    else:
                        ts = bass.ds(b * TOK + t * P, P)
                        turned_low(m, xt_lo[:, :, ts], xt_hi[:, :, ts], use(i))

                def second(t):
                    hold(dve, "dve", m["xb"], TT * b + t + 1)
                    joined(t, 4 + t, bank[2 + t % 2][:, 0:E], x2[t], x1b[t])

                for t in range(TT):
                    if t >= 2:
                        norm(t - 2, 4 + t - 2, x2[t - 2])
                    mix(t)
                    if t >= 1:
                        late("cm", t - 1)
                    if t >= 2:
                        late("x2", t - 2)
                    if t >= 1:
                        second(t - 1)
                norm(2, 6, x2[2])
                late("cm", 3)
                late("x2", 2)
                second(3)
                norm(3, 7, x2[3])
                late("x2", 3)
                assert chain.n == M_CHAIN, chain.n

            dve.wait_ge(m["out"], NT + 1)

            def l1_low(which, g, use, j=0):
                hold(dve, "dve", c["phi"], use + 1)
                half = (g % 2) * TOK
                lo, hi = {"q": lambda: (qt_lo[j % 2][:, :], qt_hi[j % 2][:, :]),
                          "k": lambda: (k1_lo[:, bass.ds(half, TOK)], k1_hi[:, bass.ds(half, TOK)]),
                          "v": lambda: (v1_lo[:, bass.ds(half, TOK)], v1_hi[:, bass.ds(half, TOK)])}[which]()
                low(lo, bank[4][:, :], hi).then_inc(c["plo"], 1)

            def l1_context_low(g, j):
                u = 4 * g + j
                hold(dve, "dve", c["chi"], u + 1)
                at = ((g // 4) % 2) * HEADS * TOK + (g % 4) * 4 * TOK + j * TOK
                low(ct_lo[:, bass.ds(at, TOK)], bank[6][:, :], ct_hi[:, bass.ds(at, TOK)]).then_inc(c["clo"], 1)

            def l1_norm(t):
                rows = x_tok[:, bass.ds(t * E, E)]
                hold(dve, "dve", c["o"], t + 1)
                dve.tensor_tensor(rows, bank[7][:, 0:E], rows, ALU.add).then_inc(c["od"], 1)
                hold(dve, "dve", c["od"], t + 2)
                dve.bn_stats(stats[:, 0, :], rows).then_inc(c["st"], 1)
                hold(dve, "dve", c["st"], t + 1)
                dve.bn_aggr(mv[:, 0, :], stats[:, 0, :]).then_inc(c["mv"], 1)
                hold(dve, "dve", c["rstd"], t + 1)
                dve.tensor_scalar(rows, rows, mv[:, 0, 0:1], rstd[:, 0:1], ALU.subtract, ALU.mult
                                  ).then_inc(c["x"], 1)

            def l1_group(g, dense):
                for j in range(4):
                    u = 4 * g + j
                    first = is_first(g) and j == 0
                    jp = (j + 1) % 2
                    maxima(c, g, j, 0, D1 ** -0.5)
                    maxima(c, g, j, 1, D1 ** -0.5)
                    if not first:
                        probs_low(c, u - 1, jp, 0)
                    if not (is_last(g) and j == 3):
                        gn, jn = (g, j + 1) if j < 3 else (g + 1, 0)
                        l1_low("q", gn, proj_use(gn, jn), jn)
                    maxima(c, g, j, 2, D1 ** -0.5)
                    if not first:
                        probs_low(c, u - 1, jp, 1)
                        probs_low(c, u - 1, jp, 2)
                    inverse_sums(c, u, j % 2)
                    if not is_last(g) and j < 2:
                        l1_low("kv"[j], g + 1, 3 + 6 * g + 2 * j + 1)
                    if not first:
                        l1_context_low(*((g, j - 1) if j else (g - 1, 3)))
                if dense:
                    l1_norm(g - TT)

            dve.sem_inc(c["od"], 1)
            for i, which in enumerate("kvq"):
                l1_low(which, 0, i)
            l1_group(0, False)
            with dve.Fori(1, TT) as g:
                l1_group(g, False)
            with dve.Fori(TT, NT - 1) as g:
                l1_group(g, True)
            l1_group(NT - 1, True)
            for chunk in range(3):
                probs_low(c, NH - 1, 1, chunk)
            l1_context_low(NT - 1, 3)
            with dve.Fori(NT, NT + TT) as g:
                l1_norm(g - TT)

            dve.wait_ge(c["x"], NT)
            dve.sem_inc(e["tlo"], 2)
            dve.sem_inc(e["lgc"], 1)
            with dve.Fori(0, NB) as b:
                for t in range(TT):
                    ts = bass.ds(b * TOK + t * P, P)
                    turned_low(e, xt_lo[:, :, ts], xt_hi[:, :, ts], (TT * b + t, t))
                hold(dve, "dve", e["lg"], b + 1)
                dve.tensor_copy(lg[:, bass.ds(b * TT, TT), :],
                                bank[2][:, 0:TT * NX].rearrange("p (t x) -> p t x", x=NX)).then_inc(e["lgc"], 1)
            dve.wait_ge(e["lgc"], NB + 1)
            chain = Chain(dve, "dve", e["dve"], 0)
            row, wide, top = router(dve, chain, lg[:, :, :], NT, None, e["lgd"], e["ex"], 1)
            for i in range(2):
                dve.tensor_copy(picks[:, i * NT:(i + 1) * NT, :], row(5 + i)).then_inc(e["picks"], 1)
            dve.wait_ge(e["rank"], 1)
            chain(dve.tensor_scalar(cnt[:, :], bank[3][:, 0:2 * NT * NX], float(CAP), None, ALU.is_le))
            for i in range(2):
                chain(dve.tensor_tensor(row(i), cnt[:, i * NT * NX:(i + 1) * NT * NX].rearrange(
                    "p (t x) -> p t x", x=NX), row(5 + i), ALU.mult))
                chain(dve.tensor_reduce(top[2 + i], row(i), AX.X, ALU.add))
                chain(dve.tensor_tensor(top[2 + i], top[2 + i], top[i], ALU.mult))
            dve.tensor_tensor(g1[:, :], top[2], top[3], ALU.add).then_inc(e["gates"], 1)

            dve.sem_inc(e["yr"], 1)
            dve.wait_ge(e["gates"], 1)
            with dve.Fori(0, NB) as b:
                chain = Chain(dve, "dve", e["dve"], E_CHAIN + TT * b)
                for i in range(NF):
                    hold(dve, "dve", e["hhi"], NF * b + i + 1)
                    low(h_lo[i % 2], hf[i % 2], h_hi[i % 2]).then_inc(e["hlo"], 1)
                hold(dve, "dve", e["y"], NF * (b + 1) + 2)
                for t in range(TT):
                    hold(dve, "dve", e["xb"], TT * b + t + 1)
                    dve.scalar_tensor_tensor(y4[t], bank[6 + t // 2][:, (t % 2) * E:(t % 2 + 1) * E], g1b[:, t:t + 1],
                                             x3b[t], ALU.mult, ALU.add).then_inc(e["yr"], 1)
                    hold(dve, "dve", e["yr"], TT * b + t + 2)
                    chain(dve.bn_stats(stats[:, t, :], y4[t]))
                    dve.bn_aggr(mv[:, t, :], stats[:, t, :]).then_inc(e["agg"], 1)
                for t in range(TT):
                    hold(dve, "dve", e["rstd"], TT * b + t + 1)
                    dve.tensor_scalar(x_tok[:, bass.ds(b * TT * E + t * E, E)], y4[t], mv[:, t, 0:1],
                                      rstd[:, t:t + 1], ALU.subtract, ALU.mult).then_inc(e["x"], 1)

        @block.gpsimd
        def _(pool):
            pool.memset(one_f[:, :], 1.0).then_inc(c_ready, 1)
            pool.memset(neg_half[:, :], -0.5).then_inc(c_ready, 1)
            pool.memset(e_base[:, :], 2.718281828459045).then_inc(c_ready, 1)
            pool.memset(ones_b[:, :], 1.0).then_inc(c_ready, 1)
            pool.wait_ge(ld_c, 16)
            pool.tensor_copy(ident_b[:, :], ident_f).then_inc(c_ready, 1)
            pool.tensor_copy(upper_b[:, :], upper_f).then_inc(c_ready, 1)

            def duplicates(g):
                hold(pool, "pool", a["phi"], 2 * g + 1)
                for tok, src, dst in ((q_tok, Q_HI, Q_HI2), (k_tok, K_HI, K_HI2)):
                    pool.tensor_copy(tok[:, :, dst:dst + D0], tok[:, :, src:src + D0]).then_inc(a["dup"], 1)

            def split_chunk(n):
                slot = stage[:, bass.ds((n % 2) * CH, CH)]
                at = bass.ds(n * CH, CH)
                if isinstance(n, int):
                    pool.wait_ge(ld_ch[n % 2], 16 * (n // 2 + 1))
                else:
                    hold(pool, "pool", ld_ch[0], 16 * ((n + 2) // 2))
                    hold(pool, "pool", ld_ch[1], 16 * ((n + 1) // 2))
                pool.tensor_tensor(w_hi[:, at], slot, one_f[:, 0:1].to_broadcast([P, CH]), ALU.mult).then_inc(pool_seq, 1)
                hold(pool, "pool", pool_seq, n + 1)
                pool.tensor_tensor(w_lo[:, at], slot, w_hi[:, at], ALU.subtract).then_inc(ch_done, 1)

            def l0_group(g):
                if not is_last(g):
                    duplicates(g + 1)
                    for n in (range(TT + 1) if is_first(g) else [g + TT]):
                        split_chunk(n)

            pool.wait_ge(c_ready, C_ALL)
            pool.wait_ge(z_ready, 2)
            duplicates(0)
            loop_groups(pool, l0_group)
            pool.wait_ge(ld_xtok, 16)
            pool.wait_ge(ld_b, 8 * 16)
            for b in range(NB):
                rows = x_tok[:, b * TT * E:(b + 1) * TT * E].rearrange("p (t e) -> p t e", e=E)
                pool.tensor_tensor(rows, rows, bp_bc[:, :].unsqueeze(1).to_broadcast([P, TT, E]), ALU.add
                                   ).then_inc(xb_done, 1)
            chain = Chain(pool, "pool", eb_seq, 0)
            chain(pool.tensor_copy(rw_hi[:, :, :], rw_f[:, :, :]))
            chain(pool.tensor_tensor(rw_lo[:, :, :], rw_f[:, :, :], rw_hi[:, :, :], ALU.subtract))
            chain(pool.tensor_copy(eb_p[:, 0, :], eb_f[:, :]))
            chain(pool.tensor_tensor(eb_r[:, 0, :], eb_f[:, :], eb_p[:, 0, :], ALU.subtract))
            chain(pool.tensor_copy(eb_p[:, 1, :], eb_r[:, 0, :]))
            chain(pool.tensor_tensor(eb_r[:, 1, :], eb_r[:, 0, :], eb_p[:, 1, :], ALU.subtract))
            pool.tensor_copy(eb_p[:, 2, :], eb_r[:, 1, :]).then_inc(eb_ready, 1)

            def inverse_deviation(p, t, ready, seq, value):
                hold(pool, "pool", p[ready], value)
                pool.tensor_scalar(var_e[:, t:t + 1], mv[:, t, 1:2], EPS, 1.0, ALU.add, ALU.mult).then_inc(p[seq], 1)
                hold(pool, "pool", p[seq], value)
                pool.tensor_tensor(rstd[:, t:t + 1], var_e[:, t:t + 1], neg_half[:, 0:1], ALU.pow
                                   ).then_inc(p["rstd"], 1)

            def exponentials(lgd, ex, value, w):
                hold(pool, "pool", lgd, value)
                pool.tensor_tensor(rt[:, 1, 0:w], e_base[:, 0:w], rt[:, 0, 0:w], ALU.pow).then_inc(ex, 1)

            pool.wait_ge(c_ready, C_ALL)
            with pool.Fori(0, NB) as b:
                for t in range(TT):
                    inverse_deviation(m, t, "agg", "pool", 8 * b + t + 1)
                for t in range(TT):
                    hold(pool, "pool", m["x"], 8 * b + t + 1)
                    pool.tensor_tensor(x1b[t], x1[t], outb_bc[:, :], ALU.add).then_inc(m["xb"], 1)
                exponentials(m["lgd"], m["ex"], b + 1, TT * NX)
                for t in range(TT):
                    inverse_deviation(m, t, "agg", "pool", 8 * b + 4 + t + 1)

            def l1_group(g, dense):
                for j in range(4):
                    u = 4 * g + j
                    hold(pool, "pool", c["rr"], u + 1)
                    for qt in range(TT):
                        at = s_sb[j % 2][:, S_OFF[qt]:S_OFF[qt] + (qt + 1) * P]
                        last = pool.tensor_scalar(at, at, rr[:, j % 2, qt:qt + 1], 1.0, ALU.mult, ALU.mult)
                    last.then_inc(c["nrm"], 1)
                if dense:
                    inverse_deviation(c, 0, "mv", "seq", g - TT + 1)

            with pool.Fori(0, TT) as g:
                l1_group(g, False)
            with pool.Fori(TT, NT) as g:
                l1_group(g, True)
            with pool.Fori(NT, NT + TT) as g:
                inverse_deviation(c, 0, "mv", "seq", g - TT + 1)

            exponentials(e["lgd"], e["ex"], 1, NT * NX)
            pool.wait_ge(e["gates"], 1)
            with pool.Fori(0, NB) as b:
                chain = Chain(pool, "pool", e["pool"], (1 + TT) * b)
                hold(pool, "pool", e["yr"], TT * b + 1)
                chain(pool.tensor_copy(g1b[:, :], g1[:, bass.ds(b * TT, TT)]))
                for t in range(TT):
                    chain(pool.tensor_scalar(x3b[t], b2_bc[:, :], g1b[:, t:t + 1], 1.0, ALU.mult, ALU.mult))
                    pool.tensor_tensor(x3b[t], x3b[t], x_tok[:, bass.ds(b * TT * E + t * E, E)], ALU.add
                                       ).then_inc(e["xb"], 1)
                for t in range(TT):
                    inverse_deviation(e, t, "agg", "seq", TT * b + t + 1)


def kernel(**inputs):
    import numpy as np
    import concourse.bacc as bacc
    from concourse.bass_utils import run_bass_kernel_spmd

    v = {n: np.asarray(x) for n, x in inputs.items()}

    def rows(w):
        return w.reshape(-1, P, w.shape[-1]).transpose(1, 0, 2)

    def cols(w):
        return rows(w).reshape(P, -1)

    x = v["L0_attn_x"].reshape(NT, P, E)
    up = np.arange(P)
    constants = np.concatenate([
        np.eye(P), up[:, None] <= up[None, :], np.zeros((P, 512 - P)),
        np.where(up[None, :] > up[:, None], MASKED, 0.0),
        np.broadcast_to(np.tile(NX - np.arange(NX), NT), (P, P))], axis=1).astype(np.float32)
    experts = v["L0_ffn_expert_w"].transpose(1, 0, 2).reshape(E, NX * E)
    arrays = {
        "x_tok": x.transpose(1, 0, 2),
        "x_t": v["L0_attn_x"].reshape(NB, TOK, KE, P).transpose(3, 0, 2, 1).reshape(P, NB, KE * TOK),
        "wqkv": cols(np.concatenate([v["L0_attn_W" + n].T for n in "qkv"], axis=1)),
        "wall": np.concatenate([cols(w) for w in (
            v["L0_attn_Wp"].T, v["L0_ffn_out_w"], experts, v["L1_attn_w_q"], v["L1_attn_w_kv"],
            v["L1_attn_w_dense"], v["L1_ffn_w1"].T, v["L1_ffn_w2"].T)], axis=1),
        "constants": constants,
        "bp": v["L0_attn_bp"], "outb": v["L0_ffn_out_b"], "b2": v["L1_ffn_b2"], "rb": v["L0_ffn_router_b"],
        "eb": v["L0_ffn_expert_b"].reshape(16, P),
        "rw0": cols(v["L0_ffn_router_w"]), "rw1": cols(v["L1_ffn_router_w"].T),
        "b1": v["L1_ffn_b1"].reshape(NF, P).T,
    }
    arrays = {n: np.ascontiguousarray(z) for n, z in arrays.items()}
    nc = bacc.Bacc("TRN2", target_bir_lowering=False, num_devices=1)
    args = [nc.dram_tensor(f"{n}_in", z.shape, mybir.dt.from_np(z.dtype), kind="ExternalInput").ap()
            for n, z in arrays.items()]
    out = nc.dram_tensor("out", (P, NT, E), F32, kind="ExternalOutput").ap()
    build(nc, *args, out)
    r = run_bass_kernel_spmd(nc, [{f"{n}_in": z for n, z in arrays.items()}], core_ids=[0])
    return np.asarray(r.results[0]["out"]).transpose(1, 0, 2).reshape(NB, TOK, E)
```

```python
from contextlib import ExitStack

import concourse.bass as bass
from concourse import mybir

F32 = mybir.dt.float32
BF16 = mybir.dt.bfloat16
ALU = mybir.AluOpType
ACT = mybir.ActivationFunctionType
AX = mybir.AxisListType

P = 128
E = 256
KE = E // P
NB = 4
TOK = 512
TT = TOK // P
NT = NB * TT
HEADS = 16
D0 = E // HEADS
D1 = 128
NH = NB * HEADS
VC = D0 + 1
NX = 8
FF = 1024
NF = FF // P
CAP = 64
EPS = 1e-5
CH = 1024
NCH = 19
CONSTS = 3 * P + 512
MASKED = -1e30
HUGE = 3e38

S_CHUNKS = (((3, 0),), ((2, 0), (0, 384)), ((1, 0),))
S_OFF = {3: 0, 2: 512, 0: 896, 1: 1024}
S_COLS = 1280
T_CHUNKS = (
    tuple((0, qt, qt * P) for qt in range(4)),
    tuple((1, qt, (qt - 1) * P) for qt in range(1, 4)) + ((3, 3, 384),),
    tuple((2, qt, (qt - 2) * P) for qt in range(2, 4)),
)
T_OFF = (0, 512, 1024)
T_LEN = (512, 512, 256)
PT_COL = {(kt, qt): T_OFF[c] + col for c, chunk in enumerate(T_CHUNKS) for kt, qt, col in chunk}

Q_HI, Q_HI2, Q_LO, Q_ROWS = 0, 16, 32, 48
K_HI, K_LO, K_HI2, V_HI, V_LO, K_ROWS = 0, 16, 32, 48, 64, 80

LATE = [("cm", 0), ("cm", 1), ("x2", 0), ("cm", 2), ("x2", 1), ("cm", 3), ("x2", 2), ("x2", 3)]
USES = 8 + len(LATE)
E_CHAIN = 22
C_ALL = 8


WP, OUTW, EXPW, WQ, WKV, WD, W1, W2 = 0, 512, CH, 5 * CH, 9 * CH, 11 * CH, 15 * CH, 17 * CH


def build(nc, x_tok_d, x_t_d, wqkv_d, wall_d, const_d, bp_d, outb_d, b2_d, rb_d, eb_d, rw0_d, rw1_d, b1_d, out_d):
    ctx = ExitStack()
    with ctx:
        def sb(name, shape, dt=F32):
            return ctx.enter_context(nc.sbuf_tensor(name, shape, dt))

        def sem(name):
            return ctx.enter_context(nc.semaphore(name))

        def ds(start, size):
            return slice(start, start + size)

        x_tok = sb("x_tok", [P, NT * E])
        xt_hi = sb("xt_hi", [P, KE, NB * TOK], BF16)
        xt_lo = sb("xt_lo", [P, KE, NB * TOK], BF16)
        w_hi = sb("w_hi", [P, NCH * CH], BF16)
        w_lo = sb("w_lo", [P, NCH * CH], BF16)
        wqkv_hi = sb("wqkv_hi", [P, KE, 3 * E], BF16)
        wqkv_lo = sb("wqkv_lo", [P, KE, 3 * E], BF16)
        scr = sb("scr", [P, 16384])
        s_sb = [sb(f"s_sb{i}", [P, S_COLS]) for i in range(2)]
        pt_hi = [sb(f"pt_hi{i}", [P, S_COLS], BF16) for i in range(2)]
        pt_lo = [sb(f"pt_lo{i}", [P, S_COLS], BF16) for i in range(2)]
        consts = sb("consts", [P, CONSTS])
        ident_b = sb("ident_b", [P, P], BF16)
        ones_b = sb("ones_b", [P, P], BF16)
        upper_b = sb("upper_b", [P, P], BF16)
        bp_bc = sb("bp_bc", [P, E])
        outb_bc = sb("outb_bc", [P, E])
        b2_bc = sb("b2_bc", [P, E])
        rb_bc = sb("rb_bc", [P, NX])
        b1_col = sb("b1_col", [P, NF])
        rw_f = sb("rw_f", [P, 2, KE * NX])
        rw_hi = sb("rw_hi", [P, 2, KE * NX], BF16)
        rw_lo = sb("rw_lo", [P, 2, KE * NX], BF16)
        nm = sb("nm", [P, 2, 4])
        rs = sb("rs", [P, 2, 4])
        rr = sb("rr", [P, 2, 4])
        v0 = [sb(f"v0_{i}", [P, 4, 2, VC], BF16) for i in range(2)]
        stats = sb("stats", [P, 4, 6])
        mv = sb("mv", [P, 4, 2])
        var_e = sb("var_e", [P, 4])
        rstd = sb("rstd", [P, 4])
        one_f = sb("one_f", [P, 1])
        neg_half = sb("neg_half", [P, 4])
        e_base = sb("e_base", [P, NT * NX])
        r1c = sb("r1c", [P, 4, NT])
        g1 = sb("g1", [P, NT])
        g1b = sb("g1b", [P, TT])

        ident_f = consts[:, 0:P]
        upper_f = consts[:, P:2 * P]
        mask = consts[:, 2 * P:2 * P + 512]
        iota8 = consts[:, 768:768 + P]

        qt_hi = [w_hi[:, TOK * i:TOK * (i + 1)] for i in range(2)]
        qt_lo = [w_lo[:, TOK * i:TOK * (i + 1)] for i in range(2)]
        k1_hi, k1_lo = w_hi[:, 1024:2048], w_lo[:, 1024:2048]
        v1_hi, v1_lo = w_hi[:, 2048:3072], w_lo[:, 2048:3072]
        rcc = s_sb[1][:, 384:448]
        rt = s_sb[0][:, 0:8 * NT * NX].rearrange("p (i c) -> p i c", i=8)
        lg = s_sb[0][:, 1024:1152].rearrange("p (t x) -> p t x", x=NX)
        gates = s_sb[0][:, 1152:1280].rearrange("p (t x) -> p t x", x=NX)
        cnt = s_sb[1][:, 0:2 * NT * NX]
        picks = s_sb[1][:, 256:384].bitcast(BF16).rearrange("p (t x) -> p t x", x=NX)

        xt_f = scr[:, 0:2048].rearrange("p (s c) -> p s c", s=2)
        ctx0 = scr[:, 2048:2048 + NH * TT * VC].rearrange("p (u q d) -> p u q d", q=TT, d=VC)
        q_st = [scr[:, 8192 + 1024 * i:9216 + 1024 * i].bitcast(BF16) for i in range(2)]
        k_st = [scr[:, 10240 + 1024 * i:11264 + 1024 * i].bitcast(BF16) for i in range(2)]
        q_tok = scr[:, 12288:13312].bitcast(BF16).rearrange("p (c s) -> p c s", s=P)
        k_tok = scr[:, 13312:14336].bitcast(BF16).rearrange("p (c s) -> p c s", s=P)
        wqkv_f = scr[:, 14336:14336 + KE * 3 * E]
        stage = scr[:, 14336:16384]
        eb_f = scr[0:16, 6400:6528]
        eb_p = scr[0:16, 6528:6720].bitcast(BF16).rearrange("p (i d) -> p i d", i=3)
        eb_r = scr[0:16, 6720:6976].rearrange("p (i d) -> p i d", i=2)
        eb3 = scr[0:3, 15360:16384].bitcast(BF16)
        def tiles(base, n, width, dt=F32):
            return [scr[:, base + width * i:base + width * (i + 1)].bitcast(dt) if dt != F32
                    else scr[:, base + width * i:base + width * (i + 1)] for i in range(n)]

        ta_hi, ta_lo = tiles(0, 4, P, BF16), tiles(512, 4, P, BF16)
        tb_hi, tb_lo = tiles(1024, 4, P, BF16), tiles(1536, 4, P, BF16)
        cc = tiles(8192, 4, E)
        x1 = tiles(9216, 4, E)
        x1b = tiles(10240, 4, E)
        comb = tiles(11264, 4, E)
        x2 = tiles(12288, 4, E)
        ge = tiles(13312, 4, 512)
        ct_hi = scr[:, 0:8192].bitcast(BF16)
        ct_lo = scr[:, 8192:16384].bitcast(BF16)
        x3 = tiles(0, 4, E)
        hf = tiles(1024, 2, 512)
        h_hi, h_lo = tiles(2048, 2, 256, BF16), tiles(2560, 2, 256, BF16)
        x3b = tiles(3072, 4, E)
        y4 = tiles(4096, 4, E)

        bank = [ctx.enter_context(nc.psum_tensor(f"bank{i}", [P, 512], F32)) for i in range(8)]

        ld_w = sem("ld_w")
        ld_x = [sem(f"ld_x{i}") for i in range(2)]
        ld_xtok = sem("ld_xtok")
        ld_c = sem("ld_c")
        ld_b = sem("ld_b")
        ld_ch = [sem(f"ld_ch{i}") for i in range(2)]
        ch_done = sem("ch_done")
        eb_ready = sem("eb_ready")
        eb_moved = sem("eb_moved")
        c_ready = sem("c_ready")
        z_ready = sem("z_ready")
        w_hi_d = sem("w_hi_d")
        w_lo_d = sem("w_lo_d")
        x_hi_d = sem("x_hi_d")
        x_lo_d = sem("x_lo_d")
        pool_seq = sem("pool_seq")
        eb_seq = sem("eb_seq")
        xb_done = sem("xb_done")
        out_done = sem("out_done")

        names = ("pe", "act", "dve", "pool")
        stepped = {n: sem(f"stepped_{n}") for n in names}

        def hold(eng, who, semaphore, value):
            if isinstance(value, int):
                if value > 0:
                    eng.wait_ge(semaphore, value)
            else:
                eng.wait_ge(semaphore, value).then_inc(stepped[who], 1)

        def group_sems(p):
            return {n: sem(f"{p}_{n}") for n in (
                "proj", "stk", "s", "w", "t", "pv", "phi", "plo", "dup", "kv", "kvh", "kvl", "stka", "stkd", "max", "exp",
                "thi", "tlo", "vc", "rr", "nrm", "chi", "clo", "o", "od", "st", "mv", "seq", "rstd", "x")}

        a = group_sems("l0")
        c = group_sems("l1")
        m = {n: sem(f"mix_{n}") for n in (
            "cc", "tp", "thi", "tlo", "o", "r", "agg", "rstd", "x", "xb", "lg", "lgc", "lgd", "ex", "gates",
            "f", "ge", "mul", "out", "dve", "pool")}
        e = {n: sem(f"ffn_{n}") for n in (
            "cc", "tp", "thi", "tlo", "lg", "lgc", "lgd", "ex", "picks", "rank", "gates", "h", "ge", "hhi", "hlo",
            "y", "yr", "xb", "seq",  "agg", "rstd", "x", "dve", "pool")}

        block = ctx.enter_context(nc.Block())

        def loop_groups(eng, body):
            for g in range(NT):
                body(g)

        def is_first(g):
            return isinstance(g, int) and g == 0

        def is_last(g):
            return isinstance(g, int) and g == NT - 1

        def par(g):
            return g % 2

        @block.sync
        def _(sp):
            sp.dma_start(wqkv_f, wqkv_d).then_inc(ld_w, 16)
            for b in range(2):
                sp.dma_start(xt_f[:, b, :], x_t_d[:, b, :]).then_inc(ld_x[b], 16)
            sp.dma_start(consts[:, :], const_d).then_inc(ld_c, 16)
            sp.wait_ge(w_lo_d, 1)
            for cc in range(2):
                sp.dma_start(stage[:, cc * CH:cc * CH + CH], wall_d[:, cc * CH:cc * CH + CH]).then_inc(ld_ch[cc], 16)
            sp.dma_start(x_tok[:, :].rearrange("p (t e) -> p t e", e=E), x_tok_d).then_inc(ld_xtok, 16)
            sp.dma_start(bp_bc[:, :], bp_d.partition_broadcast(P)).then_inc(ld_b, 16)
            sp.dma_start(outb_bc[:, :], outb_d.partition_broadcast(P)).then_inc(ld_b, 16)
            sp.dma_start(b2_bc[:, :], b2_d.partition_broadcast(P)).then_inc(ld_b, 16)
            sp.dma_start(rb_bc[:, :], rb_d.partition_broadcast(P)).then_inc(ld_b, 16)
            sp.dma_start(rw_f[:, 0, :], rw0_d).then_inc(ld_b, 16)
            sp.dma_start(rw_f[:, 1, :], rw1_d).then_inc(ld_b, 16)
            sp.dma_start(b1_col[:, :], b1_d).then_inc(ld_b, 16)
            for b in range(2, NB):
                sp.wait_ge(x_lo_d, b - 1)
                sp.dma_start(xt_f[:, b % 2, :], x_t_d[:, b, :]).then_inc(ld_x[b % 2], 16)
            for cc in range(2, NCH):
                sp.wait_ge(ch_done, cc - 1)
                sp.dma_start(stage[:, (cc % 2) * CH:(cc % 2) * CH + CH],
                             wall_d[:, cc * CH:cc * CH + CH]).then_inc(ld_ch[cc % 2], 16)
            sp.wait_ge(ch_done, NCH)
            sp.dma_start(eb_f, eb_d).then_inc(ld_b, 16)
            sp.wait_ge(eb_ready, 1)
            for i in range(3):
                sp.dma_start(eb3[i:i + 1, :], eb_p[:, i, :]).then_inc(eb_moved, 16)
            for b in range(NB):
                sp.wait_ge(e["x"], TT * (b + 1))
                sp.dma_start(out_d[:, b * TT:(b + 1) * TT, :],
                             x_tok[:, b * TT * E:(b + 1) * TT * E].rearrange("p (t e) -> p t e", e=E)
                             ).then_inc(out_done, 16)
            sp.wait_ge(out_done, 16 * NB)

        @block.tensor
        def _(pe):
            def mm3(out, l_hi, l_lo, r_hi, r_lo, start, stop, check=False):
                pe.matmul(out, l_hi, r_hi, start=start, stop=False, skip_group_check=check)
                pe.matmul(out, l_hi, r_lo, start=False, stop=False, skip_group_check=check)
                return pe.matmul(out, l_lo, r_hi, start=False, stop=stop, skip_group_check=check)

            def l0_project(g):
                t0 = g * P
                b = g // TT
                hold(pe, "pe", x_lo_d, b + 1)
                if is_first(g):
                    pe.wait_ge(w_lo_d, 1)
                hold(pe, "pe", a["stka"], 2 * g)
                hold(pe, "pe", a["stkd"], 2 * g)
                for k in range(KE):
                    last = mm3(bank[4][:, 0:512], xt_hi[:, k, ds(t0, P)], xt_lo[:, k, ds(t0, P)],
                               wqkv_hi[:, k, 0:512], wqkv_lo[:, k, 0:512], k == 0, k == KE - 1)
                last.then_inc(a["proj"], 1)
                for k in range(KE):
                    last = mm3(bank[5][:, 0:E], xt_hi[:, k, ds(t0, P)], xt_lo[:, k, ds(t0, P)],
                               wqkv_hi[:, k, 512:768], wqkv_lo[:, k, 512:768], k == 0, k == KE - 1)
                last.then_inc(a["proj"], 1)

            def l0_stack(g, which):
                tok = (q_tok, k_tok)[which]
                if which == 0:
                    hold(pe, "pe", a["plo"], 2 * g + 2)
                    hold(pe, "pe", a["dup"], 2 * g + 2)
                    if is_first(g):
                        pe.wait_ge(z_ready, 2)
                        pe.wait_ge(c_ready, C_ALL)
                for half in range(2):
                    if which == 1:
                        hold(pe, "pe", a[("stka", "stkd")[half]], 2 * g + 1)
                    out = bank[4 + half][:, :].bitcast(BF16)
                    for i in range(8):
                        last = pe.transpose(out[:, i * P:(i + 1) * P], tok[:, 8 * half + i, :], ident_b[:, :])
                    last.then_inc(a["stk"], 1)

            def l0_scores(g, j, chunk):
                u = g * 4 + j
                if j == 0 and chunk == 0:
                    hold(pe, "pe", a["stka"], 2 * g + 2)
                    hold(pe, "pe", a["stkd"], 2 * g + 2)
                n = 3 * u + chunk
                hold(pe, "pe", a["max"], n - 1)
                for qt, col in S_CHUNKS[chunk]:
                    w = (qt + 1) * P
                    last = pe.matmul(bank[(3 * j + chunk) % 2][:, col:col + w],
                                     q_stv(g)[:, ds(q_off(g) + j * TOK + qt * P, P)],
                                     k_stv(g)[:, ds(q_off(g) + j * TOK, w)], start=True, stop=True)
                last.then_inc(a["s"], 1)

            def q_stv(g):
                return scr[:, 8192:10240].bitcast(BF16)

            def k_stv(g):
                return scr[:, 10240:12288].bitcast(BF16)

            def q_off(g):
                return par(g) * 2048

            def l0_step(n):
                hold(pe, "pe", a["vc"], n)
                if n < NH:
                    for kt in range(TT):
                        last = pe.matmul(bank[6][:, kt * 32:kt * 32 + 32],
                                         k_stv(n // 4)[:, ds(q_off(n // 4) + (n % 4) * TOK + kt * P, P)],
                                         ident_b[:, V_HI:V_HI + 2 * D0], start=True, stop=True)
                if n >= 2:
                    u, jp = n - 2, n % 2
                    hold(pe, "pe", a["tlo"], 3 * u + 3)
                    for qt in range(TT):
                        sums = bank[6][:, P + qt * VC:P + (qt + 1) * VC]
                        out = bank[6][:, P + qt * VC:P + qt * VC + D0]
                        for kt in range(qt + 1):
                            col = PT_COL[kt, qt]
                            hi, lo = pt_hi[jp][:, col:col + P], pt_lo[jp][:, col:col + P]
                            pe.matmul(sums, hi, v0[jp][:, kt, 0, :], start=(kt == 0), stop=False,
                                      skip_group_check=True)
                            pe.matmul(out, hi, v0[jp][:, kt, 1, 0:D0], start=False, stop=False,
                                      skip_group_check=True)
                            last = pe.matmul(sums, lo, v0[jp][:, kt, 0, :], start=False, stop=(kt == qt),
                                             skip_group_check=True)
                last.then_inc(a["w"], 1)

            def transposes(s, u, jp, chunk):
                if s is a:
                    if chunk == 0:
                        hold(pe, "pe", s["exp"], 3 * u + 3)
                    hold(pe, "pe", s["tlo"], 3 * u + chunk - 2)
                    tb = bank[(2, 3, 7)[chunk]]
                else:
                    if chunk == 0:
                        hold(pe, "pe", s["nrm"], u + 1)
                    hold(pe, "pe", s["tlo"], 3 * u + chunk - 1)
                    tb = bank[2 + (jp * 3 + chunk) % 2]
                for kt, qt, col in T_CHUNKS[chunk]:
                    last = pe.transpose(tb[:, col:col + P], s_sb[jp][:, S_OFF[qt] + kt * P:S_OFF[qt] + kt * P + P],
                                        ident_f)
                last.then_inc(s["t"], 1)

            def l0_group(g):
                for j in range(4):
                    u = g * 4 + j
                    behind = 4 * g + j if is_first(g) else 2
                    l0_scores(g, j, 2)
                    if behind >= 1:
                        for chunk in range(3):
                            transposes(a, u - 1, (j + 1) % 2, chunk)
                    if not (is_last(g) and j == 3):
                        gn, jn = (g, j + 1) if j < 3 else (g + 1, 0)
                        l0_scores(gn, jn, 0)
                        l0_scores(gn, jn, 1)
                    if j in (1, 2) and g + 1 < NT:
                        l0_stack(g + 1, j - 1)
                    if j == 3 and g + 2 < NT:
                        l0_project(g + 2)
                    l0_step(u)

            pe.wait_ge(ld_c, 16)
            l0_project(0)
            l0_stack(0, 0)
            l0_stack(0, 1)
            l0_project(1)
            l0_scores(0, 0, 0)
            l0_scores(0, 0, 1)
            loop_groups(pe, l0_group)
            for chunk in range(3):
                transposes(a, NH - 1, 1, chunk)
            l0_step(NH)
            l0_step(NH + 1)

            def turn(p, use, src):
                hold(pe, "pe", p["tlo"], use[0] + 1)
                for k in range(KE):
                    last = pe.transpose(bank[use[1] % 2][:, k * P:(k + 1) * P], src[:, k * P:(k + 1) * P], ident_f)
                last.then_inc(p["tp"], 1)

            def project(out, t_hi, t_lo, base, n=E):
                for k in range(KE):
                    last = mm3(out, t_hi[:, k * P:(k + 1) * P], t_lo[:, k * P:(k + 1) * P],
                               w_hi[:, base + k * n:base + (k + 1) * n], w_lo[:, base + k * n:base + (k + 1) * n],
                               k == 0, k == KE - 1)
                return last

            pe.wait_ge(ch_done, NCH)
            pe.wait_ge(eb_moved, 48)
            pe.wait_ge(c_ready, C_ALL)
            pe.wait_ge(a["vc"], NH + 2)
            for b in range(0, NB):
                def use(i):
                    return (USES * b + i, i)

                for t in range(TT):
                    hold(pe, "pe", m["cc"], TT * b + t + 1)
                    turn(m, use(t), cc[t])
                for t in range(TT):
                    hold(pe, "pe", m["tlo"], USES * b + t + 1 + 2)
                    hold(pe, "pe", m["r"], 8 * b + t + 1)
                    project(bank[2 + t % 2][:, 0:E], ta_hi[t], ta_lo[t], WP).then_inc(m["o"], 1)
                for t in range(TT):
                    hold(pe, "pe", m["x"], 8 * b + t + 1)
                    turn(m, use(4 + t), x1[t])
                hold(pe, "pe", m["tlo"], USES * b + 8 + 2)
                hold(pe, "pe", m["ge"], 16 * b + 4)
                for t in range(TT):
                    for k in range(KE):
                        ks = slice(k * NX, (k + 1) * NX)
                        last = mm3(bank[4][:, t * NX:(t + 1) * NX], tb_hi[t][:, k * P:(k + 1) * P],
                                   tb_lo[t][:, k * P:(k + 1) * P], rw_hi[:, 0, ks], rw_lo[:, 0, ks],
                                   k == 0, k == KE - 1)
                last.then_inc(m["lg"], 1)
                hold(pe, "pe", m["lgc"], b + 1)

                def experts(t):
                    for p in range(4):
                        hold(pe, "pe", m["ge"], 16 * b + 4 * t + p + 1)
                        out = bank[4 + p][:, :]
                        pe.matmul(out, ones_b[0:3, :], eb3[:, p * 512:(p + 1) * 512], start=True, stop=False)
                        for k in range(KE):
                            cs = slice(EXPW + k * NX * E + p * 512, EXPW + k * NX * E + (p + 1) * 512)
                            last = mm3(out, tb_hi[t][:, k * P:(k + 1) * P], tb_lo[t][:, k * P:(k + 1) * P],
                                       w_hi[:, cs], w_lo[:, cs], False, k == KE - 1)
                        last.then_inc(m["f"], 1)

                def mixed(t):
                    hold(pe, "pe", m["mul"], 32 * b + 8 * t + 8 + 8)
                    turn(m, use(LATE.index(("cm", t)) + 8), comb[t])

                def out_project(t):
                    hold(pe, "pe", m["tlo"], USES * b + LATE.index(("cm", t)) + 8 + 1 + 2)
                    hold(pe, "pe", m["r"], 8 * b + 4 + t + 1)
                    project(bank[2 + t % 2][:, 0:E], ta_hi[t], ta_lo[t], OUTW).then_inc(m["o"], 1)

                def normed(t):
                    hold(pe, "pe", m["x"], 8 * b + 4 + t + 1)
                    turn(m, use(LATE.index(("x2", t)) + 8), x2[t])

                for t in range(TT):
                    experts(t)
                    if t >= 1:
                        mixed(t - 1)
                    if t >= 2:
                        normed(t - 2)
                    if t >= 1:
                        out_project(t - 1)
                mixed(TT - 1)
                normed(TT - 2)
                out_project(TT - 1)
                normed(TT - 1)

            def l1_project(which, g, j=0):
                tok = (g // 4) * TOK
                if which == "q":
                    hold(pe, "pe", c["plo"], 4 * g + j)
                    out = bank[4]
                else:
                    hold(pe, "pe", c["kvl"], 2 * g + (which == "v"))
                    out = bank[5]
                if which == "v":
                    for tt in range(TT):
                        for k in range(KE):
                            base = WKV + k * 1024 + 512
                            last = mm3(out[:, tt * P:(tt + 1) * P],
                                       xt_hi[:, k, ds(tok + tt * P, P)], xt_lo[:, k, ds(tok + tt * P, P)],
                                       w_hi[:, ds(base + (g % 4) * P, P)],
                                       w_lo[:, ds(base + (g % 4) * P, P)], k == 0, k == KE - 1)
                else:
                    for k in range(KE):
                        base = WKV + k * 1024 + (g % 4) * P if which == "k" else WQ + k * 2048 + (g % 4) * TOK + j * P
                        last = mm3(out[:, :], w_hi[:, ds(base, P)], w_lo[:, ds(base, P)],
                                   xt_hi[:, k, ds(tok, TOK)], xt_lo[:, k, ds(tok, TOK)],
                                   k == 0, k == KE - 1)
                last.then_inc(c["proj" if which == "q" else "kv"], 1)

            def l1_scores(g, j, chunk):
                u = 4 * g + j
                if chunk == 0:
                    hold(pe, "pe", c["plo"], u + 1)
                    if j == 0:
                        hold(pe, "pe", c["kvl"], 2 * g + 1)
                n = 3 * u + chunk
                hold(pe, "pe", c["max"], n - 1)
                kb = (g % 2) * TOK
                for qt, col in S_CHUNKS[chunk]:
                    w = (qt + 1) * P
                    qs = slice(qt * P, (qt + 1) * P)
                    last = mm3(bank[(3 * j + chunk) % 2][:, col:col + w], qt_hi[j % 2][:, qs], qt_lo[j % 2][:, qs],
                               k1_hi[:, ds(kb, w)], k1_lo[:, ds(kb, w)], True, True)
                last.then_inc(c["s"], 1)

            def l1_pv(g, j):
                u = 4 * g + j
                hold(pe, "pe", c["tlo"], 3 * u + 3)
                hold(pe, "pe", c["clo"], u)
                if j == 0:
                    hold(pe, "pe", c["kvl"], 2 * g + 2)
                vb = (g % 2) * TOK
                for kt in range(TT):
                    col = PT_COL[kt, kt]
                    w = TOK - kt * P
                    ps = slice(col, col + w)
                    vs = ds(vb + kt * P, P)
                    out = bank[6][:, kt * P:TOK]
                    pe.matmul(out, v1_hi[:, vs], pt_hi[j % 2][:, ps], start=(kt == 0), stop=False)
                    pe.matmul(out, v1_hi[:, vs], pt_lo[j % 2][:, ps], start=False, stop=False)
                    last = pe.matmul(out, v1_lo[:, vs], pt_hi[j % 2][:, ps], start=False, stop=(kt == TT - 1))
                last.then_inc(c["pv"], 1)

            def l1_dense(g, part, parts, ready):
                hold(pe, "pe", c["clo"], ready)
                if part == 0:
                    hold(pe, "pe", c["od"], g - TT + 1)
                cb = ((g // 4 + 1) % 2) * HEADS * TOK + (g % 4) * P
                edges = [HEADS * i // parts for i in range(parts + 1)]
                for hd in range(edges[part], edges[part + 1]):
                    cs = ds(cb + hd * TOK, P)
                    ws = slice(WD + hd * E, WD + (hd + 1) * E)
                    last = mm3(bank[7][:, 0:E], ct_hi[:, cs], ct_lo[:, cs], w_hi[:, ws], w_lo[:, ws],
                               hd == 0, hd == HEADS - 1)
                if part == parts - 1:
                    last.then_inc(c["o"], 1)

            def l1_group(g, dense):
                for j in range(4):
                    u = 4 * g + j
                    behind = 4 * g + j if is_first(g) else 2
                    ahead = 3 - j if is_last(g) else 4
                    l1_scores(g, j, 2)
                    if behind >= 1:
                        transposes(c, u - 1, (j + 1) % 2, 0)
                        transposes(c, u - 1, (j + 1) % 2, 1)
                    if behind >= 2:
                        l1_pv(*((g, j - 2) if j >= 2 else (g - 1, j + 2)))
                    if ahead >= 2:
                        l1_project("q", *((g, j + 2) if j < 2 else (g + 1, j - 2)))
                    if behind >= 1:
                        transposes(c, u - 1, (j + 1) % 2, 2)
                    if ahead >= 1:
                        l1_scores(*((g, j + 1) if j < 3 else (g + 1, 0)), 0)
                    if not is_last(g) and j < 2:
                        l1_project("kv"[j], g + 1)
                    if dense and j >= 2:
                        l1_dense(g, j - 2, 2, u - 2)
                    if ahead >= 1:
                        l1_scores(*((g, j + 1) if j < 3 else (g + 1, 0)), 1)

            pe.wait_ge(m["tlo"], USES * NB + 2)
            l1_project("k", 0)
            l1_project("q", 0, 0)
            l1_project("v", 0)
            l1_project("q", 0, 1)
            l1_scores(0, 0, 0)
            l1_scores(0, 0, 1)
            l1_group(0, False)
            for g in range(1, TT):
                l1_group(g, False)
            for g in range(TT, NT - 1):
                l1_group(g, True)
            l1_group(NT - 1, True)
            l1_pv(NT - 1, 2)
            for chunk in range(3):
                transposes(c, NH - 1, 1, chunk)
            l1_pv(NT - 1, 3)
            for g in range(NT, NT + TT):
                l1_dense(g, 0, 1, NH)

            pe.wait_ge(c["x"], NT)
            for b in range(0, NB):
                for t in range(TT):
                    hold(pe, "pe", e["cc"], TT * b + t + 1)
                    turn(e, (TT * b + t, t), x3[t])
                hold(pe, "pe", e["tlo"], TT * b + TT + 2)
                hold(pe, "pe", e["lgc"], b + 1)
                for t in range(TT):
                    tok = b * TOK + t * P
                    for k in range(KE):
                        ks = slice(k * NX, (k + 1) * NX)
                        last = mm3(bank[2][:, t * NX:(t + 1) * NX], xt_hi[:, k, ds(tok, P)],
                                   xt_lo[:, k, ds(tok, P)], rw_hi[:, 1, ks], rw_lo[:, 1, ks],
                                   k == 0, k == KE - 1)
                last.then_inc(e["lg"], 1)
            pe.wait_ge(e["picks"], 2)
            pe.matmul(bank[3][:, 0:2 * NT * NX], upper_b[:, :], picks[:, :, :], start=True, stop=False)
            for n in range(2 * NT - 1):
                after = 2 * NT - 1 - n
                last = pe.matmul(bank[3][:, (n + 1) * NX:2 * NT * NX], ones_b[:, :],
                                 picks[:, n:n + 1, :].to_broadcast([P, after, NX]),
                                 start=False, stop=(after == 1))
            last.then_inc(e["rank"], 1)
            pe.sem_inc(e["y"], 2)
            for b in range(0, NB):
                def outputs(i):
                    hold(pe, "pe", e["hlo"], NF * b + i + 1)
                    if i == 0:
                        hold(pe, "pe", e["yr"], TT * b + 1)
                    for t in range(TT):
                        ts = slice(t * P, (t + 1) * P)
                        ws = slice(W2 + i * E, W2 + (i + 1) * E)
                        last = mm3(bank[6 + t // 2][:, (t % 2) * E:(t % 2 + 1) * E], h_hi[i % 2][:, ts],
                                   h_lo[i % 2][:, ts], w_hi[:, ws], w_lo[:, ws],
                                   i == 0 and t % 2 == 0, i == NF - 1 and t % 2 == 1, True)
                    last.then_inc(e["y"], 1)

                for i in range(NF):
                    hold(pe, "pe", e["ge"], NF * b + i + 1)
                    for k in range(KE):
                        ws = slice(W1 + k * FF + i * P, W1 + k * FF + (i + 1) * P)
                        last = mm3(bank[4 + i % 2][:, :], w_hi[:, ws], w_lo[:, ws],
                                   xt_hi[:, k, ds(b * TOK, TOK)], xt_lo[:, k, ds(b * TOK, TOK)],
                                   k == 0, k == KE - 1)
                    last.then_inc(e["h"], 1)
                    if i >= 1:
                        outputs(i - 1)
                outputs(NF - 1)

        @block.scalar
        def _(act):
            def copy(out, in_):
                return act.activation(out, in_, ACT.Copy)

            act.wait_ge(ld_w, 16)
            copy(wqkv_hi[:, :, :].rearrange("p k n -> p (k n)"), wqkv_f).then_inc(w_hi_d, 1)

            def x_high(b):
                act.wait_ge(ld_x[b % 2], 16 * (b // 2 + 1))
                copy(xt_hi[:, :, b * TOK:(b + 1) * TOK], xt_f[:, b % 2, :].rearrange("p (k t) -> p k t", k=KE)
                     ).then_inc(x_hi_d, 1)

            def l0_parts_high(g):
                hold(act, "act", a["stk"], 4 * g)
                hold(act, "act", a["proj"], 2 * g + 1)
                copy(q_tok[:, :, Q_HI:Q_HI + D0], bank[4][:, 0:E].rearrange("p (c d) -> p c d", d=D0))
                copy(k_tok[:, :, K_HI:K_HI + D0], bank[4][:, E:2 * E].rearrange("p (c d) -> p c d", d=D0)
                     ).then_inc(a["phi"], 1)
                hold(act, "act", a["proj"], 2 * g + 2)
                copy(k_tok[:, :, V_HI:V_HI + D0], bank[5][:, 0:E].rearrange("p (c d) -> p c d", d=D0)
                     ).then_inc(a["phi"], 1)

            def l0_rows_even(g, which):
                hold(act, "act", a["stk"], 4 * g + 2 * which + 1)
                rows = (Q_ROWS, K_ROWS)[which]
                base = (8192, 10240)[which]
                dst = scr[:, base:base + 2048].bitcast(BF16)
                copy(dst[0:rows, ds((g % 2) * 2048, 2048)].rearrange("p (t c) -> p t c", c=16)[:, :, 0:8],
                     bank[4][:, :].bitcast(BF16).rearrange("p (c t) -> p t c", t=P)[0:rows]
                     ).then_inc(a["stka"], 1)

            def exponentials(s, g, j, chunk):
                u = 4 * g + j
                hold(act, "act", s["max"], 3 * u + chunk + 1)
                if chunk == 0 and s is c:
                    hold(act, "act", s["rr"], u - 1)
                for qt, _ in S_CHUNKS[chunk]:
                    at = s_sb[j % 2][:, S_OFF[qt]:S_OFF[qt] + (qt + 1) * P]
                    if s is a:
                        last = act.activation(at, at, ACT.Exp, bias=nm[:, j % 2, qt:qt + 1], scale=-1.0)
                    else:
                        last = act.activation(at, at, ACT.Exp, bias=nm[:, j % 2, qt:qt + 1], scale=-1.0,
                                              accum_out=rs[:, j % 2, qt:qt + 1])
                last.then_inc(s["exp"], 1)

            def probs_high(s, u, jp, chunk):
                hold(act, "act", s["t"], 3 * u + chunk + 1)
                w = T_LEN[chunk]
                tb = bank[(2, 3, 7)[chunk] if s is a else 2 + (3 * jp + chunk) % 2]
                copy(pt_hi[jp][:, T_OFF[chunk]:T_OFF[chunk] + w], tb[:, 0:w]).then_inc(s["thi"], 1)

            def l0_step(n):
                hold(act, "act", a["w"], n + 1)
                if n < NH:
                    last = copy(v0[n % 2][:, :, :, 0:D0], bank[6][:, 0:P].rearrange("p (k i d) -> p k i d", i=2, d=D0))
                if n >= 2:
                    last = copy(ctx0[:, n - 2, :, :].rearrange("p q d -> p (q d)"), bank[6][:, P:P + TT * VC])
                last.then_inc(a["vc"], 1)

            def l0_group(g):
                for j in range(4):
                    u = 4 * g + j
                    first = is_first(g) and j == 0
                    exponentials(a, g, j, 0)
                    if not first:
                        l0_step(u - 1)
                        probs_high(a, u - 1, (j + 1) % 2, 0)
                    exponentials(a, g, j, 1)
                    if not first:
                        probs_high(a, u - 1, (j + 1) % 2, 1)
                    exponentials(a, g, j, 2)
                    if not first:
                        probs_high(a, u - 1, (j + 1) % 2, 2)
                    if not is_last(g):
                        if j == 0:
                            l0_parts_high(g + 1)
                        if j in (1, 2):
                            l0_rows_even(g + 1, j - 1)

            x_high(0)
            act.wait_ge(c_ready, C_ALL)
            l0_parts_high(0)
            x_high(1)
            act.wait_ge(z_ready, 2)
            l0_rows_even(0, 0)
            l0_rows_even(0, 1)
            x_high(2)
            x_high(3)
            loop_groups(act, l0_group)
            l0_step(NH - 1)
            for chunk in range(3):
                probs_high(a, NH - 1, 1, chunk)
            l0_step(NH)
            l0_step(NH + 1)

            def turned_high(p, dst, use):
                hold(act, "act", p["tp"], use[0] + 1)
                copy(dst, bank[use[1] % 2][:, 0:E].rearrange("p (k t) -> p k t", k=KE)).then_inc(p["thi"], 1)

            def kt(ap):
                return ap.rearrange("p (k t) -> p k t", k=KE)

            act.wait_ge(a["vc"], NH + 2)
            act.sem_inc(m["ge"], 4)
            for b in range(0, NB):
                def use(i):
                    return (USES * b + i, i)

                for t in range(TT):
                    turned_high(m, kt(ta_hi[t]), use(t))
                for t in range(TT):
                    turned_high(m, kt(tb_hi[t]), use(4 + t))

                def gelus(t):
                    for p in range(4):
                        hold(act, "act", m["f"], 16 * b + 4 * t + p + 1)
                        hold(act, "act", m["mul"], 32 * b + 8 * t + 2 * p + 2)
                        act.activation(ge[p], bank[4 + p][:, :], ACT.Gelu_apprx_tanh).then_inc(m["ge"], 1)

                def late(kind, t):
                    i = LATE.index((kind, t)) + 8
                    if kind == "cm":
                        turned_high(m, kt(ta_hi[t]), use(i))
                    else:
                        turned_high(m, xt_hi[:, :, ds(b * TOK + t * P, P)], use(i))
                        copy(x_tok[:, ds(b * TT * E + t * E, E)], x2[t]).then_inc(m["out"], 1)

                for t in range(TT):
                    gelus(t)
                    if t >= 1:
                        late("cm", t - 1)
                    if t >= 2:
                        late("x2", t - 2)
                late("cm", TT - 1)
                late("x2", TT - 2)
                late("x2", TT - 1)

            def l1_high(which, g, j=0):
                half = (g % 2) * TOK
                if which == "q":
                    hold(act, "act", c["s"], 12 * g + 3 * j - 3)
                    hold(act, "act", c["proj"], 4 * g + j + 1)
                    copy(qt_hi[j % 2], bank[4][:, :]).then_inc(c["phi"], 1)
                elif which == "k":
                    hold(act, "act", c["kv"], 2 * g + 1)
                    copy(k1_hi[:, ds(half, TOK)], bank[5][:, :]).then_inc(c["kvh"], 1)
                else:
                    hold(act, "act", c["kv"], 2 * g + 2)
                    copy(v1_hi[:, ds(half, TOK)], bank[5][:, :]).then_inc(c["kvh"], 1)

            def l1_context_high(g, j):
                u = 4 * g + j
                hold(act, "act", c["pv"], u + 1)
                at = ((g // 4) % 2) * HEADS * TOK + (g % 4) * 4 * TOK + j * TOK
                copy(ct_hi[:, ds(at, TOK)], bank[6][:, :]).then_inc(c["chi"], 1)

            def l1_group(g):
                for j in range(4):
                    u = 4 * g + j
                    behind = 4 * g + j if is_first(g) else 2
                    ahead = 3 - j if is_last(g) else 4
                    exponentials(c, g, j, 0)
                    if behind >= 1:
                        probs_high(c, u - 1, (j + 1) % 2, 0)
                    exponentials(c, g, j, 1)
                    if behind >= 1:
                        probs_high(c, u - 1, (j + 1) % 2, 1)
                    exponentials(c, g, j, 2)
                    if behind >= 2:
                        l1_context_high(*((g, j - 2) if j >= 2 else (g - 1, j + 2)))
                    if ahead >= 2:
                        l1_high("q", *((g, j + 2) if j < 2 else (g + 1, j - 2)))
                    if behind >= 1:
                        probs_high(c, u - 1, (j + 1) % 2, 2)
                    if not is_last(g) and j < 2:
                        l1_high("kv"[j], g + 1)

            l1_high("k", 0)
            l1_high("q", 0, 0)
            l1_high("v", 0)
            l1_high("q", 0, 1)
            loop_groups(act, l1_group)
            l1_context_high(NT - 1, 2)
            for chunk in range(3):
                probs_high(c, NH - 1, 1, chunk)
            l1_context_high(NT - 1, 3)

            act.wait_ge(c["x"], NT)
            for b in range(0, NB):
                hold(act, "act", e["tlo"], TT * b + 2)
                for t in range(TT):
                    copy(x3[t], x_tok[:, ds(b * TT * E + t * E, E)]).then_inc(e["cc"], 1)
                for t in range(TT):
                    turned_high(e, xt_hi[:, :, ds(b * TOK + t * P, P)], (TT * b + t, t))
            act.sem_inc(e["ge"], 2)
            act.wait_ge(ld_b, 8 * 16)
            for b in range(0, NB):
                for i in range(NF):
                    n = NF * b + i
                    hold(act, "act", e["h"], n + 1)
                    hold(act, "act", e["y"], n + 1)
                    act.activation(hf[i % 2], bank[4 + i % 2][:, :], ACT.Gelu, bias=b1_col[:, i:i + 1]
                                   ).then_inc(e["ge"], 1)
                    hold(act, "act", e["ge"], n + 1 + 2)
                    copy(h_hi[i % 2], hf[i % 2]).then_inc(e["hhi"], 1)

        class Chain:

            def __init__(self, eng, who, semaphore, base):
                self.eng, self.who, self.sem, self.base, self.n = eng, who, semaphore, base, 0

            def __call__(self, ins):
                ins.then_inc(self.sem, 1)
                self.n += 1
                hold(self.eng, self.who, self.sem, self.base + self.n)

        def router(dve, chain, logits, n, ex_ready, lgd, ex, turn):
            w = n * NX

            def row(i):
                return rt[:, i, 0:w].rearrange("p (t x) -> p t x", x=NX)

            def wide(i):
                return r1c[:, i, 0:n].unsqueeze(2).to_broadcast([P, n, NX])

            rev = iota8[:, 0:w].rearrange("p (t x) -> p t x", x=NX)
            top = [r1c[:, i, 0:n] for i in range(4)]
            chain(dve.tensor_reduce(top[2], logits, AX.X, ALU.max))
            dve.tensor_tensor(row(0), logits, wide(2), ALU.subtract).then_inc(lgd, 1)
            hold(dve, "dve", ex, turn)
            chain(dve.tensor_reduce(top[2], row(1), AX.X, ALU.add))
            chain(dve.reciprocal(top[3], top[2]))
            chain(dve.tensor_tensor(row(2), row(1), wide(3), ALU.mult))
            for i, (src, ones) in enumerate(((2, 5), (3, 6))):
                chain(dve.tensor_reduce(top[i], row(src), AX.X, ALU.max))
                chain(dve.tensor_tensor(row(4), row(src), wide(i), ALU.is_equal))
                chain(dve.tensor_tensor(row(4), row(4), rev, ALU.mult))
                chain(dve.tensor_reduce(top[2], row(4), AX.X, ALU.max))
                chain(dve.tensor_tensor(row(ones), rev, wide(2), ALU.is_equal))
                if i == 0:
                    chain(dve.scalar_tensor_tensor(rt[:, 3, 0:w], rt[:, 5, 0:w], -2.0, rt[:, 2, 0:w],
                                                   ALU.mult, ALU.add))
            return row, wide, top

        @block.vector
        def _(dve):
            def low(out, bank_cols, hi):
                return dve.tensor_tensor(out, bank_cols, hi, ALU.subtract)

            dve.memset(scr[:, 12288:14336], 0.0).then_inc(z_ready, 1)
            dve.memset(scr[:, 8192:12288], 0.0).then_inc(z_ready, 1)
            dve.wait_ge(z_ready, 2)
            dve.wait_ge(w_hi_d, 1)
            low(wqkv_lo[:, :, :].rearrange("p k n -> p (k n)"), wqkv_f,
                wqkv_hi[:, :, :].rearrange("p k n -> p (k n)")).then_inc(w_lo_d, 1)

            def x_low(b):
                dve.wait_ge(x_hi_d, b + 1)
                low(xt_lo[:, :, b * TOK:(b + 1) * TOK], xt_f[:, b % 2, :].rearrange("p (k t) -> p k t", k=KE),
                    xt_hi[:, :, b * TOK:(b + 1) * TOK]).then_inc(x_lo_d, 1)

            def l0_parts_low(g):
                hold(dve, "dve", a["phi"], 2 * g + 1)
                low(q_tok[:, :, Q_LO:Q_LO + D0], bank[4][:, 0:E].rearrange("p (c d) -> p c d", d=D0),
                    q_tok[:, :, Q_HI:Q_HI + D0])
                low(k_tok[:, :, K_LO:K_LO + D0], bank[4][:, E:2 * E].rearrange("p (c d) -> p c d", d=D0),
                    k_tok[:, :, K_HI:K_HI + D0]).then_inc(a["plo"], 1)
                hold(dve, "dve", a["phi"], 2 * g + 2)
                low(k_tok[:, :, V_LO:V_LO + D0], bank[5][:, 0:E].rearrange("p (c d) -> p c d", d=D0),
                    k_tok[:, :, V_HI:V_HI + D0]).then_inc(a["plo"], 1)

            def l0_rows_odd(g, which):
                hold(dve, "dve", a["stk"], 4 * g + 2 * which + 2)
                rows = (Q_ROWS, K_ROWS)[which]
                base = (8192, 10240)[which]
                dst = scr[:, base:base + 2048].bitcast(BF16)
                dve.tensor_copy(
                    dst[0:rows, ds((g % 2) * 2048, 2048)].rearrange("p (t c) -> p t c", c=16)[:, :, 8:16],
                    bank[5][:, :].bitcast(BF16).rearrange("p (c t) -> p t c", t=P)[0:rows]).then_inc(a["stkd"], 1)

            def maxima(s, g, j, chunk, scale):
                u = 4 * g + j
                hold(dve, "dve", s["s"], 3 * u + chunk + 1)
                for qt, col in S_CHUNKS[chunk]:
                    w = (qt + 1) * P
                    last = dve.tensor_tensor_reduce(
                        s_sb[j % 2][:, S_OFF[qt]:S_OFF[qt] + w], bank[(3 * j + chunk) % 2][:, col:col + w],
                        mask[:, 512 - w:512], -scale, HUGE, ALU.add, ALU.min, nm[:, j % 2, qt:qt + 1])
                last.then_inc(s["max"], 1)

            def probs_low(s, u, jp, chunk):
                hold(dve, "dve", s["thi"], 3 * u + chunk + 1)
                w = T_LEN[chunk]
                at = slice(T_OFF[chunk], T_OFF[chunk] + w)
                tb = bank[(2, 3, 7)[chunk] if s is a else 2 + (3 * jp + chunk) % 2]
                low(pt_lo[jp][:, at], tb[:, 0:w], pt_hi[jp][:, at]).then_inc(s["tlo"], 1)

            def inverse_sums(s, u, jp):
                hold(dve, "dve", s["exp"], 3 * u + 3)
                dve.reciprocal(rr[:, jp, :], rs[:, jp, :]).then_inc(s["rr"], 1)

            def l0_group(g):
                for j in range(4):
                    u = 4 * g + j
                    behind = 4 * g + j if is_first(g) else 2
                    maxima(a, g, j, 1, D0 ** -0.5)
                    maxima(a, g, j, 2, D0 ** -0.5)
                    if behind >= 1:
                        probs_low(a, u - 1, (j + 1) % 2, 0)
                        probs_low(a, u - 1, (j + 1) % 2, 1)
                    if not (is_last(g) and j == 3):
                        maxima(a, *((g, j + 1) if j < 3 else (g + 1, 0)), 0, D0 ** -0.5)
                    if behind >= 1:
                        probs_low(a, u - 1, (j + 1) % 2, 2)
                    if not is_last(g):
                        if j == 0:
                            l0_parts_low(g + 1)
                        if j in (1, 2):
                            l0_rows_odd(g + 1, j - 1)

            x_low(0)
            l0_parts_low(0)
            x_low(1)
            l0_rows_odd(0, 0)
            l0_rows_odd(0, 1)
            x_low(2)
            x_low(3)
            dve.wait_ge(ld_c, 16)
            maxima(a, 0, 0, 0, D0 ** -0.5)
            loop_groups(dve, l0_group)
            for chunk in range(3):
                probs_low(a, NH - 1, 1, chunk)

            def turned_low(p, dst, hi, use):
                hold(dve, "dve", p["thi"], use[0] + 1)
                low(dst, bank[use[1] % 2][:, 0:E].rearrange("p (k t) -> p k t", k=KE), hi).then_inc(p["tlo"], 1)

            def kt(ap):
                return ap.rearrange("p (k t) -> p k t", k=KE)

            dve.sem_inc(m["tlo"], 2)
            dve.sem_inc(m["r"], 2)
            dve.sem_inc(m["mul"], 8)
            dve.sem_inc(m["out"], 1)
            dve.wait_ge(a["vc"], NH + 2)
            dve.wait_ge(xb_done, NB)
            M_CHAIN = 1 + 15 + 8 + 6
            for b in range(0, NB):
                chain = Chain(dve, "dve", m["dve"], M_CHAIN * b)

                def use(i):
                    return (USES * b + i, i)

                def joined(t, n, src, out, add):
                    hold(dve, "dve", m["o"], 8 * b + n + 1)
                    dve.tensor_tensor(out, src, add, ALU.add).then_inc(m["r"], 1)
                    hold(dve, "dve", m["r"], 8 * b + n + 1 + 2)
                    chain(dve.bn_stats(stats[:, t, :], out))
                    dve.bn_aggr(mv[:, t, :], stats[:, t, :]).then_inc(m["agg"], 1)

                def norm(t, n, rows):
                    hold(dve, "dve", m["rstd"], 8 * b + n + 1)
                    dve.tensor_scalar(rows, rows, mv[:, t, 0:1], rstd[:, t:t + 1], ALU.subtract, ALU.mult
                                      ).then_inc(m["x"], 1)

                norms = rcc.rearrange("p (h q) -> p h q", q=TT)
                chain(dve.reciprocal(norms, ctx0[:, ds(b * HEADS, HEADS), :, D0:VC].rearrange("p h q d -> p h (q d)")))
                for t in range(TT):
                    dve.tensor_tensor(cc[t].rearrange("p (h d) -> p h d", d=D0),
                                      ctx0[:, ds(b * HEADS, HEADS), t, 0:D0],
                                      norms[:, :, t:t + 1].to_broadcast([P, HEADS, D0]), ALU.mult
                                      ).then_inc(m["cc"], 1)
                for t in range(TT):
                    turned_low(m, kt(ta_lo[t]), kt(ta_hi[t]), use(t))
                for t in range(TT):
                    joined(t, t, bank[2 + t % 2][:, 0:E], x1[t], x_tok[:, ds(b * TT * E + t * E, E)])
                for t in range(TT):
                    norm(t, t, x1[t])
                for t in range(TT):
                    turned_low(m, kt(tb_lo[t]), kt(tb_hi[t]), use(4 + t))
                hold(dve, "dve", m["lg"], b + 1)
                dve.tensor_tensor(lg[:, 0:TT, :], bank[4][:, 0:TT * NX].rearrange("p (t x) -> p t x", x=NX),
                                  rb_bc[:, :].unsqueeze(1).to_broadcast([P, TT, NX]), ALU.add).then_inc(m["lgc"], 1)
                hold(dve, "dve", m["lgc"], b + 1)
                row, wide, top = router(dve, chain, lg[:, 0:TT, :], TT, None, m["lgd"], m["ex"], b + 1)
                chain(dve.tensor_tensor(top[2], top[0], top[1], ALU.add))
                chain(dve.reciprocal(top[3], top[2]))
                chain(dve.tensor_tensor(row(0), row(5), wide(0), ALU.mult))
                chain(dve.tensor_tensor(row(1), row(6), wide(1), ALU.mult))
                chain(dve.tensor_tensor(row(0), row(0), row(1), ALU.add))
                chain(dve.tensor_tensor(gates[:, 0:TT, :], row(0), wide(3), ALU.mult))
                hold(dve, "dve", m["out"], TT * b + 1)

                def mix(t):
                    for x in range(NX):
                        p = x // 2
                        hold(dve, "dve", m["ge"], 16 * b + 4 * t + p + 1 + 4)
                        part = ge[p][:, (x % 2) * E:(x % 2 + 1) * E]
                        gate = gates[:, t, x:x + 1]
                        if x == 0:
                            ins = dve.tensor_scalar(comb[t], part, gate, None, ALU.mult)
                        else:
                            hold(dve, "dve", m["mul"], 32 * b + 8 * t + x + 8)
                            ins = dve.scalar_tensor_tensor(comb[t], part, gate, comb[t], ALU.mult, ALU.add)
                        ins.then_inc(m["mul"], 1)

                def late(kind, t):
                    i = LATE.index((kind, t)) + 8
                    if kind == "cm":
                        turned_low(m, kt(ta_lo[t]), kt(ta_hi[t]), use(i))
                    else:
                        ts = ds(b * TOK + t * P, P)
                        turned_low(m, xt_lo[:, :, ts], xt_hi[:, :, ts], use(i))

                def second(t):
                    hold(dve, "dve", m["xb"], TT * b + t + 1)
                    joined(t, 4 + t, bank[2 + t % 2][:, 0:E], x2[t], x1b[t])

                for t in range(TT):
                    if t >= 2:
                        norm(t - 2, 4 + t - 2, x2[t - 2])
                    mix(t)
                    if t >= 1:
                        late("cm", t - 1)
                    if t >= 2:
                        late("x2", t - 2)
                    if t >= 1:
                        second(t - 1)
                norm(2, 6, x2[2])
                late("cm", 3)
                late("x2", 2)
                second(3)
                norm(3, 7, x2[3])
                late("x2", 3)
                assert chain.n == M_CHAIN, chain.n

            dve.wait_ge(m["out"], NT + 1)

            def l1_low(which, g, j=0):
                half = (g % 2) * TOK
                if which == "q":
                    hold(dve, "dve", c["phi"], 4 * g + j + 1)
                    low(qt_lo[j % 2], bank[4][:, :], qt_hi[j % 2]).then_inc(c["plo"], 1)
                elif which == "k":
                    hold(dve, "dve", c["kvh"], 2 * g + 1)
                    low(k1_lo[:, ds(half, TOK)], bank[5][:, :], k1_hi[:, ds(half, TOK)]
                        ).then_inc(c["kvl"], 1)
                else:
                    hold(dve, "dve", c["kvh"], 2 * g + 2)
                    low(v1_lo[:, ds(half, TOK)], bank[5][:, :], v1_hi[:, ds(half, TOK)]
                        ).then_inc(c["kvl"], 1)

            def l1_context_low(g, j):
                u = 4 * g + j
                hold(dve, "dve", c["chi"], u + 1)
                at = ((g // 4) % 2) * HEADS * TOK + (g % 4) * 4 * TOK + j * TOK
                low(ct_lo[:, ds(at, TOK)], bank[6][:, :], ct_hi[:, ds(at, TOK)]).then_inc(c["clo"], 1)

            def l1_join(t):
                rows = x_tok[:, ds(t * E, E)]
                hold(dve, "dve", c["o"], t + 1)
                dve.tensor_tensor(rows, bank[7][:, 0:E], rows, ALU.add).then_inc(c["od"], 1)
                hold(dve, "dve", c["od"], t + 2)
                dve.bn_stats(stats[:, 0, :], rows).then_inc(c["st"], 1)
                hold(dve, "dve", c["st"], t + 1)
                dve.bn_aggr(mv[:, 0, :], stats[:, 0, :]).then_inc(c["mv"], 1)

            def l1_norm(t):
                rows = x_tok[:, ds(t * E, E)]
                hold(dve, "dve", c["rstd"], t + 1)
                dve.tensor_scalar(rows, rows, mv[:, 0, 0:1], rstd[:, 0:1], ALU.subtract, ALU.mult
                                  ).then_inc(c["x"], 1)

            def l1_group(g, dense):
                for j in range(4):
                    u = 4 * g + j
                    behind = 4 * g + j if is_first(g) else 2
                    ahead = 3 - j if is_last(g) else 4
                    maxima(c, g, j, 1, D1 ** -0.5)
                    maxima(c, g, j, 2, D1 ** -0.5)
                    if behind >= 1:
                        probs_low(c, u - 1, (j + 1) % 2, 0)
                        probs_low(c, u - 1, (j + 1) % 2, 1)
                    inverse_sums(c, u, j % 2)
                    if behind >= 2:
                        l1_context_low(*((g, j - 2) if j >= 2 else (g - 1, j + 2)))
                    if ahead >= 2:
                        l1_low("q", *((g, j + 2) if j < 2 else (g + 1, j - 2)))
                    if behind >= 1:
                        probs_low(c, u - 1, (j + 1) % 2, 2)
                    if ahead >= 1:
                        maxima(c, *((g, j + 1) if j < 3 else (g + 1, 0)), 0, D1 ** -0.5)
                    if not is_last(g) and j < 2:
                        l1_low("kv"[j], g + 1)
                    if g > TT and j == 0:
                        l1_norm(g - TT - 1)
                    if dense and j == 3:
                        l1_join(g - TT)

            dve.sem_inc(c["od"], 1)
            l1_low("k", 0)
            l1_low("q", 0, 0)
            l1_low("v", 0)
            l1_low("q", 0, 1)
            maxima(c, 0, 0, 0, D1 ** -0.5)
            l1_group(0, False)
            for g in range(1, TT):
                l1_group(g, False)
            for g in range(TT, NT - 1):
                l1_group(g, True)
            l1_group(NT - 1, True)
            l1_context_low(NT - 1, 2)
            for chunk in range(3):
                probs_low(c, NH - 1, 1, chunk)
            l1_context_low(NT - 1, 3)
            l1_norm(NT - TT - 1)
            for g in range(NT, NT + TT):
                l1_join(g - TT)
                l1_norm(g - TT)

            dve.wait_ge(c["x"], NT)
            dve.sem_inc(e["tlo"], 2)
            dve.sem_inc(e["lgc"], 1)
            for b in range(0, NB):
                for t in range(TT):
                    ts = ds(b * TOK + t * P, P)
                    turned_low(e, xt_lo[:, :, ts], xt_hi[:, :, ts], (TT * b + t, t))
                hold(dve, "dve", e["lg"], b + 1)
                dve.tensor_copy(lg[:, ds(b * TT, TT), :],
                                bank[2][:, 0:TT * NX].rearrange("p (t x) -> p t x", x=NX)).then_inc(e["lgc"], 1)
            dve.wait_ge(e["lgc"], NB + 1)
            chain = Chain(dve, "dve", e["dve"], 0)
            row, wide, top = router(dve, chain, lg[:, :, :], NT, None, e["lgd"], e["ex"], 1)
            for i in range(2):
                dve.tensor_copy(picks[:, i * NT:(i + 1) * NT, :], row(5 + i)).then_inc(e["picks"], 1)
            dve.wait_ge(e["rank"], 1)
            chain(dve.tensor_scalar(cnt[:, :], bank[3][:, 0:2 * NT * NX], float(CAP), None, ALU.is_le))
            for i in range(2):
                chain(dve.tensor_tensor(row(i), cnt[:, i * NT * NX:(i + 1) * NT * NX].rearrange(
                    "p (t x) -> p t x", x=NX), row(5 + i), ALU.mult))
                chain(dve.tensor_reduce(top[2 + i], row(i), AX.X, ALU.add))
                chain(dve.tensor_tensor(top[2 + i], top[2 + i], top[i], ALU.mult))
            dve.tensor_tensor(g1[:, :], top[2], top[3], ALU.add).then_inc(e["gates"], 1)

            dve.sem_inc(e["yr"], 1)
            dve.wait_ge(e["gates"], 1)
            for b in range(0, NB):
                chain = Chain(dve, "dve", e["dve"], E_CHAIN + TT * b)
                for i in range(NF):
                    hold(dve, "dve", e["hhi"], NF * b + i + 1)
                    low(h_lo[i % 2], hf[i % 2], h_hi[i % 2]).then_inc(e["hlo"], 1)
                hold(dve, "dve", e["y"], NF * (b + 1) + 2)
                for t in range(TT):
                    hold(dve, "dve", e["xb"], TT * b + t + 1)
                    dve.scalar_tensor_tensor(y4[t], bank[6 + t // 2][:, (t % 2) * E:(t % 2 + 1) * E], g1b[:, t:t + 1],
                                             x3b[t], ALU.mult, ALU.add).then_inc(e["yr"], 1)
                    hold(dve, "dve", e["yr"], TT * b + t + 2)
                    chain(dve.bn_stats(stats[:, t, :], y4[t]))
                    dve.bn_aggr(mv[:, t, :], stats[:, t, :]).then_inc(e["agg"], 1)
                for t in range(TT):
                    hold(dve, "dve", e["rstd"], TT * b + t + 1)
                    dve.tensor_scalar(x_tok[:, ds(b * TT * E + t * E, E)], y4[t], mv[:, t, 0:1],
                                      rstd[:, t:t + 1], ALU.subtract, ALU.mult).then_inc(e["x"], 1)

        @block.gpsimd
        def _(pool):
            pool.memset(one_f[:, :], 1.0).then_inc(c_ready, 1)
            pool.memset(neg_half[:, :], -0.5).then_inc(c_ready, 1)
            pool.memset(e_base[:, :], 2.718281828459045).then_inc(c_ready, 1)
            pool.memset(ones_b[:, :], 1.0).then_inc(c_ready, 1)
            for i in range(2):
                pool.memset(v0[i][:, :, :, :], 1.0).then_inc(c_ready, 1)
            pool.wait_ge(ld_c, 16)
            pool.tensor_copy(ident_b[:, :], ident_f).then_inc(c_ready, 1)
            pool.tensor_copy(upper_b[:, :], upper_f).then_inc(c_ready, 1)

            def duplicates(g):
                hold(pool, "pool", a["phi"], 2 * g + 1)
                for tok, src, dst in ((q_tok, Q_HI, Q_HI2), (k_tok, K_HI, K_HI2)):
                    pool.tensor_copy(tok[:, :, dst:dst + D0], tok[:, :, src:src + D0]).then_inc(a["dup"], 1)

            def split_chunk(n, part):
                slot = stage[:, ds((n % 2) * CH, CH)]
                at = ds(n * CH, CH)
                if part == 0:
                    pool.wait_ge(ld_ch[n % 2], 16 * (n // 2 + 1))
                    pool.tensor_tensor(w_hi[:, at], slot, one_f[:, 0:1].to_broadcast([P, CH]), ALU.mult
                                       ).then_inc(pool_seq, 1)
                else:
                    pool.wait_ge(pool_seq, n + 1)
                    pool.tensor_tensor(w_lo[:, at], slot, w_hi[:, at], ALU.subtract).then_inc(ch_done, 1)

            def l0_group(g):
                for j in range(4):
                    u = 4 * g + j
                    if j == 0 and not is_last(g):
                        duplicates(g + 1)
                    for n in range(2 * NCH * u // NH, 2 * NCH * (u + 1) // NH):
                        split_chunk(n // 2, n % 2)

            pool.wait_ge(c_ready, C_ALL)
            pool.wait_ge(z_ready, 2)
            duplicates(0)
            loop_groups(pool, l0_group)
            pool.wait_ge(ld_xtok, 16)
            pool.wait_ge(ld_b, 8 * 16)
            for b in range(NB):
                rows = x_tok[:, b * TT * E:(b + 1) * TT * E].rearrange("p (t e) -> p t e", e=E)
                pool.tensor_tensor(rows, rows, bp_bc[:, :].unsqueeze(1).to_broadcast([P, TT, E]), ALU.add
                                   ).then_inc(xb_done, 1)
            chain = Chain(pool, "pool", eb_seq, 0)
            chain(pool.tensor_copy(rw_hi[:, :, :], rw_f[:, :, :]))
            chain(pool.tensor_tensor(rw_lo[:, :, :], rw_f[:, :, :], rw_hi[:, :, :], ALU.subtract))
            chain(pool.tensor_copy(eb_p[:, 0, :], eb_f[:, :]))
            chain(pool.tensor_tensor(eb_r[:, 0, :], eb_f[:, :], eb_p[:, 0, :], ALU.subtract))
            chain(pool.tensor_copy(eb_p[:, 1, :], eb_r[:, 0, :]))
            chain(pool.tensor_tensor(eb_r[:, 1, :], eb_r[:, 0, :], eb_p[:, 1, :], ALU.subtract))
            pool.tensor_copy(eb_p[:, 2, :], eb_r[:, 1, :]).then_inc(eb_ready, 1)

            def inverse_deviation(p, t, ready, seq, value):
                hold(pool, "pool", p[ready], value)
                pool.tensor_scalar(var_e[:, t:t + 1], mv[:, t, 1:2], EPS, 1.0, ALU.add, ALU.mult).then_inc(p[seq], 1)
                hold(pool, "pool", p[seq], value)
                pool.tensor_tensor(rstd[:, t:t + 1], var_e[:, t:t + 1], neg_half[:, 0:1], ALU.pow
                                   ).then_inc(p["rstd"], 1)

            def exponentials(lgd, ex, value, w):
                hold(pool, "pool", lgd, value)
                pool.tensor_tensor(rt[:, 1, 0:w], e_base[:, 0:w], rt[:, 0, 0:w], ALU.pow).then_inc(ex, 1)

            pool.wait_ge(c_ready, C_ALL)
            for b in range(0, NB):
                for t in range(TT):
                    inverse_deviation(m, t, "agg", "pool", 8 * b + t + 1)
                for t in range(TT):
                    hold(pool, "pool", m["x"], 8 * b + t + 1)
                    pool.tensor_tensor(x1b[t], x1[t], outb_bc[:, :], ALU.add).then_inc(m["xb"], 1)
                exponentials(m["lgd"], m["ex"], b + 1, TT * NX)
                for t in range(TT):
                    inverse_deviation(m, t, "agg", "pool", 8 * b + 4 + t + 1)

            def l1_group(g, dense):
                for j in range(4):
                    u = 4 * g + j
                    hold(pool, "pool", c["rr"], u + 1)
                    for qt in range(TT):
                        at = s_sb[j % 2][:, S_OFF[qt]:S_OFF[qt] + (qt + 1) * P]
                        last = pool.tensor_scalar(at, at, rr[:, j % 2, qt:qt + 1], 1.0, ALU.mult, ALU.mult)
                    last.then_inc(c["nrm"], 1)
                if dense:
                    inverse_deviation(c, 0, "mv", "seq", g - TT + 1)

            for g in range(0, TT):
                l1_group(g, False)
            for g in range(TT, NT):
                l1_group(g, True)
            for g in range(NT, NT + TT):
                inverse_deviation(c, 0, "mv", "seq", g - TT + 1)

            exponentials(e["lgd"], e["ex"], 1, NT * NX)
            pool.wait_ge(e["gates"], 1)
            for b in range(0, NB):
                chain = Chain(pool, "pool", e["pool"], (1 + TT) * b)
                hold(pool, "pool", e["yr"], TT * b + 1)
                chain(pool.tensor_copy(g1b[:, :], g1[:, ds(b * TT, TT)]))
                for t in range(TT):
                    chain(pool.tensor_scalar(x3b[t], b2_bc[:, :], g1b[:, t:t + 1], 1.0, ALU.mult, ALU.mult))
                    pool.tensor_tensor(x3b[t], x3b[t], x_tok[:, ds(b * TT * E + t * E, E)], ALU.add
                                       ).then_inc(e["xb"], 1)
                for t in range(TT):
                    inverse_deviation(e, t, "agg", "seq", TT * b + t + 1)


def kernel(**inputs):
    import numpy as np
    import concourse.bacc as bacc
    from concourse.bass_utils import run_bass_kernel_spmd

    v = {n: np.asarray(x) for n, x in inputs.items()}

    def rows(w):
        return w.reshape(-1, P, w.shape[-1]).transpose(1, 0, 2)

    def cols(w):
        return rows(w).reshape(P, -1)

    x = v["L0_attn_x"].reshape(NT, P, E)
    up = np.arange(P)
    constants = np.concatenate([
        np.eye(P), up[:, None] <= up[None, :], np.zeros((P, 512 - P)),
        np.where(up[None, :] > up[:, None], MASKED, 0.0),
        np.broadcast_to(np.tile(NX - np.arange(NX), NT), (P, P))], axis=1).astype(np.float32)
    experts = v["L0_ffn_expert_w"].transpose(1, 0, 2).reshape(E, NX * E)
    arrays = {
        "x_tok": x.transpose(1, 0, 2),
        "x_t": v["L0_attn_x"].reshape(NB, TOK, KE, P).transpose(3, 0, 2, 1).reshape(P, NB, KE * TOK),
        "wqkv": cols(np.concatenate([v["L0_attn_W" + n].T for n in "qkv"], axis=1)),
        "wall": np.concatenate([cols(w) for w in (
            v["L0_attn_Wp"].T, v["L0_ffn_out_w"], experts, v["L1_attn_w_q"], v["L1_attn_w_kv"],
            v["L1_attn_w_dense"], v["L1_ffn_w1"].T, v["L1_ffn_w2"].T)], axis=1),
        "constants": constants,
        "bp": v["L0_attn_bp"], "outb": v["L0_ffn_out_b"], "b2": v["L1_ffn_b2"], "rb": v["L0_ffn_router_b"],
        "eb": v["L0_ffn_expert_b"].reshape(16, P),
        "rw0": cols(v["L0_ffn_router_w"]), "rw1": cols(v["L1_ffn_router_w"].T),
        "b1": v["L1_ffn_b1"].reshape(NF, P).T,
    }
    arrays = {n: np.ascontiguousarray(z) for n, z in arrays.items()}
    nc = bacc.Bacc("TRN2", target_bir_lowering=False, num_devices=1)
    args = [nc.dram_tensor(f"{n}_in", z.shape, mybir.dt.from_np(z.dtype), kind="ExternalInput").ap()
            for n, z in arrays.items()]
    out = nc.dram_tensor("out", (P, NT, E), F32, kind="ExternalOutput").ap()
    build(nc, *args, out)
    r = run_bass_kernel_spmd(nc, [{f"{n}_in": z for n, z in arrays.items()}], core_ids=[0])
    return np.asarray(r.results[0]["out"]).transpose(1, 0, 2).reshape(NB, TOK, E)
```

```python
from contextlib import ExitStack

import concourse.bass as bass
from concourse import mybir

F32 = mybir.dt.float32
BF16 = mybir.dt.bfloat16
ALU = mybir.AluOpType
ACT = mybir.ActivationFunctionType
AX = mybir.AxisListType

P = 128
E = 256
KE = E // P
NB = 4
TOK = 512
TT = TOK // P
NT = NB * TT
HEADS = 16
D0 = E // HEADS
D1 = 128
NH = NB * HEADS
VC = D0 + 1
NX = 8
FF = 1024
NF = FF // P
CAP = 64
EPS = 1e-5
CH = 1024
NCH = 19
CONSTS = 3 * P + 512
MASKED = -1e30
HUGE = 3e38

S_CHUNKS = (((3, 0),), ((2, 0), (0, 384)), ((1, 0),))
S_OFF = {3: 0, 2: 512, 0: 896, 1: 1024}
S_COLS = 1280
T_CHUNKS = (
    tuple((0, qt, qt * P) for qt in range(4)),
    tuple((1, qt, (qt - 1) * P) for qt in range(1, 4)) + ((3, 3, 384),),
    tuple((2, qt, (qt - 2) * P) for qt in range(2, 4)),
)
T_OFF = (0, 512, 1024)
T_LEN = (512, 512, 256)
PT_COL = {(kt, qt): T_OFF[c] + col for c, chunk in enumerate(T_CHUNKS) for kt, qt, col in chunk}

Q_HI, Q_HI2, Q_LO, Q_ROWS = 0, 16, 32, 48
K_HI, K_LO, K_HI2, V_HI, V_LO, K_ROWS = 0, 16, 32, 48, 64, 80

LEAD = 5
TURN_LEADS = (("x1", LEAD), ("x2", -2), ("cm", -1), ("cc", LEAD + 2))
STEPS = range(-LEAD - 2, NT + 2)
EARLY = range(-LEAD - 2, -2)
TURNS = [(kind, n + lead) for n in STEPS for kind, lead in TURN_LEADS if 0 <= n + lead < NT]
DVE_X = 5
MIX = DVE_X + 1
EARLY_TURNS = sum(0 <= n + lead < NT for n in EARLY for _, lead in TURN_LEADS)
EARLY_SLOTS = range(-len(EARLY), 0)
X_PIECES = (((0, P), (P, TOK)), ((0, TOK),))


def x_pieces(b):
    return b + (b > 0)


TB = 7
C_ALL = 7


def tail_steps():
    steps = []
    between = {(0, 1, "hidden"): [("pv", 0)], (0, 0, "outputs"): [("dense", 12)],
               (0, 1, "outputs"): [("turn", 11), ("dense", 13)], (0, 2, "outputs"): [("logits", 11), ("turn", 12)],
               (0, 3, "outputs"): [("dense", 14), ("logits", 12)], (0, 4, "outputs"): [("turn", 13), ("dense", 15)],
               (0, 5, "outputs"): [("logits", 13), ("turn", 14)], (0, 6, "outputs"): [("logits", 14)],
               (0, 7, "outputs"): [("turn", 15)], (1, 0, "outputs"): [("logits", 15)],
               (1, 1, "outputs"): [("route", 0)], (1, 3, "outputs"): [("choose", 0)],
               (1, 5, "outputs"): [("ranks", 0), ("gates", 0)], (1, 6, "outputs"): [("join", 0), ("join", 1)],
               (1, 7, "outputs"): [("norm", 0), ("join", 2)], (2, 0, "hidden"): [("norm", 1), ("join", 3)],
               (2, 0, "outputs"): [("norm", 2)], (2, 1, "outputs"): [("norm", 3)],
               (NB - 1, NF - 1, "outputs"): [(what, NT - TT + t) for what, t in (
                   ("join", 0), ("join", 1), ("norm", 0), ("join", 2), ("norm", 1), ("join", 3), ("norm", 2),
                   ("norm", 3))]}
    for b in range(1, NB - 1):
        for t in range(TT):
            between.setdefault((b + 1, t + 2, "hidden"), []).append(("join", b * TT + t))
            between.setdefault((b + 1, t + 3, "hidden"), []).append(("norm", b * TT + t))
    for b in range(NB):
        for i in range(NF + 1):
            for step in ([(b, i, "hidden")] if i < NF else []) + ([(b, i - 1, "outputs")] if i else []):
                steps.append(step)
                steps += [(b, k, what) for what, k in between.get(step, [])]
    return steps


TAIL = tail_steps()
Y_BANKS = ((2, 3), (4, 6), (5, 7), (2, 3))

WP, OUTW, EXPW, WQ, WKV, WD, W1, W2 = 0, 512, CH, 5 * CH, 9 * CH, 11 * CH, 15 * CH, 17 * CH


def build(nc, x_tok_d, x_t_d, wqkv_d, wall_d, const_d, bp_d, outb_d, b2_d, rb_d, eb_d, rw0_d, rw1_d, b1_d, out_d):
    ctx = ExitStack()
    with ctx:
        def sb(name, shape, dt=F32):
            return ctx.enter_context(nc.sbuf_tensor(name, shape, dt))

        def sem(name):
            return ctx.enter_context(nc.semaphore(name))

        def ds(start, size):
            return slice(start, start + size)

        x_tok = sb("x_tok", [P, NT * E])
        xt_hi = sb("xt_hi", [P, KE, NB * TOK], BF16)
        xt_lo = sb("xt_lo", [P, KE, NB * TOK], BF16)
        w_hi = sb("w_hi", [P, NCH * CH], BF16)
        w_lo = sb("w_lo", [P, NCH * CH], BF16)
        wqkv_hi = sb("wqkv_hi", [P, KE, 3 * E], BF16)
        wqkv_lo = sb("wqkv_lo", [P, KE, 3 * E], BF16)
        scr = sb("scr", [P, 16384])
        s_sb = [sb(f"s_sb{i}", [P, S_COLS]) for i in range(2)]
        pt_hi = [sb(f"pt_hi{i}", [P, S_COLS], BF16) for i in range(2)]
        pt_lo = [sb(f"pt_lo{i}", [P, S_COLS], BF16) for i in range(2)]
        consts = sb("consts", [P, CONSTS])
        ident_b = sb("ident_b", [P, P], BF16)
        ones_b = sb("ones_b", [P, P], BF16)
        upper_b = sb("upper_b", [P, P], BF16)
        bp_bc = sb("bp_bc", [P, E])
        outb_bc = sb("outb_bc", [P, E])
        b2_bc = sb("b2_bc", [P, E])
        rb_bc = sb("rb_bc", [P, NX])
        b1_col = sb("b1_col", [P, NF])
        rw_f = sb("rw_f", [P, 2, KE * NX])
        rw_hi = sb("rw_hi", [P, 2, KE * NX], BF16)
        rw_lo = sb("rw_lo", [P, 2, KE * NX], BF16)
        nm = sb("nm", [P, 2, 4])
        rs = sb("rs", [P, 2, 4])
        rr = sb("rr", [P, 2, 4])
        v0 = [sb(f"v0_{i}", [P, 4, 2, VC], BF16) for i in range(2)]
        stats = sb("stats", [P, 4, 6])
        mv = sb("mv", [P, 4, 2])
        var_e = sb("var_e", [P, 4])
        rstd = sb("rstd", [P, 4])
        one_f = sb("one_f", [P, 1])
        neg_half = sb("neg_half", [P, 4])
        r1c = sb("r1c", [P, 4, NT])
        g1 = sb("g1", [P, NT])
        lg_sb = sb("lg_sb", [P, NT * NX])

        ident_f = consts[:, 0:P]
        upper_f = consts[:, P:2 * P]
        mask = consts[:, 2 * P:2 * P + 512]
        iota8 = consts[:, 768:768 + P]

        qt_hi = [w_hi[:, TOK * i:TOK * (i + 1)] for i in range(2)]
        qt_lo = [w_lo[:, TOK * i:TOK * (i + 1)] for i in range(2)]
        k1_hi, k1_lo = w_hi[:, 1024:2048], w_lo[:, 1024:2048]
        v1_hi, v1_lo = w_hi[:, 2048:3072], w_lo[:, 2048:3072]
        lg = lg_sb[:, :].rearrange("p (t x) -> p t x", x=NX)
        rt = s_sb[0][:, 0:8 * NT * NX].rearrange("p (i c) -> p i c", i=8)
        gates = s_sb[0][:, 1152:1280].rearrange("p (t x) -> p t x", x=NX)
        cnt = s_sb[1][:, 0:2 * NT * NX]
        picks = s_sb[1][:, 256:384].bitcast(BF16).rearrange("p (t x) -> p t x", x=NX)

        xt_f = scr[:, 0:2048].rearrange("p (s c) -> p s c", s=2)
        ctx0 = scr[:, 2048:2048 + NH * TT * VC].rearrange("p (u q d) -> p u q d", q=TT, d=VC)
        q_tok = scr[:, 12288:13312].bitcast(BF16).rearrange("p (c s) -> p c s", s=P)
        k_tok = scr[:, 13312:14336].bitcast(BF16).rearrange("p (c s) -> p c s", s=P)
        wqkv_f = scr[:, 14336:14336 + KE * 3 * E]
        stage = scr[:, 14336:16384]
        eb_f = scr[0:16, 6400:6528]
        eb_p = scr[0:16, 6528:6720].bitcast(BF16).rearrange("p (i d) -> p i d", i=3)
        eb_r = scr[0:16, 6720:6976].rearrange("p (i d) -> p i d", i=2)
        eb3 = scr[0:3, 15360:16384].bitcast(BF16)
        def tiles(base, n, width, dt=F32):
            return [scr[:, base + width * i:base + width * (i + 1)].bitcast(dt) if dt != F32
                    else scr[:, base + width * i:base + width * (i + 1)] for i in range(n)]

        rcc = scr[:, 7168:7168 + NH * TT].rearrange("p (u q) -> p u q", q=TT)
        ta_hi, ta_lo = tiles(0, 2, P, BF16), tiles(256, 2, P, BF16)
        tc_hi, tc_lo = tiles(512, 2, P, BF16), tiles(768, 2, P, BF16)
        cc = tiles(1024, 2, E)
        comb = tiles(1536, 2, E)
        tb_hi, tb_lo = tiles(12288, TB, P, BF16), tiles(13184, TB, P, BF16)
        ge = tiles(8192, 4, 512)
        pc = tiles(10240, 2, E)
        pc_x = tiles(10752, 2, E)
        ct_hi = scr[:, 0:8192].bitcast(BF16)
        ct_lo = scr[:, 8192:16384].bitcast(BF16)
        hf = tiles(0, 2, 512)
        h_hi, h_lo = tiles(1024, 2, 256, BF16), tiles(1536, 2, 256, BF16)
        b2g = tiles(2048, 2, E)

        bank = [ctx.enter_context(nc.psum_tensor(f"bank{i}", [P, 512], F32)) for i in range(8)]

        ld_w = sem("ld_w")
        ld_x = [sem(f"ld_x{i}") for i in range(2)]
        ld_xtok = sem("ld_xtok")
        ld_c = sem("ld_c")
        ld_b = sem("ld_b")
        ld_ch = [sem(f"ld_ch{i}") for i in range(2)]
        ch_done = sem("ch_done")
        eb_ready = sem("eb_ready")
        eb_moved = sem("eb_moved")
        c_ready = sem("c_ready")
        z_ready = sem("z_ready")
        w_hi_d = sem("w_hi_d")
        w_lo_d = sem("w_lo_d")
        x_hi_d = sem("x_hi_d")
        x_lo_d = sem("x_lo_d")
        pool_seq = sem("pool_seq")
        eb_seq = sem("eb_seq")
        xb_done = sem("xb_done")
        out_done = sem("out_done")

        def hold(eng, semaphore, value):
            if value > 0:
                eng.wait_ge(semaphore, value)

        def group_sems(p):
            return {n: sem(f"{p}_{n}") for n in (
                "proj", "stk", "s", "w", "t", "pv", "phi", "plo", "dup", "kv", "kvh", "kvl", "stka", "stkd", "max", "exp",
                "thi", "tlo", "vc", "rr", "nrm", "chi", "clo", "o", "od", "st", "mv", "seq", "rstd", "x")}

        a = group_sems("l0")
        c = group_sems("l1")
        m = {n: sem(f"mix_{n}") for n in (
            "rc", "cc", "tp", "thi", "tlo", "o1", "o2", "r1", "r2", "agg1", "agg2", "rstd1", "rstd2", "x1", "x2", "xb",
            "lg", "lgc", "lgd", "ex", "gates", "f", "ge", "mul", "pmul", "psum", "dve", "pool")}
        e = {n: sem(f"ffn_{n}") for n in (
            "tp", "thi", "tlo", "lg", "lgc", "lgd", "ex", "picks", "rank", "gates", "h", "ge", "hhi", "hlo",
            "y", "yr", "bg", "xb", "seq", "agg", "rstd", "x", "dve")}

        def turn_bank(i):
            return 4 if i < EARLY_TURNS else i % 2

        def first_bank(t):
            return 5 if t <= EARLY[-1] + LEAD + 1 else 2

        block = ctx.enter_context(nc.Block())

        def is_first(g):
            return g == 0

        def is_last(g):
            return g == NT - 1

        @block.sync
        def _(sp):
            sp.dma_start(wqkv_f, wqkv_d).then_inc(ld_w, 16)
            for b in range(2):
                sp.dma_start(xt_f[:, b, :], x_t_d[:, b, :]).then_inc(ld_x[b], 16)
            sp.dma_start(consts[:, :], const_d).then_inc(ld_c, 16)
            sp.wait_ge(w_lo_d, KE)
            for cc in range(2):
                sp.dma_start(stage[:, cc * CH:cc * CH + CH], wall_d[:, cc * CH:cc * CH + CH]).then_inc(ld_ch[cc], 16)
            sp.dma_start(x_tok[:, :].rearrange("p (t e) -> p t e", e=E), x_tok_d).then_inc(ld_xtok, 16)
            sp.dma_start(bp_bc[:, :], bp_d.partition_broadcast(P)).then_inc(ld_b, 16)
            sp.dma_start(outb_bc[:, :], outb_d.partition_broadcast(P)).then_inc(ld_b, 16)
            sp.dma_start(b2_bc[:, :], b2_d.partition_broadcast(P)).then_inc(ld_b, 16)
            sp.dma_start(rb_bc[:, :], rb_d.partition_broadcast(P)).then_inc(ld_b, 16)
            sp.dma_start(rw_f[:, 0, :], rw0_d).then_inc(ld_b, 16)
            sp.dma_start(rw_f[:, 1, :], rw1_d).then_inc(ld_b, 16)
            sp.dma_start(b1_col[:, :], b1_d).then_inc(ld_b, 16)
            for b in range(2, NB):
                sp.wait_ge(x_lo_d, x_pieces(b - 1))
                sp.dma_start(xt_f[:, b % 2, :], x_t_d[:, b, :]).then_inc(ld_x[b % 2], 16)
            for cc in range(2, NCH):
                sp.wait_ge(ch_done, cc - 1)
                sp.dma_start(stage[:, (cc % 2) * CH:(cc % 2) * CH + CH],
                             wall_d[:, cc * CH:cc * CH + CH]).then_inc(ld_ch[cc % 2], 16)
            sp.wait_ge(ch_done, NCH)
            sp.dma_start(eb_f, eb_d).then_inc(ld_b, 16)
            sp.wait_ge(eb_ready, 1)
            for i in range(3):
                sp.dma_start(eb3[i:i + 1, :], eb_p[:, i, :]).then_inc(eb_moved, 16)
            outputs = [(b * TT, TT) for b in range(NB - 1)] + [(t, 1) for t in range(NT - TT, NT)]
            for t, n in outputs:
                sp.wait_ge(e["x"], t + n)
                sp.dma_start(out_d[:, t:t + n, :],
                             x_tok[:, t * E:(t + n) * E].rearrange("p (t e) -> p t e", e=E)).then_inc(out_done, 16)
            sp.wait_ge(out_done, 16 * len(outputs))

        @block.tensor
        def _(pe):
            def mm3(out, l_hi, l_lo, r_hi, r_lo, start, stop, check=False):
                pe.matmul(out, l_hi, r_hi, start=start, stop=False, skip_group_check=check)
                pe.matmul(out, l_hi, r_lo, start=False, stop=False, skip_group_check=check)
                return pe.matmul(out, l_lo, r_hi, start=False, stop=stop, skip_group_check=check)

            def l0_project(g):
                t0 = g * P
                b = g // TT
                pe.wait_ge(x_lo_d, 1 if g == 0 else x_pieces(b + 1))
                if is_first(g):
                    pe.wait_ge(w_lo_d, KE)
                hold(pe, a["stka"], 2 * g)
                hold(pe, a["stkd"], 2 * g)
                for k in range(KE):
                    last = mm3(bank[4][:, 0:512], xt_hi[:, k, ds(t0, P)], xt_lo[:, k, ds(t0, P)],
                               wqkv_hi[:, k, 0:512], wqkv_lo[:, k, 0:512], k == 0, k == KE - 1)
                last.then_inc(a["proj"], 1)
                for k in range(KE):
                    last = mm3(bank[5][:, 0:E], xt_hi[:, k, ds(t0, P)], xt_lo[:, k, ds(t0, P)],
                               wqkv_hi[:, k, 512:768], wqkv_lo[:, k, 512:768], k == 0, k == KE - 1)
                last.then_inc(a["proj"], 1)

            def l0_stack(g, which):
                tok = (q_tok, k_tok)[which]
                if which == 0:
                    hold(pe, a["plo"], 2 * g + 2)
                    hold(pe, a["dup"], 2 * g + 2)
                    if is_first(g):
                        pe.wait_ge(z_ready, 2)
                        pe.wait_ge(c_ready, C_ALL)
                for half in range(2):
                    if which == 1:
                        hold(pe, a[("stka", "stkd")[half]], 2 * g + 1)
                    out = bank[4 + half][:, :].bitcast(BF16)
                    for i in range(8):
                        last = pe.transpose(out[:, i * P:(i + 1) * P], tok[:, 8 * half + i, :], ident_b[:, :])
                    last.then_inc(a["stk"], 1)

            def l0_scores(g, j, chunk):
                u = g * 4 + j
                if j == 0 and chunk == 0:
                    hold(pe, a["stka"], 2 * g + 2)
                    hold(pe, a["stkd"], 2 * g + 2)
                n = 3 * u + chunk
                hold(pe, a["max"], n - 1)
                for qt, col in S_CHUNKS[chunk]:
                    w = (qt + 1) * P
                    last = pe.matmul(bank[(3 * j + chunk) % 2][:, col:col + w],
                                     q_stv(g)[:, ds(q_off(g) + j * TOK + qt * P, P)],
                                     k_stv(g)[:, ds(q_off(g) + j * TOK, w)], start=True, stop=True)
                last.then_inc(a["s"], 1)

            def q_stv(g):
                return scr[:, 8192:10240].bitcast(BF16)

            def k_stv(g):
                return scr[:, 10240:12288].bitcast(BF16)

            def q_off(g):
                return g % 2 * 2048

            def l0_step(n):
                hold(pe, a["vc"], n)
                if n < NH:
                    for kt in range(TT):
                        last = pe.matmul(bank[6][:, kt * 32:kt * 32 + 32],
                                         k_stv(n // 4)[:, ds(q_off(n // 4) + (n % 4) * TOK + kt * P, P)],
                                         ident_b[:, V_HI:V_HI + 2 * D0], start=True, stop=True)
                if n >= 2:
                    u, jp = n - 2, n % 2
                    hold(pe, a["tlo"], 3 * u + 3)
                    for qt in range(TT):
                        sums = bank[6][:, P + qt * VC:P + (qt + 1) * VC]
                        out = bank[6][:, P + qt * VC:P + qt * VC + D0]
                        for kt in range(qt + 1):
                            col = PT_COL[kt, qt]
                            hi, lo = pt_hi[jp][:, col:col + P], pt_lo[jp][:, col:col + P]
                            pe.matmul(sums, hi, v0[jp][:, kt, 0, :], start=(kt == 0), stop=False,
                                      skip_group_check=True)
                            pe.matmul(out, hi, v0[jp][:, kt, 1, 0:D0], start=False, stop=False,
                                      skip_group_check=True)
                            last = pe.matmul(sums, lo, v0[jp][:, kt, 0, :], start=False, stop=(kt == qt),
                                             skip_group_check=True)
                last.then_inc(a["w"], 1)

            def transposes(s, u, jp, chunk):
                if s is a:
                    if chunk == 0:
                        hold(pe, s["exp"], 3 * u + 3)
                    hold(pe, s["tlo"], 3 * u + chunk - 2)
                    tb = bank[(2, 3, 7)[chunk]]
                else:
                    if chunk == 0:
                        hold(pe, s["nrm"], u + 1)
                    hold(pe, s["tlo"], 3 * u + chunk - 1)
                    tb = bank[2 + (jp * 3 + chunk) % 2]
                for kt, qt, col in T_CHUNKS[chunk]:
                    last = pe.transpose(tb[:, col:col + P], s_sb[jp][:, S_OFF[qt] + kt * P:S_OFF[qt] + kt * P + P],
                                        ident_f)
                last.then_inc(s["t"], 1)

            def turn_mix(kind, t):
                i = TURNS.index((kind, t))
                if kind == "cc":
                    pe.wait_ge(m["cc"], t + 1)
                    src = cc[t % 2]
                elif kind == "cm":
                    pe.wait_ge(m["mul"], MIX * (t + 1))
                    src = comb[t % 2]
                else:
                    pe.wait_ge(m[kind], t + 1)
                    src = x_tok[:, t * E:(t + 1) * E]
                hold(pe, m["tlo"], i if i < EARLY_TURNS else i - 1)
                for k in range(KE):
                    last = pe.transpose(bank[turn_bank(i)][:, k * P:(k + 1) * P], src[:, k * P:(k + 1) * P], ident_f)
                last.then_inc(m["tp"], 1)

            def project(out, t_hi, t_lo, base, n=E):
                for k in range(KE):
                    last = mm3(out, t_hi[:, k * P:(k + 1) * P], t_lo[:, k * P:(k + 1) * P],
                               w_hi[:, base + k * n:base + (k + 1) * n], w_lo[:, base + k * n:base + (k + 1) * n],
                               k == 0, k == KE - 1)
                return last

            def first_project(t):
                pe.wait_ge(m["tlo"], TURNS.index(("cc", t)) + 1)
                hold(pe, m["r1"], t)
                hold(pe, m["lgc"], (t - 1) // TT)
                project(bank[first_bank(t)][:, 0:E], ta_hi[t % 2], ta_lo[t % 2], WP).then_inc(m["o1"], 1)

            def second_project(t):
                pe.wait_ge(m["tlo"], TURNS.index(("cm", t)) + 1)
                hold(pe, m["r2"], t)
                project(bank[3][:, 0:E], tc_hi[t % 2], tc_lo[t % 2], OUTW).then_inc(m["o2"], 1)

            def logits(b):
                pe.wait_ge(m["tlo"], TURNS.index(("x1", TT * b + TT - 1)) + 1)
                pe.wait_ge(m["r1"], min(TT * (b + 1) + 1, NT))
                for t in range(TT):
                    hi, lo = tb_hi[(TT * b + t) % TB], tb_lo[(TT * b + t) % TB]
                    for k in range(KE):
                        ks = slice(k * NX, (k + 1) * NX)
                        last = mm3(bank[2][:, t * NX:(t + 1) * NX], hi[:, k * P:(k + 1) * P],
                                   lo[:, k * P:(k + 1) * P], rw_hi[:, 0, ks], rw_lo[:, 0, ks],
                                   k == 0, k == KE - 1)
                last.then_inc(m["lg"], 1)

            def experts(t, p):
                hold(pe, m["ge"], 4 * (t - 1) + p + 1)
                out = bank[4 + p][:, :]
                pe.matmul(out, ones_b[0:3, :], eb3[:, p * 512:(p + 1) * 512], start=True, stop=False)
                for k in range(KE):
                    cs = slice(EXPW + k * NX * E + p * 512, EXPW + k * NX * E + (p + 1) * 512)
                    last = mm3(out, tb_hi[t % TB][:, k * P:(k + 1) * P], tb_lo[t % TB][:, k * P:(k + 1) * P],
                               w_hi[:, cs], w_lo[:, cs], False, k == KE - 1)
                last.then_inc(m["f"], 1)

            def early_step(n):
                if 0 <= n + LEAD:
                    turn_mix("x1", n + LEAD)
                if 0 <= n + LEAD + 1:
                    first_project(n + LEAD + 1)
                turn_mix("cc", n + LEAD + 2)

            def l0_group(g):
                for j in range(4):
                    u = g * 4 + j
                    behind = 4 * g + j if is_first(g) else 2
                    l0_scores(g, j, 2)
                    if behind >= 1:
                        for chunk in range(3):
                            transposes(a, u - 1, (j + 1) % 2, chunk)
                    if not (is_last(g) and j == 3):
                        gn, jn = (g, j + 1) if j < 3 else (g + 1, 0)
                        l0_scores(gn, jn, 0)
                        l0_scores(gn, jn, 1)
                    if j in (1, 2) and g + 1 < NT:
                        l0_stack(g + 1, j - 1)
                    if j == 3 and g + 2 < NT:
                        l0_project(g + 2)
                    l0_step(u)
                    if u - NH in EARLY_SLOTS:
                        if u - NH == EARLY_SLOTS[0]:
                            pe.wait_ge(ch_done, 1)
                        early_step(u - NH + 1 + EARLY[-1])

            pe.wait_ge(ld_c, 16)
            l0_project(0)
            l0_stack(0, 0)
            l0_stack(0, 1)
            l0_scores(0, 0, 0)
            l0_scores(0, 0, 1)
            l0_project(1)
            for g in range(NT):
                l0_group(g)
            for chunk in range(3):
                transposes(a, NH - 1, 1, chunk)
            l0_step(NH)
            l0_step(NH + 1)

            pe.wait_ge(ch_done, NCH)
            pe.wait_ge(eb_moved, 48)
            pe.wait_ge(a["vc"], NH + 2)
            def l1_project(which, g, j=0):
                tok = (g // 4) * TOK
                if which == "q":
                    hold(pe, c["plo"], 4 * g + j)
                    out = bank[4]
                else:
                    hold(pe, c["kvl"], 2 * g + (which == "v"))
                    if which == "k":
                        hold(pe, e["lgc"], g - TT - 2)
                    out = bank[5]
                if which == "v":
                    for tt in range(TT):
                        for k in range(KE):
                            base = WKV + k * 1024 + 512
                            last = mm3(out[:, tt * P:(tt + 1) * P],
                                       xt_hi[:, k, ds(tok + tt * P, P)], xt_lo[:, k, ds(tok + tt * P, P)],
                                       w_hi[:, ds(base + (g % 4) * P, P)],
                                       w_lo[:, ds(base + (g % 4) * P, P)], k == 0, k == KE - 1)
                else:
                    for k in range(KE):
                        base = WKV + k * 1024 + (g % 4) * P if which == "k" else WQ + k * 2048 + (g % 4) * TOK + j * P
                        last = mm3(out[:, :], w_hi[:, ds(base, P)], w_lo[:, ds(base, P)],
                                   xt_hi[:, k, ds(tok, TOK)], xt_lo[:, k, ds(tok, TOK)],
                                   k == 0, k == KE - 1)
                last.then_inc(c["proj" if which == "q" else "kv"], 1)

            for n in STEPS[len(EARLY):]:
                here, ahead, behind = 0 <= n < NT, n + LEAD + 1, n - 1
                if 0 <= n + LEAD < NT:
                    turn_mix("x1", n + LEAD)
                if n == NT:
                    pe.wait_ge(m["ge"], 4 * NT)
                    l1_project("k", 0)
                if here:
                    experts(n, 0)
                if 0 <= n + 4 < NT and (n + 4) % TT == TT - 1:
                    logits((n + 4) // TT)
                if 0 <= n - 2:
                    turn_mix("x2", n - 2)
                routed = 0 <= n + 4 < NT and (n + 4) % TT == TT - 1
                if 0 <= ahead < NT and not routed:
                    first_project(ahead)
                if here:
                    experts(n, 1)
                if 0 <= ahead < NT and routed:
                    first_project(ahead)
                if 0 <= behind < NT:
                    turn_mix("cm", behind)
                if 0 <= n + LEAD + 2 < NT:
                    turn_mix("cc", n + LEAD + 2)
                if n == NT:
                    l1_project("q", 0, 0)
                if here:
                    experts(n, 2)
                if 0 <= behind < NT:
                    second_project(behind)
                if n == NT:
                    l1_project("v", 0)
                if here:
                    experts(n, 3)
            l1_project("q", 0, 1)

            def l1_scores(g, j, chunk):
                u = 4 * g + j
                if chunk == 0:
                    hold(pe, c["plo"], u + 1)
                    if j == 0:
                        hold(pe, c["kvl"], 2 * g + 1)
                n = 3 * u + chunk
                hold(pe, c["max"], n - 1)
                kb = (g % 2) * TOK
                for qt, col in S_CHUNKS[chunk]:
                    w = (qt + 1) * P
                    qs = slice(qt * P, (qt + 1) * P)
                    last = mm3(bank[(3 * j + chunk) % 2][:, col:col + w], qt_hi[j % 2][:, qs], qt_lo[j % 2][:, qs],
                               k1_hi[:, ds(kb, w)], k1_lo[:, ds(kb, w)], True, True)
                last.then_inc(c["s"], 1)

            def l1_pv(g, j):
                u = 4 * g + j
                hold(pe, c["tlo"], 3 * u + 3)
                hold(pe, c["clo"], u)
                if j == 0:
                    hold(pe, c["kvl"], 2 * g + 2)
                vb = (g % 2) * TOK
                for kt in range(TT):
                    col = PT_COL[kt, kt]
                    w = TOK - kt * P
                    ps = slice(col, col + w)
                    vs = ds(vb + kt * P, P)
                    out = bank[6][:, kt * P:TOK]
                    pe.matmul(out, v1_hi[:, vs], pt_hi[j % 2][:, ps], start=(kt == 0), stop=False)
                    pe.matmul(out, v1_hi[:, vs], pt_lo[j % 2][:, ps], start=False, stop=False)
                    last = pe.matmul(out, v1_lo[:, vs], pt_hi[j % 2][:, ps], start=False, stop=(kt == TT - 1))
                last.then_inc(c["pv"], 1)

            def l1_dense(g, part, parts, ready):
                hold(pe, c["clo"], ready)
                if part == 0:
                    hold(pe, c["od"], g - TT + 1)
                cb = ((g // 4 + 1) % 2) * HEADS * TOK + (g % 4) * P
                edges = [HEADS * i // parts for i in range(parts + 1)]
                for hd in range(edges[part], edges[part + 1]):
                    cs = ds(cb + hd * TOK, P)
                    ws = slice(WD + hd * E, WD + (hd + 1) * E)
                    last = mm3(bank[7][:, 0:E], ct_hi[:, cs], ct_lo[:, cs], w_hi[:, ws], w_lo[:, ws],
                               hd == 0, hd == HEADS - 1)
                if part == parts - 1:
                    last.then_inc(c["o"], 1)

            def last_turn(t):
                pe.wait_ge(c["x"], t + 1)
                hold(pe, e["lgc"], t)
                for k in range(KE):
                    last = pe.transpose(bank[5][:, k * P:(k + 1) * P],
                                        x_tok[:, t * E + k * P:t * E + (k + 1) * P], ident_f)
                last.then_inc(e["tp"], 1)

            def last_logits(t):
                pe.wait_ge(e["tlo"], t + 1)
                for k in range(KE):
                    ks = slice(k * NX, (k + 1) * NX)
                    last = mm3(bank[5][:, E:E + NX], xt_hi[:, k, t * P:(t + 1) * P], xt_lo[:, k, t * P:(t + 1) * P],
                               rw_hi[:, 1, ks], rw_lo[:, 1, ks], k == 0, k == KE - 1)
                last.then_inc(e["lg"], 1)

            def l1_group(g, dense):
                for j in range(4):
                    u = 4 * g + j
                    behind = 4 * g + j if is_first(g) else 2
                    ahead = 3 - j if is_last(g) else 4
                    l1_scores(g, j, 2)
                    if behind >= 1:
                        transposes(c, u - 1, (j + 1) % 2, 0)
                        transposes(c, u - 1, (j + 1) % 2, 1)
                    if behind >= 2:
                        l1_pv(*((g, j - 2) if j >= 2 else (g - 1, j + 2)))
                    if ahead >= 2:
                        l1_project("q", *((g, j + 2) if j < 2 else (g + 1, j - 2)))
                    if behind >= 1:
                        transposes(c, u - 1, (j + 1) % 2, 2)
                    if ahead >= 1:
                        l1_scores(*((g, j + 1) if j < 3 else (g + 1, 0)), 0)
                    if not is_last(g) and j < 2:
                        l1_project("kv"[j], g + 1)
                    if g > TT and j == 2:
                        hold(pe, c["kvl"], 2 * min(g + 1, NT - 1) + 2)
                        last_turn(g - TT - 1)
                    if g > TT and j == 3:
                        last_logits(g - TT - 1)
                    if dense and j >= 2:
                        l1_dense(g, j - 2, 2, u - 2)
                    if ahead >= 1:
                        l1_scores(*((g, j + 1) if j < 3 else (g + 1, 0)), 1)

            pe.wait_ge(m["tlo"], len(TURNS))
            l1_scores(0, 0, 0)
            l1_scores(0, 0, 1)
            for g in range(NT):
                l1_group(g, g >= TT)

            def hidden(b, i):
                n = NF * b + i
                hold(pe, e["ge"], n - 1)
                for k in range(KE):
                    ws = slice(W1 + k * FF + i * P, W1 + k * FF + (i + 1) * P)
                    last = mm3(bank[i % 2][:, :], w_hi[:, ws], w_lo[:, ws],
                               xt_hi[:, k, b * TOK:(b + 1) * TOK], xt_lo[:, k, b * TOK:(b + 1) * TOK],
                               k == 0, k == KE - 1)
                last.then_inc(e["h"], 1)

            def outputs(b, i):
                pe.wait_ge(e["hlo"], NF * b + i + 1)
                if (b, i) == (2, 0):
                    pe.wait_ge(e["lgc"], NT)
                    pe.wait_ge(e["gates"], 1)
                if (b, i) == (3, 0):
                    pe.wait_ge(e["yr"], TT)
                for t in range(TT):
                    ts = slice(t * P, (t + 1) * P)
                    ws = slice(W2 + i * E, W2 + (i + 1) * E)
                    last = mm3(bank[Y_BANKS[b][t // 2]][:, (t % 2) * E:(t % 2 + 1) * E], h_hi[i % 2][:, ts],
                               h_lo[i % 2][:, ts], w_hi[:, ws], w_lo[:, ws],
                               i == 0 and t % 2 == 0, i == NF - 1 and t % 2 == 1, True)
                last.then_inc(e["y"], 1)

            def ranks():
                pe.wait_ge(e["picks"], 2)
                pe.matmul(bank[7][:, 0:2 * NT * NX], upper_b[:, :], picks[:, :, :], start=True, stop=False)
                for n in range(2 * NT - 1):
                    after = 2 * NT - 1 - n
                    last = pe.matmul(bank[7][:, (n + 1) * NX:2 * NT * NX], ones_b[:, :],
                                     picks[:, n:n + 1, :].to_broadcast([P, after, NX]),
                                     start=False, stop=(after == 1))
                last.then_inc(e["rank"], 1)

            l1_pv(NT - 1, 2)
            for chunk in range(3):
                transposes(c, NH - 1, 1, chunk)
            pe.wait_ge(c["plo"], NH)
            pe.wait_ge(c["max"], 3 * NH)
            for b, i, what in TAIL:
                if what == "hidden":
                    hidden(b, i)
                elif what == "outputs":
                    if (b, i) == (0, 0):
                        pe.wait_ge(c["tlo"], 3 * NH)
                    if (b, i) == (1, 0):
                        pe.wait_ge(c["clo"], NH)
                    outputs(b, i)
                elif what == "pv":
                    l1_pv(NT - 1, 3)
                elif what == "dense":
                    l1_dense(i + TT, 0, 1, NH)
                elif what == "turn":
                    last_turn(i)
                elif what == "logits":
                    last_logits(i)
                elif what == "ranks":
                    ranks()

        @block.scalar
        def _(act):
            def copy(out, in_):
                return act.activation(out, in_, ACT.Copy)

            act.wait_ge(ld_w, 16)
            for k in range(KE):
                copy(wqkv_hi[:, k, :], wqkv_f[:, k * 3 * E:(k + 1) * 3 * E]).then_inc(w_hi_d, 1)

            def x_high(b):
                act.wait_ge(ld_x[b % 2], 16 * (b // 2 + 1))
                for t0, t1 in X_PIECES[min(b, 1)]:
                    copy(xt_hi[:, :, b * TOK + t0:b * TOK + t1],
                         xt_f[:, b % 2, :].rearrange("p (k t) -> p k t", k=KE)[:, :, t0:t1]).then_inc(x_hi_d, 1)

            def l0_parts_high(g):
                hold(act, a["stk"], 4 * g)
                hold(act, a["proj"], 2 * g + 1)
                copy(q_tok[:, :, Q_HI:Q_HI + D0], bank[4][:, 0:E].rearrange("p (c d) -> p c d", d=D0))
                copy(k_tok[:, :, K_HI:K_HI + D0], bank[4][:, E:2 * E].rearrange("p (c d) -> p c d", d=D0)
                     ).then_inc(a["phi"], 1)
                hold(act, a["proj"], 2 * g + 2)
                copy(k_tok[:, :, V_HI:V_HI + D0], bank[5][:, 0:E].rearrange("p (c d) -> p c d", d=D0)
                     ).then_inc(a["phi"], 1)

            def l0_rows_even(g, which):
                hold(act, a["stk"], 4 * g + 2 * which + 1)
                rows = (Q_ROWS, K_ROWS)[which]
                base = (8192, 10240)[which]
                dst = scr[:, base:base + 2048].bitcast(BF16)
                copy(dst[0:rows, ds((g % 2) * 2048, 2048)].rearrange("p (t c) -> p t c", c=16)[:, :, 0:8],
                     bank[4][:, :].bitcast(BF16).rearrange("p (c t) -> p t c", t=P)[0:rows]
                     ).then_inc(a["stka"], 1)

            def exponentials(s, g, j, chunk):
                u = 4 * g + j
                hold(act, s["max"], 3 * u + chunk + 1)
                if chunk == 0 and s is c:
                    hold(act, s["rr"], u - 1)
                for qt, _ in S_CHUNKS[chunk]:
                    at = s_sb[j % 2][:, S_OFF[qt]:S_OFF[qt] + (qt + 1) * P]
                    if s is a:
                        last = act.activation(at, at, ACT.Exp, bias=nm[:, j % 2, qt:qt + 1], scale=-1.0)
                    else:
                        last = act.activation(at, at, ACT.Exp, bias=nm[:, j % 2, qt:qt + 1], scale=-1.0,
                                              accum_out=rs[:, j % 2, qt:qt + 1])
                last.then_inc(s["exp"], 1)

            def probs_high(s, u, jp, chunk):
                hold(act, s["t"], 3 * u + chunk + 1)
                w = T_LEN[chunk]
                tb = bank[(2, 3, 7)[chunk] if s is a else 2 + (3 * jp + chunk) % 2]
                copy(pt_hi[jp][:, T_OFF[chunk]:T_OFF[chunk] + w], tb[:, 0:w]).then_inc(s["thi"], 1)

            def kt(ap):
                return ap.rearrange("p (k t) -> p k t", k=KE)

            def turned(kind, t, parts):
                if kind == "x2":
                    return (xt_hi, xt_lo)[parts][:, :, t * P:(t + 1) * P]
                return kt({"cc": (ta_hi, ta_lo), "cm": (tc_hi, tc_lo), "x1": (tb_hi, tb_lo)}[kind][parts][
                    t % (TB if kind == "x1" else 2)])

            def turned_high(kind, t):
                i = TURNS.index((kind, t))
                act.wait_ge(m["tp"], i + 1)
                copy(turned(kind, t, 0), kt(bank[turn_bank(i)][:, 0:E])).then_inc(m["thi"], 1)

            def l0_step(n):
                hold(act, a["w"], n + 1)
                if n < NH:
                    last = copy(v0[n % 2][:, :, :, 0:D0], bank[6][:, 0:P].rearrange("p (k i d) -> p k i d", i=2, d=D0))
                if n >= 2:
                    last = copy(ctx0[:, n - 2, :, :].rearrange("p q d -> p (q d)"), bank[6][:, P:P + TT * VC])
                last.then_inc(a["vc"], 1)

            def l0_group(g):
                for j in range(4):
                    u = 4 * g + j
                    first = is_first(g) and j == 0
                    exponentials(a, g, j, 0)
                    if not first:
                        l0_step(u - 1)
                        probs_high(a, u - 1, (j + 1) % 2, 0)
                        probs_high(a, u - 1, (j + 1) % 2, 1)
                    exponentials(a, g, j, 1)
                    if not first:
                        probs_high(a, u - 1, (j + 1) % 2, 2)
                    exponentials(a, g, j, 2)
                    if not is_last(g):
                        if j == 0:
                            l0_parts_high(g + 1)
                        if j in (1, 2):
                            l0_rows_even(g + 1, j - 1)
                    if j == 3 and g in (1, 5):
                        x_high(2 + g // 4)
                    if u - NH in EARLY_SLOTS:
                        n = u - NH + 1 + EARLY[-1]
                        if 0 <= n + LEAD:
                            turned_high("x1", n + LEAD)
                        turned_high("cc", n + LEAD + 2)

            x_high(0)
            act.wait_ge(c_ready, C_ALL)
            l0_parts_high(0)
            x_high(1)
            act.wait_ge(z_ready, 2)
            l0_rows_even(0, 0)
            l0_rows_even(0, 1)
            for g in range(NT):
                l0_group(g)
            l0_step(NH - 1)
            for chunk in range(3):
                probs_high(a, NH - 1, 1, chunk)
            l0_step(NH)
            l0_step(NH + 1)

            def router_exp(p, count, w):
                act.wait_ge(p["lgd"], count)
                act.activation(rt[:, 1, 0:w], rt[:, 0, 0:w], ACT.Exp).then_inc(p["ex"], 1)

            def gelu(t, p):
                act.wait_ge(m["f"], 4 * t + p + 1)
                hold(act, m["mul"], MIX * (t - 1) + min(2 * p + 2, DVE_X))
                if 2 * p + 2 > DVE_X:
                    hold(act, m["pmul"], (NX - DVE_X) * (t - 1) + 2 * p + 2 - DVE_X)
                act.activation(ge[p], bank[4 + p][:, :], ACT.Gelu_apprx_tanh).then_inc(m["ge"], 1)

            def l1_high(which, g, j=0):
                half = (g % 2) * TOK
                if which == "q":
                    hold(act, c["s"], 12 * g + 3 * j - 3)
                    hold(act, c["proj"], 4 * g + j + 1)
                    copy(qt_hi[j % 2], bank[4][:, :]).then_inc(c["phi"], 1)
                elif which == "k":
                    hold(act, c["kv"], 2 * g + 1)
                    copy(k1_hi[:, ds(half, TOK)], bank[5][:, :]).then_inc(c["kvh"], 1)
                else:
                    hold(act, c["kv"], 2 * g + 2)
                    copy(v1_hi[:, ds(half, TOK)], bank[5][:, :]).then_inc(c["kvh"], 1)

            for n in STEPS[len(EARLY):]:
                here = 0 <= n < NT
                if 0 <= n + LEAD < NT:
                    turned_high("x1", n + LEAD)
                if n == NT:
                    l1_high("k", 0)
                if here:
                    gelu(n, 0)
                if 0 <= n - 2:
                    turned_high("x2", n - 2)
                if here:
                    gelu(n, 1)
                if 0 <= n - 1 < NT:
                    turned_high("cm", n - 1)
                if 0 <= n + LEAD + 2 < NT:
                    turned_high("cc", n + LEAD + 2)
                if 0 <= n + 4 < NT and (n + 4) % TT == TT - 1:
                    router_exp(m, (n + 4) // TT + 1, TT * NX)
                if n == NT:
                    l1_high("q", 0, 0)
                    l1_high("v", 0)
                if here:
                    gelu(n, 2)
                    gelu(n, 3)
            l1_high("q", 0, 1)

            def l1_context_high(g, j):
                u = 4 * g + j
                hold(act, c["pv"], u + 1)
                at = ((g // 4) % 2) * HEADS * TOK + (g % 4) * 4 * TOK + j * TOK
                copy(ct_hi[:, ds(at, TOK)], bank[6][:, :]).then_inc(c["chi"], 1)

            def l1_group(g):
                for j in range(4):
                    u = 4 * g + j
                    behind = 4 * g + j if is_first(g) else 2
                    ahead = 3 - j if is_last(g) else 4
                    exponentials(c, g, j, 0)
                    if behind >= 1:
                        probs_high(c, u - 1, (j + 1) % 2, 0)
                    exponentials(c, g, j, 1)
                    if behind >= 1:
                        probs_high(c, u - 1, (j + 1) % 2, 1)
                    exponentials(c, g, j, 2)
                    if behind >= 2:
                        l1_context_high(*((g, j - 2) if j >= 2 else (g - 1, j + 2)))
                    if ahead >= 2:
                        l1_high("q", *((g, j + 2) if j < 2 else (g + 1, j - 2)))
                    if behind >= 1:
                        probs_high(c, u - 1, (j + 1) % 2, 2)
                    if not is_last(g) and j < 2:
                        l1_high("kv"[j], g + 1)
                    if g > TT and j == 2:
                        last_high(g - TT - 1)

            def last_high(t):
                act.wait_ge(e["tp"], t + 1)
                copy(xt_hi[:, :, t * P:(t + 1) * P], kt(bank[5][:, 0:E])).then_inc(e["thi"], 1)

            for g in range(NT):
                l1_group(g)
            l1_context_high(NT - 1, 2)
            for chunk in range(3):
                probs_high(c, NH - 1, 1, chunk)

            act.wait_ge(ld_b, 8 * 16)
            for b, i, what in TAIL:
                if what == "hidden":
                    n = NF * b + i
                    act.wait_ge(e["h"], n + 1)
                    hold(act, e["y"], n - 1)
                    act.activation(hf[i % 2], bank[i % 2][:, :], ACT.Gelu, bias=b1_col[:, i:i + 1]
                                   ).then_inc(e["ge"], 1)
                    act.wait_ge(e["ge"], n + 1)
                    copy(h_hi[i % 2], hf[i % 2]).then_inc(e["hhi"], 1)
                elif what == "pv":
                    l1_context_high(NT - 1, 3)
                elif what == "turn":
                    last_high(i)
                elif what == "route":
                    router_exp(e, 1, NT * NX)

        class Chain:

            def __init__(self, eng, semaphore, base):
                self.eng, self.sem, self.base, self.n = eng, semaphore, base, 0

            def __call__(self, ins):
                ins.then_inc(self.sem, 1)
                self.n += 1
                hold(self.eng, self.sem, self.base + self.n)

        def router_max(dve, chain, logits, n, lgd):
            w = n * NX
            chain(dve.tensor_reduce(r1c[:, 2, 0:n], logits, AX.X, ALU.max))
            dve.tensor_tensor(rt[:, 0, 0:w].rearrange("p (t x) -> p t x", x=NX), logits,
                              r1c[:, 2, 0:n].unsqueeze(2).to_broadcast([P, n, NX]), ALU.subtract).then_inc(lgd, 1)

        def router_views(n):
            w = n * NX

            def row(i):
                return rt[:, i, 0:w].rearrange("p (t x) -> p t x", x=NX)

            def wide(i):
                return r1c[:, i, 0:n].unsqueeze(2).to_broadcast([P, n, NX])

            return row, wide, [r1c[:, i, 0:n] for i in range(4)]

        def router_pick(dve, chain, n, i, src, ones):
            row, wide, top = router_views(n)
            rev = iota8[:, 0:n * NX].rearrange("p (t x) -> p t x", x=NX)
            chain(dve.tensor_reduce(top[i], row(src), AX.X, ALU.max))
            chain(dve.tensor_tensor(row(4), row(src), wide(i), ALU.is_equal))
            chain(dve.tensor_tensor(row(4), row(4), rev, ALU.mult))
            chain(dve.tensor_reduce(top[2], row(4), AX.X, ALU.max))
            chain(dve.tensor_tensor(row(ones), rev, wide(2), ALU.is_equal))

        def router_first(dve, chain, n, ex, turn):
            row, wide, top = router_views(n)
            w = n * NX
            dve.wait_ge(ex, turn)
            chain(dve.tensor_reduce(top[2], row(1), AX.X, ALU.add))
            chain(dve.reciprocal(top[3], top[2]))
            chain(dve.tensor_tensor(row(2), row(1), wide(3), ALU.mult))
            router_pick(dve, chain, n, 0, 2, 5)
            chain(dve.scalar_tensor_tensor(rt[:, 3, 0:w], rt[:, 5, 0:w], -2.0, rt[:, 2, 0:w], ALU.mult, ALU.add))

        def router_second(dve, chain, n):
            router_pick(dve, chain, n, 1, 3, 6)

        @block.vector
        def _(dve):
            def low(out, bank_cols, hi):
                return dve.tensor_tensor(out, bank_cols, hi, ALU.subtract)

            dve.memset(scr[:, 12288:14336], 0.0).then_inc(z_ready, 1)
            for k in range(KE):
                dve.wait_ge(w_hi_d, k + 1)
                low(wqkv_lo[:, k, :], wqkv_f[:, k * 3 * E:(k + 1) * 3 * E], wqkv_hi[:, k, :]).then_inc(w_lo_d, 1)

            def x_low(b, piece=0):
                t0, t1 = X_PIECES[min(b, 1)][piece]
                dve.wait_ge(x_hi_d, x_pieces(b) + piece + 1)
                low(xt_lo[:, :, b * TOK + t0:b * TOK + t1],
                    xt_f[:, b % 2, :].rearrange("p (k t) -> p k t", k=KE)[:, :, t0:t1],
                    xt_hi[:, :, b * TOK + t0:b * TOK + t1]).then_inc(x_lo_d, 1)

            def l0_parts_low(g):
                hold(dve, a["phi"], 2 * g + 1)
                low(q_tok[:, :, Q_LO:Q_LO + D0], bank[4][:, 0:E].rearrange("p (c d) -> p c d", d=D0),
                    q_tok[:, :, Q_HI:Q_HI + D0])
                low(k_tok[:, :, K_LO:K_LO + D0], bank[4][:, E:2 * E].rearrange("p (c d) -> p c d", d=D0),
                    k_tok[:, :, K_HI:K_HI + D0]).then_inc(a["plo"], 1)
                hold(dve, a["phi"], 2 * g + 2)
                low(k_tok[:, :, V_LO:V_LO + D0], bank[5][:, 0:E].rearrange("p (c d) -> p c d", d=D0),
                    k_tok[:, :, V_HI:V_HI + D0]).then_inc(a["plo"], 1)

            def l0_rows_odd(g, which):
                hold(dve, a["stk"], 4 * g + 2 * which + 2)
                rows = (Q_ROWS, K_ROWS)[which]
                base = (8192, 10240)[which]
                dst = scr[:, base:base + 2048].bitcast(BF16)
                dve.tensor_copy(
                    dst[0:rows, ds((g % 2) * 2048, 2048)].rearrange("p (t c) -> p t c", c=16)[:, :, 8:16],
                    bank[5][:, :].bitcast(BF16).rearrange("p (c t) -> p t c", t=P)[0:rows]).then_inc(a["stkd"], 1)

            def maxima(s, g, j, chunk, scale):
                u = 4 * g + j
                hold(dve, s["s"], 3 * u + chunk + 1)
                for qt, col in S_CHUNKS[chunk]:
                    w = (qt + 1) * P
                    last = dve.tensor_tensor_reduce(
                        s_sb[j % 2][:, S_OFF[qt]:S_OFF[qt] + w], bank[(3 * j + chunk) % 2][:, col:col + w],
                        mask[:, 512 - w:512], -scale, HUGE, ALU.add, ALU.min, nm[:, j % 2, qt:qt + 1])
                last.then_inc(s["max"], 1)

            def probs_low(s, u, jp, chunk):
                hold(dve, s["thi"], 3 * u + chunk + 1)
                w = T_LEN[chunk]
                at = slice(T_OFF[chunk], T_OFF[chunk] + w)
                tb = bank[(2, 3, 7)[chunk] if s is a else 2 + (3 * jp + chunk) % 2]
                low(pt_lo[jp][:, at], tb[:, 0:w], pt_hi[jp][:, at]).then_inc(s["tlo"], 1)

            def inverse_sums(s, u, jp):
                hold(dve, s["exp"], 3 * u + 3)
                dve.reciprocal(rr[:, jp, :], rs[:, jp, :]).then_inc(s["rr"], 1)

            def kt(ap):
                return ap.rearrange("p (k t) -> p k t", k=KE)

            def turned_low(kind, t):
                i = TURNS.index((kind, t))
                dve.wait_ge(m["thi"], i + 1)
                if kind == "x2":
                    hi, lo = xt_hi[:, :, t * P:(t + 1) * P], xt_lo[:, :, t * P:(t + 1) * P]
                else:
                    his, los = {"cc": (ta_hi, ta_lo), "cm": (tc_hi, tc_lo), "x1": (tb_hi, tb_lo)}[kind]
                    slot = t % (TB if kind == "x1" else 2)
                    hi, lo = kt(his[slot]), kt(los[slot])
                low(lo, kt(bank[turn_bank(i)][:, 0:E]), hi).then_inc(m["tlo"], 1)

            chain = Chain(dve, m["dve"], 0)

            def context(t):
                b, q = t // TT, t % TT
                if t >= 2:
                    dve.wait_ge(m["tp"], TURNS.index(("cc", t - 2)) + 1)
                dve.tensor_tensor(cc[t % 2].rearrange("p (h d) -> p h d", d=D0),
                                  ctx0[:, b * HEADS:(b + 1) * HEADS, q, 0:D0],
                                  rcc[:, b * HEADS:(b + 1) * HEADS, q:q + 1].to_broadcast([P, HEADS, D0]), ALU.mult
                                  ).then_inc(m["cc"], 1)

            def joined(t, which):
                rows = x_tok[:, t * E:(t + 1) * E]
                slot = 2 * (which - 1) + t % 2
                dve.wait_ge(m[f"o{which}"], t + 1)
                if which == 1 and t % TT == 0:
                    dve.wait_ge(xb_done, t // TT + 1)
                if which == 2:
                    dve.wait_ge(m["xb"], t + 1)
                dve.tensor_tensor(rows, bank[first_bank(t) if which == 1 else 3][:, 0:E], rows, ALU.add).then_inc(m[f"r{which}"], 1)
                dve.wait_ge(m[f"r{which}"], t + 1)
                chain(dve.bn_stats(stats[:, slot, :], rows))
                dve.bn_aggr(mv[:, slot, :], stats[:, slot, :]).then_inc(m[f"agg{which}"], 1)

            def norm(t, which):
                rows = x_tok[:, t * E:(t + 1) * E]
                slot = 2 * (which - 1) + t % 2
                dve.wait_ge(m[f"rstd{which}"], t + 1)
                dve.tensor_scalar(rows, rows, mv[:, slot, 0:1], rstd[:, slot:slot + 1], ALU.subtract, ALU.mult
                                  ).then_inc(m[f"x{which}"], 1)

            def sums_inverse(half):
                heads = slice(half * NH // 2, (half + 1) * NH // 2)
                dve.wait_ge(a["vc"], (half + 1) * NH // 2 + 2)
                dve.reciprocal(rcc[:, heads, :], ctx0[:, heads, :, D0:VC].rearrange("p h q d -> p h (q d)")
                               ).then_inc(m["rc"], 1)
                dve.wait_ge(m["rc"], half + 1)

            def early_step(n):
                if 0 <= n + LEAD:
                    turned_low("x1", n + LEAD)
                if 0 <= n + LEAD + 1:
                    joined(n + LEAD + 1, 1)
                turned_low("cc", n + LEAD + 2)
                context(n + LEAD + 3)

            def l0_group(g):
                for j in range(4):
                    u = 4 * g + j
                    behind = 4 * g + j if is_first(g) else 2
                    early = u - NH in EARLY_SLOTS
                    n = u - NH + 1 + EARLY[-1]
                    if u - NH == EARLY_SLOTS[0]:
                        sums_inverse(0)
                        context(0)
                    if early and 0 <= n + LEAD:
                        norm(n + LEAD, 1)
                    maxima(a, g, j, 1, D0 ** -0.5)
                    maxima(a, g, j, 2, D0 ** -0.5)
                    if behind >= 1:
                        probs_low(a, u - 1, (j + 1) % 2, 0)
                        probs_low(a, u - 1, (j + 1) % 2, 1)
                    if not (is_last(g) and j == 3):
                        maxima(a, *((g, j + 1) if j < 3 else (g + 1, 0)), 0, D0 ** -0.5)
                    if behind >= 1:
                        probs_low(a, u - 1, (j + 1) % 2, 2)
                    if not is_last(g):
                        if j == 0:
                            l0_parts_low(g + 1)
                        if j in (1, 2):
                            l0_rows_odd(g + 1, j - 1)
                    if j == 3 and g in (1, 5):
                        x_low(2 + g // 4)
                    if early:
                        early_step(n)

            x_low(0, 0)
            x_low(0, 1)
            l0_parts_low(0)
            x_low(1)
            l0_rows_odd(0, 0)
            l0_rows_odd(0, 1)
            dve.wait_ge(ld_c, 16)
            maxima(a, 0, 0, 0, D0 ** -0.5)
            for g in range(NT):
                l0_group(g)
            for chunk in range(3):
                probs_low(a, NH - 1, 1, chunk)

            def mix(t, p):
                dve.wait_ge(m["ge"], 4 * t + p + 1)
                if p == 0:
                    if t >= 2:
                        dve.wait_ge(m["tp"], TURNS.index(("cm", t - 2)) + 1)
                    if t % TT == 0:
                        dve.wait_ge(m["gates"], t // TT + 1)
                for x in range(2 * p, min(2 * p + 2, DVE_X)):
                    part = ge[p][:, (x % 2) * E:(x % 2 + 1) * E]
                    gate = gates[:, t, x:x + 1]
                    if x == 0:
                        ins = dve.tensor_scalar(comb[t % 2], part, gate, None, ALU.mult)
                    else:
                        dve.wait_ge(m["mul"], MIX * t + x)
                        ins = dve.scalar_tensor_tensor(comb[t % 2], part, gate, comb[t % 2], ALU.mult, ALU.add)
                    ins.then_inc(m["mul"], 1)

            def join_halves(t):
                dve.wait_ge(m["psum"], (NX - DVE_X - 1) * (t + 1))
                dve.wait_ge(m["mul"], MIX * t + DVE_X)
                dve.tensor_tensor(comb[t % 2], comb[t % 2], pc[t % 2], ALU.add).then_inc(m["mul"], 1)

            def route(b):
                dve.wait_ge(m["lg"], b + 1)
                tiles_b = slice(b * TT, (b + 1) * TT)
                dve.tensor_tensor(lg[:, tiles_b, :], bank[2][:, 0:TT * NX].rearrange("p (t x) -> p t x", x=NX),
                                  rb_bc[:, :].unsqueeze(1).to_broadcast([P, TT, NX]), ALU.add).then_inc(m["lgc"], 1)
                dve.wait_ge(m["lgc"], b + 1)
                router_max(dve, chain, lg[:, tiles_b, :], TT, m["lgd"])

            def choose_first(b):
                router_first(dve, chain, TT, m["ex"], b + 1)

            def choose_second(b):
                router_second(dve, chain, TT)

            def gate(b):
                tiles_b = slice(b * TT, (b + 1) * TT)
                row, wide, top = router_views(TT)
                chain(dve.tensor_tensor(top[2], top[0], top[1], ALU.add))
                chain(dve.reciprocal(top[3], top[2]))
                chain(dve.tensor_tensor(row(0), row(5), wide(0), ALU.mult))
                chain(dve.tensor_tensor(row(1), row(6), wide(1), ALU.mult))
                chain(dve.tensor_tensor(row(0), row(0), row(1), ALU.add))
                dve.tensor_tensor(gates[:, tiles_b, :], row(0), wide(3), ALU.mult).then_inc(m["gates"], 1)

            def l1_low(which, g, j=0):
                half = (g % 2) * TOK
                if which == "q":
                    hold(dve, c["phi"], 4 * g + j + 1)
                    low(qt_lo[j % 2], bank[4][:, :], qt_hi[j % 2]).then_inc(c["plo"], 1)
                elif which == "k":
                    hold(dve, c["kvh"], 2 * g + 1)
                    low(k1_lo[:, ds(half, TOK)], bank[5][:, :], k1_hi[:, ds(half, TOK)]
                        ).then_inc(c["kvl"], 1)
                else:
                    hold(dve, c["kvh"], 2 * g + 2)
                    low(v1_lo[:, ds(half, TOK)], bank[5][:, :], v1_hi[:, ds(half, TOK)]
                        ).then_inc(c["kvl"], 1)

            norm(EARLY[-1] + LEAD + 1, 1)
            for n in STEPS[len(EARLY):]:
                here, ahead, behind = 0 <= n < NT, n + LEAD + 1, n - 1
                if 0 <= n + LEAD < NT:
                    turned_low("x1", n + LEAD)
                if n == EARLY[-1] + 1:
                    sums_inverse(1)
                if n == NT:
                    l1_low("k", 0)
                routed = 0 <= n + 4 < NT and (n + 4) % TT == TT - 1
                if routed:
                    route((n + 4) // TT)
                if 0 <= n - 2:
                    turned_low("x2", n - 2)
                if here:
                    mix(n, 0)
                if 0 <= ahead < NT:
                    joined(ahead, 1)
                if 0 <= behind < NT:
                    turned_low("cm", behind)
                if 0 <= n + LEAD + 2 < NT:
                    turned_low("cc", n + LEAD + 2)
                if n == NT:
                    l1_low("q", 0, 0)
                if here:
                    mix(n, 1)
                if 0 <= ahead < NT:
                    norm(ahead, 1)
                if 0 <= behind < NT:
                    joined(behind, 2)
                if routed:
                    choose_first((n + 4) // TT)
                if here:
                    mix(n, 2)
                if 0 <= n + LEAD + 3 < NT:
                    context(n + LEAD + 3)
                if n == NT:
                    l1_low("v", 0)
                if 0 <= behind < NT:
                    norm(behind, 2)
                if routed:
                    choose_second((n + 4) // TT)
                if routed:
                    gate((n + 4) // TT)
                if here:
                    join_halves(n)
            l1_low("q", 0, 1)

            def l1_context_low(g, j):
                u = 4 * g + j
                hold(dve, c["chi"], u + 1)
                at = ((g // 4) % 2) * HEADS * TOK + (g % 4) * 4 * TOK + j * TOK
                low(ct_lo[:, ds(at, TOK)], bank[6][:, :], ct_hi[:, ds(at, TOK)]).then_inc(c["clo"], 1)

            def l1_join(t):
                rows = x_tok[:, ds(t * E, E)]
                hold(dve, c["o"], t + 1)
                dve.tensor_tensor(rows, bank[7][:, 0:E], rows, ALU.add).then_inc(c["od"], 1)
                hold(dve, c["od"], t + 2)
                dve.bn_stats(stats[:, 0, :], rows).then_inc(c["st"], 1)
                hold(dve, c["st"], t + 1)
                dve.bn_aggr(mv[:, 0, :], stats[:, 0, :]).then_inc(c["mv"], 1)

            def l1_norm(t):
                rows = x_tok[:, ds(t * E, E)]
                hold(dve, c["rstd"], t + 1)
                dve.tensor_scalar(rows, rows, mv[:, 0, 0:1], rstd[:, 0:1], ALU.subtract, ALU.mult
                                  ).then_inc(c["x"], 1)

            def l1_group(g, dense):
                for j in range(4):
                    u = 4 * g + j
                    behind = 4 * g + j if is_first(g) else 2
                    ahead = 3 - j if is_last(g) else 4
                    maxima(c, g, j, 1, D1 ** -0.5)
                    maxima(c, g, j, 2, D1 ** -0.5)
                    if behind >= 1:
                        probs_low(c, u - 1, (j + 1) % 2, 0)
                        probs_low(c, u - 1, (j + 1) % 2, 1)
                    inverse_sums(c, u, j % 2)
                    if behind >= 2:
                        l1_context_low(*((g, j - 2) if j >= 2 else (g - 1, j + 2)))
                    if ahead >= 2:
                        l1_low("q", *((g, j + 2) if j < 2 else (g + 1, j - 2)))
                    if behind >= 1:
                        probs_low(c, u - 1, (j + 1) % 2, 2)
                    if ahead >= 1:
                        maxima(c, *((g, j + 1) if j < 3 else (g + 1, 0)), 0, D1 ** -0.5)
                    if not is_last(g) and j < 2:
                        l1_low("kv"[j], g + 1)
                    if g > TT and j == 0:
                        l1_norm(g - TT - 1)
                    if g > TT and j == 2:
                        last_low(g - TT - 1)
                    if g > TT and j == 3:
                        last_logits(g - TT - 1)
                    if dense and j == 3:
                        l1_join(g - TT)

            def last_low(t):
                dve.wait_ge(e["thi"], t + 1)
                ts = slice(t * P, (t + 1) * P)
                low(xt_lo[:, :, ts], kt(bank[5][:, 0:E]), xt_hi[:, :, ts]).then_inc(e["tlo"], 1)

            def last_logits(t):
                dve.wait_ge(e["lg"], t + 1)
                dve.tensor_copy(lg[:, t, :], bank[5][:, E:E + NX]).then_inc(e["lgc"], 1)

            dve.sem_inc(c["od"], 1)
            maxima(c, 0, 0, 0, D1 ** -0.5)
            l1_group(0, False)
            for g in range(1, TT):
                l1_group(g, False)
            for g in range(TT, NT - 1):
                l1_group(g, True)
            l1_group(NT - 1, True)
            l1_context_low(NT - 1, 2)
            for chunk in range(3):
                probs_low(c, NH - 1, 1, chunk)

            chain = Chain(dve, e["dve"], 0)
            for b, i, what in TAIL:
                if what == "hidden":
                    dve.wait_ge(e["hhi"], NF * b + i + 1)
                    low(h_lo[i % 2], hf[i % 2], h_hi[i % 2]).then_inc(e["hlo"], 1)
                elif what == "pv":
                    l1_context_low(NT - 1, 3)
                    l1_norm(NT - TT - 1)
                elif what == "dense":
                    l1_join(i)
                    l1_norm(i)
                elif what == "turn":
                    last_low(i)
                elif what == "logits":
                    last_logits(i)
                elif what == "route":
                    dve.wait_ge(e["lgc"], NT)
                    router_max(dve, chain, lg, NT, e["lgd"])
                elif what == "choose":
                    router_first(dve, chain, NT, e["ex"], 1)
                    router_second(dve, chain, NT)
                    row, wide, top = router_views(NT)
                    for k in range(2):
                        dve.tensor_copy(picks[:, k * NT:(k + 1) * NT, :], row(5 + k)).then_inc(e["picks"], 1)
                elif what == "gates":
                    dve.wait_ge(e["rank"], 1)
                    chain(dve.tensor_scalar(cnt[:, :], bank[7][:, 0:2 * NT * NX], float(CAP), None, ALU.is_le))
                    for k in range(2):
                        chain(dve.tensor_tensor(row(k), cnt[:, k * NT * NX:(k + 1) * NT * NX].rearrange(
                            "p (t x) -> p t x", x=NX), row(5 + k), ALU.mult))
                        chain(dve.tensor_reduce(top[2 + k], row(k), AX.X, ALU.add))
                        chain(dve.tensor_tensor(top[2 + k], top[2 + k], top[k], ALU.mult))
                    dve.tensor_tensor(g1[:, :], top[2], top[3], ALU.add).then_inc(e["gates"], 1)
                    dve.wait_ge(e["gates"], 1)
                elif what == "join":
                    rows = x_tok[:, i * E:(i + 1) * E]
                    t = i % TT
                    dve.wait_ge(e["y"], NF * (i // TT + 1))
                    dve.wait_ge(e["xb"], i + 1)
                    dve.scalar_tensor_tensor(
                        rows, bank[Y_BANKS[i // TT][t // 2]][:, (t % 2) * E:(t % 2 + 1) * E], g1[:, i:i + 1],
                        rows, ALU.mult, ALU.add).then_inc(e["yr"], 1)
                    dve.wait_ge(e["yr"], i + 1)
                    chain(dve.bn_stats(stats[:, t, :], rows))
                    dve.bn_aggr(mv[:, t, :], stats[:, t, :]).then_inc(e["agg"], 1)
                elif what == "norm":
                    rows = x_tok[:, i * E:(i + 1) * E]
                    t = i % TT
                    dve.wait_ge(e["rstd"], i + 1)
                    dve.tensor_scalar(rows, rows, mv[:, t, 0:1], rstd[:, t:t + 1], ALU.subtract, ALU.mult
                                      ).then_inc(e["x"], 1)

        @block.gpsimd
        def _(pool):
            pool.memset(scr[:, 8192:12288], 0.0).then_inc(z_ready, 1)
            pool.memset(one_f[:, :], 1.0).then_inc(c_ready, 1)
            pool.memset(neg_half[:, :], -0.5).then_inc(c_ready, 1)
            pool.memset(ones_b[:, :], 1.0).then_inc(c_ready, 1)
            for i in range(2):
                pool.memset(v0[i][:, :, :, :], 1.0).then_inc(c_ready, 1)
            pool.wait_ge(ld_c, 16)
            pool.tensor_copy(ident_b[:, :], ident_f).then_inc(c_ready, 1)
            pool.tensor_copy(upper_b[:, :], upper_f).then_inc(c_ready, 1)

            def duplicates(g):
                hold(pool, a["phi"], 2 * g + 1)
                for tok, src, dst in ((q_tok, Q_HI, Q_HI2), (k_tok, K_HI, K_HI2)):
                    pool.tensor_copy(tok[:, :, dst:dst + D0], tok[:, :, src:src + D0]).then_inc(a["dup"], 1)

            def split_chunk(n, part):
                slot = stage[:, ds((n % 2) * CH, CH)]
                at = ds(n * CH, CH)
                if part == 0:
                    pool.wait_ge(ld_ch[n % 2], 16 * (n // 2 + 1))
                    pool.tensor_tensor(w_hi[:, at], slot, one_f[:, 0:1].to_broadcast([P, CH]), ALU.mult
                                       ).then_inc(pool_seq, 1)
                else:
                    pool.wait_ge(pool_seq, n + 1)
                    pool.tensor_tensor(w_lo[:, at], slot, w_hi[:, at], ALU.subtract).then_inc(ch_done, 1)

            def l0_group(g):
                for j in range(4):
                    u = 4 * g + j
                    if j == 0 and not is_last(g):
                        duplicates(g + 1)
                    for n in range(2 * NCH * u // 48, min(2 * NCH * (u + 1) // 48, 2 * NCH)):
                        split_chunk(n // 2, n % 2)

            pool.wait_ge(c_ready, C_ALL)
            pool.wait_ge(z_ready, 2)
            duplicates(0)
            for g in range(NT):
                l0_group(g)
            pool.wait_ge(ld_xtok, 16)
            pool.wait_ge(ld_b, 8 * 16)
            for b in range(NB):
                rows = x_tok[:, b * TT * E:(b + 1) * TT * E].rearrange("p (t e) -> p t e", e=E)
                pool.tensor_tensor(rows, rows, bp_bc[:, :].unsqueeze(1).to_broadcast([P, TT, E]), ALU.add
                                   ).then_inc(xb_done, 1)
            chain = Chain(pool, eb_seq, 0)
            chain(pool.tensor_copy(rw_hi[:, :, :], rw_f[:, :, :]))
            chain(pool.tensor_tensor(rw_lo[:, :, :], rw_f[:, :, :], rw_hi[:, :, :], ALU.subtract))
            chain(pool.tensor_copy(eb_p[:, 0, :], eb_f[:, :]))
            chain(pool.tensor_tensor(eb_r[:, 0, :], eb_f[:, :], eb_p[:, 0, :], ALU.subtract))
            chain(pool.tensor_copy(eb_p[:, 1, :], eb_r[:, 0, :]))
            chain(pool.tensor_tensor(eb_r[:, 1, :], eb_r[:, 0, :], eb_p[:, 1, :], ALU.subtract))
            pool.tensor_copy(eb_p[:, 2, :], eb_r[:, 1, :]).then_inc(eb_ready, 1)

            def inverse_deviation(slot, ready, value, seq, seq_value, done):
                pool.wait_ge(ready, value)
                pool.tensor_scalar(var_e[:, slot:slot + 1], mv[:, slot, 1:2], EPS, 1.0, ALU.add, ALU.mult
                                   ).then_inc(seq, 1)
                pool.wait_ge(seq, seq_value)
                pool.tensor_tensor(rstd[:, slot:slot + 1], var_e[:, slot:slot + 1], neg_half[:, 0:1], ALU.pow
                                   ).then_inc(done, 1)

            def mix(t, p):
                pool.wait_ge(m["ge"], 4 * t + p + 1)
                if p == 2:
                    hold(pool, m["mul"], MIX * (t - 1))
                    if t % TT == 0:
                        pool.wait_ge(m["gates"], t // TT + 1)
                for x in range(max(2 * p, DVE_X), 2 * p + 2):
                    share = pc[t % 2] if x == DVE_X else pc_x[x % 2]
                    pool.tensor_scalar(share, ge[p][:, (x % 2) * E:(x % 2 + 1) * E], gates[:, t, x:x + 1], 1.0,
                                       ALU.mult, ALU.mult).then_inc(m["pmul"], 1)
                    if x > DVE_X:
                        pool.wait_ge(m["pmul"], (NX - DVE_X) * t + x - DVE_X + 1)
                        hold(pool, m["psum"], (NX - DVE_X - 1) * t + x - DVE_X - 1)
                        pool.tensor_tensor(pc[t % 2], pc[t % 2], share, ALU.add).then_inc(m["psum"], 1)

            norms = 0
            for n in STEPS:
                if 0 <= n + LEAD + 1 < NT:
                    norms += 1
                    t = n + LEAD + 1
                    inverse_deviation(t % 2, m["agg1"], t + 1, m["pool"], norms, m["rstd1"])
                if 0 <= n < NT:
                    mix(n, 2)
                if 0 <= n - 1 < NT:
                    norms += 1
                    inverse_deviation(2 + (n - 1) % 2, m["agg2"], n, m["pool"], norms, m["rstd2"])
                if 0 <= n < NT:
                    mix(n, 3)
                if 0 <= n + LEAD < NT:
                    t = n + LEAD
                    rows = x_tok[:, t * E:(t + 1) * E]
                    pool.wait_ge(m["tp"], TURNS.index(("x1", t)) + 1)
                    pool.tensor_tensor(rows, rows, outb_bc[:, :], ALU.add).then_inc(m["xb"], 1)

            def l1_group(g, dense):
                for j in range(4):
                    u = 4 * g + j
                    hold(pool, c["rr"], u + 1)
                    for qt in range(TT):
                        at = s_sb[j % 2][:, S_OFF[qt]:S_OFF[qt] + (qt + 1) * P]
                        last = pool.tensor_scalar(at, at, rr[:, j % 2, qt:qt + 1], 1.0, ALU.mult, ALU.mult)
                    last.then_inc(c["nrm"], 1)
                if dense:
                    inverse_deviation(0, c["mv"], g - TT + 1, c["seq"], g - TT + 1, c["rstd"])

            for g in range(NT):
                l1_group(g, g >= TT)
            for g in range(NT, NT + TT):
                inverse_deviation(0, c["mv"], g - TT + 1, c["seq"], g - TT + 1, c["rstd"])

            def gated_bias(t):
                rows = x_tok[:, t * E:(t + 1) * E]
                pool.tensor_scalar(b2g[t % 2], b2_bc[:, :], g1[:, t:t + 1], 1.0, ALU.mult, ALU.mult
                                   ).then_inc(e["bg"], 1)
                pool.wait_ge(e["bg"], t + 1)
                pool.tensor_tensor(rows, rows, b2g[t % 2], ALU.add).then_inc(e["xb"], 1)

            pool.wait_ge(e["gates"], 1)
            for t in range(TT):
                gated_bias(t)
            for t in range(NT):
                inverse_deviation(t % TT, e["agg"], t + 1, e["seq"], t + 1, e["rstd"])
                if t + TT < NT:
                    gated_bias(t + TT)


def kernel(**inputs):
    import numpy as np
    import concourse.bacc as bacc
    from concourse.bass_utils import run_bass_kernel_spmd

    v = {n: np.asarray(x) for n, x in inputs.items()}

    def rows(w):
        return w.reshape(-1, P, w.shape[-1]).transpose(1, 0, 2)

    def cols(w):
        return rows(w).reshape(P, -1)

    x = v["L0_attn_x"].reshape(NT, P, E)
    up = np.arange(P)
    constants = np.concatenate([
        np.eye(P), up[:, None] <= up[None, :], np.zeros((P, 512 - P)),
        np.where(up[None, :] > up[:, None], MASKED, 0.0),
        np.broadcast_to(np.tile(NX - np.arange(NX), NT), (P, P))], axis=1).astype(np.float32)
    experts = v["L0_ffn_expert_w"].transpose(1, 0, 2).reshape(E, NX * E)
    arrays = {
        "x_tok": x.transpose(1, 0, 2),
        "x_t": v["L0_attn_x"].reshape(NB, TOK, KE, P).transpose(3, 0, 2, 1).reshape(P, NB, KE * TOK),
        "wqkv": cols(np.concatenate([v["L0_attn_W" + n].T for n in "qkv"], axis=1)),
        "wall": np.concatenate([cols(w) for w in (
            v["L0_attn_Wp"].T, v["L0_ffn_out_w"], experts, v["L1_attn_w_q"], v["L1_attn_w_kv"],
            v["L1_attn_w_dense"], v["L1_ffn_w1"].T, v["L1_ffn_w2"].T)], axis=1),
        "constants": constants,
        "bp": v["L0_attn_bp"], "outb": v["L0_ffn_out_b"], "b2": v["L1_ffn_b2"], "rb": v["L0_ffn_router_b"],
        "eb": v["L0_ffn_expert_b"].reshape(16, P),
        "rw0": cols(v["L0_ffn_router_w"]), "rw1": cols(v["L1_ffn_router_w"].T),
        "b1": v["L1_ffn_b1"].reshape(NF, P).T,
    }
    arrays = {n: np.ascontiguousarray(z) for n, z in arrays.items()}
    nc = bacc.Bacc("TRN2", target_bir_lowering=False, num_devices=1)
    args = [nc.dram_tensor(f"{n}_in", z.shape, mybir.dt.from_np(z.dtype), kind="ExternalInput").ap()
            for n, z in arrays.items()]
    out = nc.dram_tensor("out", (P, NT, E), F32, kind="ExternalOutput").ap()
    build(nc, *args, out)
    r = run_bass_kernel_spmd(nc, [{f"{n}_in": z for n, z in arrays.items()}], core_ids=[0])
    return np.asarray(r.results[0]["out"]).transpose(1, 0, 2).reshape(NB, TOK, E)
```
